# Optimizing a Trainium2 kernel written in Bass

```python
import numpy as np
import jax
import jax.numpy as jnp

def _softmax(x, axis=-1):
    return jax.nn.softmax(x, axis=axis)

def _gelu(x):
    return jax.nn.gelu(x, approximate=True)

def _silu(x):
    return jax.nn.silu(x)

def _sigmoid(x):
    return jax.nn.sigmoid(x)

def _layernorm(x, axis=-1, eps=1e-05):
    m = jnp.mean(x, axis=axis, keepdims=True)
    v = jnp.var(x, axis=axis, keepdims=True)
    return (x - m) / jnp.sqrt(v + eps)

def _scatter_add(tgt, idx, src, axis=0):
    return tgt.at[idx].add(src)

def _segment_sum(src, seg, n):
    return jax.ops.segment_sum(src, seg, n)
kernel_name = 'mk_adaln_ffn_d2_seqx_r8_8e58f4'

def setup_inputs(seed: int=0):
    np.random.seed(seed)
    _w = jnp.asarray

    def _rec_inputs():
        import jax
        import jax.numpy as jnp
        _rk = jax.random.key(seed)
        x = -0.0003929 + 0.9999 * jax.random.normal(jax.random.fold_in(_rk, 1), (4, 256, 256), jnp.float32)
        _lenS = 256 - jax.random.randint(jax.random.fold_in(_rk, 7), (4,), 0, max(1, 256 // 4) + 1, jnp.int32)
        _lenS2 = 256 - jax.random.randint(jax.random.fold_in(_rk, 8), (4,), 0, max(1, 256 // 4) + 1, jnp.int32)
        cond_2048 = 0.00782532 + 1.00527 * jax.random.normal(jax.random.fold_in(_rk, 11), (4, 256), jnp.float32)
        return (x, cond_2048)
    x, cond_2048 = _rec_inputs()

    def _L0_cond_setup():
        import jax, jax.numpy as jnp
        import numpy as np
        HEADS = 16
        EPS = 1e-06

        def _rms_norm(x, g):
            xf = x.astype(jnp.float32)
            y = xf * jax.lax.rsqrt(jnp.mean(xf * xf, axis=-1, keepdims=True) + EPS)
            return y.astype(x.dtype) * g
        key = jax.random.key(seed)
        ks = jax.random.split(key, 6)
        b, n, dim, emb_dim = (4, 256, 256, 256)
        d_head = dim // HEADS
        return {'x': jax.random.normal(ks[0], (b, n, dim), jnp.float32), 'emb': jax.random.normal(ks[1], (b, 1, emb_dim), jnp.float32), 'W_emb': jax.random.normal(ks[2], (emb_dim, 2 * dim), jnp.float32) * emb_dim ** (-0.5), 'b_emb': jnp.zeros((2 * dim,), jnp.float32), 'g_norm': jnp.ones((dim,), jnp.float32), 'W_qkv': jax.random.normal(ks[3], (dim, 3 * dim), jnp.float32) * dim ** (-0.5), 'g_q': jnp.ones((d_head,), jnp.float32), 'g_k': jnp.ones((d_head,), jnp.float32), 'W_out': jax.random.normal(ks[4], (dim, dim), jnp.float32) * dim ** (-0.5)}
    _L0_cond_all = _L0_cond_setup()
    _L0_cond_in = {k: v for k, v in _L0_cond_all.items() if k in ('W_emb', 'b_emb', 'g_norm', 'W_qkv', 'g_q', 'g_k', 'W_out')}
    del _L0_cond_all

    def _L0_ffn_setup():
        import jax, jax.numpy as jnp
        import numpy as np
        QMAX = 127.0
        EPS = 1e-08

        def _quant_per_tensor(x):
            scale = jnp.maximum(jnp.max(jnp.abs(x)) / QMAX, EPS)
            q = jnp.clip(jnp.round(x / scale), -QMAX, QMAX).astype(jnp.int8)
            return (q, scale)

        def _quant_per_channel(w):
            scale = jnp.maximum(jnp.max(jnp.abs(w), axis=1) / QMAX, EPS)
            q = jnp.clip(jnp.round(w / scale[:, None]), -QMAX, QMAX).astype(jnp.int8)
            return (q, scale)

        def _dyn_quant_linear(x, w, b):
            qx, sx = _quant_per_tensor(x)
            qw, sw = _quant_per_channel(w)
            acc = jnp.matmul(qx.astype(jnp.int32), qw.T.astype(jnp.int32))
            return acc.astype(jnp.float32) * (sx * sw) + b
        key = jax.random.key(seed)
        k1, k2, k3, k4, k5 = jax.random.split(key, 5)
        B, S, H, I = (4, 256, 256, 1024)
        hidden_state = jax.random.normal(k1, (B, S, H), dtype=jnp.float32)
        w1 = jax.random.normal(k2, (I, H), dtype=jnp.float32) * (1.0 / np.sqrt(H))
        b1 = jax.random.normal(k3, (I,), dtype=jnp.float32) * 0.02
        w2 = jax.random.normal(k4, (H, I), dtype=jnp.float32) * (1.0 / np.sqrt(I))
        b2 = jax.random.normal(k5, (H,), dtype=jnp.float32) * 0.02
        return {'hidden_state': hidden_state, 'w1': w1, 'b1': b1, 'w2': w2, 'b2': b2}
    _L0_ffn_all = _L0_ffn_setup()
    _L0_ffn_in = {k: v for k, v in _L0_ffn_all.items() if k in ('w1', 'b1', 'w2', 'b2')}
    del _L0_ffn_all

    def _L1_cond_setup():
        import jax, jax.numpy as jnp
        import numpy as np
        NUM_BLOCKS = 8
        NUM_LAYERS = 4
        EPS = 1e-06
        key = jax.random.key(seed)
        ks = jax.random.split(key, 6)
        B, S, H = (4, 512, 256)
        inputs = jax.random.normal(ks[0], (B, S, H), dtype=jnp.float32)
        query_vectors = jax.random.normal(ks[1], (NUM_LAYERS, H), dtype=jnp.float32) * 0.01
        lim = float(np.sqrt(6.0 / (H + H)))
        Wk = jax.random.uniform(ks[2], (H, H), minval=-lim, maxval=lim, dtype=jnp.float32)
        Wo = jax.random.uniform(ks[3], (H, H), minval=-lim, maxval=lim, dtype=jnp.float32)
        rms_weight = jnp.ones((H,), dtype=jnp.float32)
        ln_gamma = jnp.ones((H,), dtype=jnp.float32)
        ln_beta = jnp.zeros((H,), dtype=jnp.float32)
        return {'inputs': inputs, 'layer_idx': 1, 'rms_weight': rms_weight, 'query_vectors': query_vectors, 'Wk': Wk, 'Wo': Wo, 'ln_gamma': ln_gamma, 'ln_beta': ln_beta}
    _L1_cond_all = _L1_cond_setup()
    _L1_cond_in = {k: v for k, v in _L1_cond_all.items() if k in ('rms_weight', 'Wk', 'Wo', 'ln_gamma', 'ln_beta')}
    del _L1_cond_all

    def _L1_ffn_setup():
        import jax, jax.numpy as jnp
        import numpy as np
        TARGET_SPARSITY = 0.9
        LN_EPS = 1e-05

        def ternary_quant(W):
            scale = jnp.mean(jnp.abs(W))
            q = jnp.clip(jnp.round(W / (scale + 1e-08)), -1.0, 1.0) * scale
            return W + jax.lax.stop_gradient(q - W)

        def layernorm(x, gamma, beta):
            mu = jnp.mean(x, axis=-1, keepdims=True)
            var = jnp.var(x, axis=-1, keepdims=True)
            return (x - mu) * jax.lax.rsqrt(var + LN_EPS) * gamma + beta
        key = jax.random.key(seed)
        ks = jax.random.split(key, 3)
        B, S, D, N = (4, 256, 256, 1024)
        x = jax.random.normal(ks[0], (B, S, D), dtype=jnp.float32)
        W_syn = jax.random.normal(ks[1], (N, D), dtype=jnp.float32) * (1.0 / np.sqrt(D))
        b_syn = jnp.zeros((N,), dtype=jnp.float32)
        W_out = jax.random.normal(ks[2], (D, N), dtype=jnp.float32) * (1.0 / np.sqrt(N))
        b_out = jnp.zeros((D,), dtype=jnp.float32)
        gamma = jnp.ones((D,), dtype=jnp.float32)
        beta = jnp.zeros((D,), dtype=jnp.float32)
        return {'x': x, 'W_syn': W_syn, 'b_syn': b_syn, 'W_out': W_out, 'b_out': b_out, 'gamma': gamma, 'beta': beta}
    _L1_ffn_all = _L1_ffn_setup()
    _L1_ffn_in = {k: v for k, v in _L1_ffn_all.items() if k in ('W_syn', 'b_syn', 'W_out', 'b_out', 'gamma', 'beta')}
    del _L1_ffn_all
    return {'x': x, 'cond_2048': cond_2048, 'L0_cond_W_emb': _L0_cond_in['W_emb'], 'L0_cond_b_emb': _L0_cond_in['b_emb'], 'L0_cond_g_norm': _L0_cond_in['g_norm'], 'L0_cond_W_qkv': _L0_cond_in['W_qkv'], 'L0_cond_g_q': _L0_cond_in['g_q'], 'L0_cond_g_k': _L0_cond_in['g_k'], 'L0_cond_W_out': _L0_cond_in['W_out'], 'L0_ffn_w1': _L0_ffn_in['w1'], 'L0_ffn_b1': _L0_ffn_in['b1'], 'L0_ffn_w2': _L0_ffn_in['w2'], 'L0_ffn_b2': _L0_ffn_in['b2'], 'L1_cond_rms_weight': _L1_cond_in['rms_weight'], 'L1_cond_Wk': _L1_cond_in['Wk'], 'L1_cond_Wo': _L1_cond_in['Wo'], 'L1_cond_ln_gamma': _L1_cond_in['ln_gamma'], 'L1_cond_ln_beta': _L1_cond_in['ln_beta'], 'L1_ffn_W_syn': _L1_ffn_in['W_syn'], 'L1_ffn_b_syn': _L1_ffn_in['b_syn'], 'L1_ffn_W_out': _L1_ffn_in['W_out'], 'L1_ffn_b_out': _L1_ffn_in['b_out'], 'L1_ffn_gamma': _L1_ffn_in['gamma'], 'L1_ffn_beta': _L1_ffn_in['beta']}

def reference(x, cond_2048, L0_cond_W_emb, L0_cond_b_emb, L0_cond_g_norm, L0_cond_W_qkv, L0_cond_g_q, L0_cond_g_k, L0_cond_W_out, L0_ffn_w1, L0_ffn_b1, L0_ffn_w2, L0_ffn_b2, L1_cond_rms_weight, L1_cond_Wk, L1_cond_Wo, L1_cond_ln_gamma, L1_cond_ln_beta, L1_ffn_W_syn, L1_ffn_b_syn, L1_ffn_W_out, L1_ffn_b_out, L1_ffn_gamma, L1_ffn_beta):
    import jax
    import jax.numpy as jnp

    def _L0_cond_ref(x, emb, W_emb, b_emb, g_norm, W_qkv, g_q, g_k, W_out):
        import jax, jax.numpy as jnp
        import numpy as np
        HEADS = 16
        EPS = 1e-06

        def _rms_norm(x, g):
            xf = x.astype(jnp.float32)
            y = xf * jax.lax.rsqrt(jnp.mean(xf * xf, axis=-1, keepdims=True) + EPS)
            return y.astype(x.dtype) * g
        b, n, dim = x.shape
        h = HEADS
        d = dim // h
        scale_shift = emb @ W_emb + b_emb
        scale, shift = jnp.split(scale_shift, 2, axis=-1)
        xn = _rms_norm(x, g_norm) * (1.0 + scale) + shift
        qkv = xn @ W_qkv
        qkv = qkv.reshape(b, n, 3, h, d)
        q, k, v = jnp.moveaxis(qkv, 2, 0)
        q = jnp.swapaxes(q, 1, 2)
        k = jnp.swapaxes(k, 1, 2)
        v = jnp.swapaxes(v, 1, 2)
        q = _rms_norm(q, g_q)
        k = _rms_norm(k, g_k)
        logits = jnp.einsum('bhqd,bhkd->bhqk', q, k) * d ** (-0.5)
        attn = jax.nn.softmax(logits, axis=-1)
        o = jnp.einsum('bhqk,bhkd->bhqd', attn, v)
        o = jnp.swapaxes(o, 1, 2).reshape(b, n, dim)
        return o + o @ W_out

    def _L0_ffn_ref(hidden_state, w1, b1, w2, b2):
        import jax, jax.numpy as jnp
        import numpy as np
        QMAX = 127.0
        EPS = 1e-08

        def _quant_per_tensor(x):
            scale = jnp.maximum(jnp.max(jnp.abs(x)) / QMAX, EPS)
            q = jnp.clip(jnp.round(x / scale), -QMAX, QMAX).astype(jnp.int8)
            return (q, scale)

        def _quant_per_channel(w):
            scale = jnp.maximum(jnp.max(jnp.abs(w), axis=1) / QMAX, EPS)
            q = jnp.clip(jnp.round(w / scale[:, None]), -QMAX, QMAX).astype(jnp.int8)
            return (q, scale)

        def _dyn_quant_linear(x, w, b):
            qx, sx = _quant_per_tensor(x)
            qw, sw = _quant_per_channel(w)
            acc = jnp.matmul(qx.astype(jnp.int32), qw.T.astype(jnp.int32))
            return acc.astype(jnp.float32) * (sx * sw) + b
        h = _dyn_quant_linear(hidden_state, w1, b1)
        h = jax.nn.gelu(h, approximate=False)
        return _dyn_quant_linear(h, w2, b2)

    def _L1_cond_ref(inputs, layer_idx, rms_weight, query_vectors, Wk, Wo, ln_gamma, ln_beta):
        import jax, jax.numpy as jnp
        import numpy as np
        NUM_BLOCKS = 8
        NUM_LAYERS = 4
        EPS = 1e-06
        B, S, H = inputs.shape
        block_size = max(1, S // NUM_BLOCKS)
        n_blocks = S // block_size
        block_repr = inputs.reshape(B, n_blocks, block_size, H).sum(axis=2)
        keys = jnp.einsum('bnh,kh->bnk', block_repr, Wk)
        rms = jnp.sqrt(jnp.mean(keys * keys, axis=-1, keepdims=True) + EPS)
        keys = keys / rms * rms_weight
        q = query_vectors[layer_idx]
        scores = jnp.einsum('bnh,h->bn', keys, q)
        attn = jax.nn.softmax(scores, axis=-1)
        attended = jnp.einsum('bn,bnh->bh', attn, block_repr)
        attended = jnp.broadcast_to(attended[:, None, :], (B, S, H))
        proj = jnp.einsum('bsh,kh->bsk', attended, Wo)
        x = inputs + proj
        mu = jnp.mean(x, axis=-1, keepdims=True)
        var = jnp.mean((x - mu) ** 2, axis=-1, keepdims=True)
        out = (x - mu) / jnp.sqrt(var + EPS) * ln_gamma + ln_beta
        return out

    def _L1_ffn_ref(x, W_syn, b_syn, W_out, b_out, gamma, beta):
        import jax, jax.numpy as jnp
        import numpy as np
        TARGET_SPARSITY = 0.9
        LN_EPS = 1e-05

        def ternary_quant(W):
            scale = jnp.mean(jnp.abs(W))
            q = jnp.clip(jnp.round(W / (scale + 1e-08)), -1.0, 1.0) * scale
            return W + jax.lax.stop_gradient(q - W)

        def layernorm(x, gamma, beta):
            mu = jnp.mean(x, axis=-1, keepdims=True)
            var = jnp.var(x, axis=-1, keepdims=True)
            return (x - mu) * jax.lax.rsqrt(var + LN_EPS) * gamma + beta
        B, S, D = x.shape
        N = W_syn.shape[0]
        x_flat = x.reshape(-1, D)
        z = x_flat @ ternary_quant(W_syn).T + b_syn
        k = max(1, int(N * (1.0 - TARGET_SPARSITY)))
        topv, _ = jax.lax.top_k(z, k)
        thresh = topv[:, -1:]
        hidden = jnp.where(z >= thresh, jax.nn.relu(z), 0.0)
        out = hidden @ ternary_quant(W_out).T + b_out
        out = out.reshape(B, S, D)
        return layernorm(x + out, gamma, beta)
    x = x + _L0_ffn_ref(_L0_cond_ref(x, cond_2048[:, None, :], L0_cond_W_emb, L0_cond_b_emb, L0_cond_g_norm, L0_cond_W_qkv, L0_cond_g_q, L0_cond_g_k, L0_cond_W_out), L0_ffn_w1, L0_ffn_b1, L0_ffn_w2, L0_ffn_b2)
    x = x + _L1_ffn_ref(_L1_cond_ref(x, 1, L1_cond_rms_weight, cond_2048, L1_cond_Wk, L1_cond_Wo, L1_cond_ln_gamma, L1_cond_ln_beta), L1_ffn_W_syn, L1_ffn_b_syn, L1_ffn_W_out, L1_ffn_b_out, L1_ffn_gamma, L1_ffn_beta)
    return x

_drawn_inputs = setup_inputs


def setup_inputs(seed=0):
    import zlib

    import numpy as np

    out = dict(_drawn_inputs(seed))
    spreads = {'L0_cond_b_emb': (0.0, 0.1),
     'L0_cond_g_norm': (1.0, 0.2),
     'L0_cond_g_q': (1.0, 0.6),
     'L0_cond_g_k': (1.0, 0.2),
     'L1_cond_rms_weight': (1.0, 0.2),
     'L1_cond_ln_gamma': (1.0, 0.2),
     'L1_cond_ln_beta': (0.0, 0.1),
     'L1_ffn_b_syn': (0.0, 0.1),
     'L1_ffn_b_out': (0.0, 0.1),
     'L1_ffn_gamma': (1.0, 0.2),
     'L1_ffn_beta': (0.0, 0.1)}
    factors = {'L0_ffn_b1': 3.237}
    for name, (base, spread) in spreads.items():
        noise = np.random.default_rng([zlib.crc32(name.encode()), seed]).standard_normal(out[name].shape)
        drawn = base * np.exp(spread * noise) if base else spread * noise
        out[name] = jnp.asarray(drawn.astype(out[name].dtype))
    for name, factor in factors.items():
        out[name] = (out[name] * factor).astype(out[name].dtype)
    return out
```

```python
from contextlib import ExitStack

import concourse.bass as bass
from concourse import mybir

F32 = mybir.dt.float32
BF16 = mybir.dt.bfloat16
FP16 = mybir.dt.float16
I32 = mybir.dt.int32
ALU = mybir.AluOpType
ACT = mybir.ActivationFunctionType
AX = mybir.AxisListType

P = 128
B, S, D = 4, 256, 256
T = B * S // P
TPB = S // P
KD = D // P
HEADS = 16
DH = D // HEADS
PAIRS = HEADS // 2
HID = 1024
FT = HID // P
BLK = 8
BLK_TOKENS = S // BLK
TOPK = max(1, int(HID * (1.0 - 0.9)))
ROUND = 1.5 * 2.0 ** 23
QMAX = 127.0
QK_SCALE = 8.0

COLS = {}
ROWS = {}


def _lay(table, names):
    at = 0
    for name, n in names:
        table[name] = (at, at + n)
        at += n
    return at


NCOLS = _lay(COLS, [("cond", KD * B), ("b_emb", 2 * KD), ("g_norm", KD), ("b1", FT), ("ln_gamma", KD),
                    ("ln_beta", KD)])
NROWS = _lay(ROWS, [("g_q", DH), ("g_k", DH), ("b2", D), ("b_out", D), ("gamma", D), ("beta", D),
                    ("ln_gamma", D), ("ln_beta", D), ("rms_w", D), ("query", D), ("b_syn", HID)])

NEWTON = (1.0, 0.8, 0.6, 0.4)
AIM = TOPK - 4.5
START = 1.2816 / 0.3989 / HID
STEP = 1.0 / 0.3989 / HID / (HID * 0.1755)
FLAT_ROUNDS = -(-TOPK // 8)


def build(nc, x, cols, rows, w_emb, w_qkv, w_out, w1, w2, wk_t, wo_t, wsyn_t, wout_t, out):
    ctx = ExitStack()
    with ctx:
        def sb(name, shape, dt=F32):
            return ctx.enter_context(nc.sbuf_tensor(name, shape, dt))

        def sem(name):
            return ctx.enter_context(nc.semaphore(name))

        pairs = [ctx.enter_context(nc.psum_tensor(f"banks{2 * i}{2 * i + 1}", [P, 1024], F32)) for i in range(4)]

        def bank(i):
            return pairs[i // 2][:, (i % 2) * 512:(i % 2) * 512 + 512]

        ident = sb("ident", [P, P])
        ident_h = sb("ident_h", [P, P], FP16)
        ones = sb("ones", [P, P])
        neg_half = sb("neg_half", [P, 32])
        round_col = sb("round_col", [P, 1])
        block_of = sb("block_of", [P, P // BLK_TOKENS])
        iota8 = sb("iota8", [P, 8])
        ones8 = sb("ones8", [P, 8])
        newton_c = sb("newton_c", [P, len(NEWTON)])
        sel3 = sb("sel3", [96, P], BF16)
        col = sb("col", [P, NCOLS])
        row = sb("row", [P, NROWS])

        def c(name):
            return col[:, COLS[name][0]:COLS[name][1]]

        def r(name):
            return row[:, ROWS[name][0]:ROWS[name][1]]

        wemb = sb("wemb", [P, KD, 2 * D])
        wqkv = sb("wqkv", [P, KD, 3 * D])
        wout = sb("wout", [P, KD, D])
        w1s = sb("w1s", [P, FT, D])
        w2s = sb("w2s", [P, KD, HID])
        w1q = sb("w1q", [P, FT, D], FP16)
        w2q = sb("w2q", [P, KD, HID], FP16)
        w1qT = sb("w1qT", [P, KD, HID], FP16)
        w2qT = sb("w2qT", [P, FT, D], FP16)
        wk = sb("wk", [P, KD, D])
        wo = sb("wo", [P, KD, D])
        wsyn = sb("wsyn", [P, KD, HID])
        wfin = sb("wfin", [P, FT, D])
        tsyn = sb("tsyn", [P, KD, HID], FP16)
        tfin = wfin
        bsyn3 = w2s[0:96, 0, 0:HID // 2].bitcast(BF16)

        xs = sb("xs", [P, T, D])
        xr = sb("xr", [P, T, D])
        xnT = sb("xnT", [P, KD, B * S])
        early = sb("early", [P, 4, 2 * 2 * D])
        qkn = early[:, 0, :].rearrange("p (i a n) -> p i a n", i=2, a=2)
        sq = early[:, 1, :].rearrange("p (i n) -> p i n", i=2)
        qst = early[:, 2, :].bitcast(FP16).rearrange("p (i h s d) -> p i h s d", i=2, h=HEADS, s=4)
        kst = early[:, 3, :].bitcast(FP16).rearrange("p (i h s d) -> p i h s d", i=2, h=HEADS, s=4)
        stacks = sb("stacks", [P, 2, PAIRS, B * S], FP16)
        qT, kT = stacks[:, 0], stacks[:, 1]
        vaug = sb("vaug", [P, T, HEADS, 2 * DH])
        probs = sb("probs", [P, 4, 1024])
        late = sb("late", [P, 4, 2 * D])
        oT = late[:, 0:2]
        otm = late[:, 2].rearrange("p (i d) -> p i d", i=TPB)
        oTn = late[:, 3]
        yT = xnT
        yq = wqkv[:, :, :].rearrange("p k n -> p (k n)")[:, 0:B * S].bitcast(FP16).rearrange("p (k n) -> p k n", k=KD)
        hid = stacks[:, :, :, :].rearrange("p a b n -> p (a b n)").bitcast(F32).rearrange("p (f n) -> p f n", f=FT)
        hq = early[:, :, :].rearrange("p a n -> p (a n)").bitcast(FP16).rearrange("p (f n) -> p f n", f=FT)
        x1 = xs
        xb2 = sb("xb2", [P, T, D])
        x1b = wsyn[:, :, :].rearrange("p k n -> p (k n)").rearrange("p (t d) -> p t d", t=T)
        x2f = wemb[:, :, :].rearrange("p k (b n) -> p b k n", b=2)
        x2h = w1q[:, :, :].rearrange("p f d -> p (f d)").rearrange("p (k n) -> p k n", k=KD)
        x2l = w2q
        zp = vaug[:, :, :, :].rearrange("p t h d -> p (t h d)").rearrange("p (i n) -> p i n", i=4)
        hidden = probs[:, 0:2]
        hT = probs[:, 2:4]
        below = w1s[:, :, :].rearrange("p f d -> p (f d)")[:, 0:HID]
        junk = [early[:, 0, HID // 2 * j:HID // 2 * (j + 1)].bitcast(BF16) for j in range(2)]
        junk_v = yT[:, 0, 0:HID // 2].bitcast(BF16)
        tmp = w2s[:, 1, :]
        fin, fin_g, x4, xh = [late[:, j].rearrange("p (i d) -> p i d", i=2) for j in range(4)]

        ssx = sb("ssx", [P, T])
        msx = sb("msx", [P, T])
        rx = sb("rx", [P, T])
        mod_a = sb("mod_a", [P, KD, B])
        mod_b = sb("mod_b", [P, KD, B])
        bemb1 = sb("bemb1", [P, KD])
        gg = sb("gg", [P, DH])
        ggt = sb("ggt", [P, D])
        ggmax = sb("ggmax", [P, 1])
        nbound = sb("nbound", [P, 1])
        ssq = sb("ssq", [P, 2, 2 * HEADS])
        msq = sb("msq", [P, 2, 2 * HEADS])
        rqk = sb("rqk", [P, 2, 2 * HEADS])
        rsum = sb("rsum", [P, 2, HEADS])
        ymax = sb("ymax", [P, B])
        amax = sb("amax", [P, 2])
        amax1 = sb("amax1", [1, 2])
        sx = sb("sx", [P, 2])
        sx_inv = sb("sx_inv", [P, 2])
        s1 = sb("s1", [P, FT])
        s1i = sb("s1i", [P, FT])
        s2 = sb("s2", [P, KD])
        s2i = sb("s2i", [P, KD])
        sc1 = sb("sc1", [P, FT])
        diag = early[:, 1, 0:KD * P].rearrange("p (m n) -> p m n", m=KD)
        s2row = ggt
        scale2 = ggt
        gmax = sb("gmax", [P, FT])
        wsum = sb("wsum", [P, 2])
        wtot = sb("wtot", [P, 2])
        wsc = sb("wsc", [P, 2])
        th = sb("th", [P, 2])
        nth = sb("nth", [P, 2])
        ssyn = sb("ssyn", [P, 1])
        ssyn_inv = sb("ssyn_inv", [P, 1])
        sfin = sb("sfin", [P, 1])
        lnbo = r("b_out")
        bs = r("b_syn")
        bsb = wqkv[:, :, :].rearrange("p k n -> p (k n)")[:, B * S:3 * D * KD].bitcast(BF16)
        brT = sb("brT", [P, KD, B * BLK])
        keys, keys_j, keys_k = [yT[0:B * BLK, 1, D * j:D * j + D] for j in range(3)]
        wq = row[0:B * BLK, ROWS["rms_w"][0]:ROWS["rms_w"][1]]
        raw = sb("raw", [B * BLK, 1])
        kss = sb("kss", [B * BLK, 1])
        kms = sb("kms", [B * BLK, 1])
        rk = sb("rk", [B * BLK, 1])
        score = sb("score", [B * BLK, 1])
        smax = sb("smax", [1, B])
        sdif = sb("sdif", [1, B, BLK])
        sexp = sb("sexp", [1, B, BLK])
        ssum = sb("ssum", [1, B])
        srec = sb("srec", [1, B])
        attn = sb("attn", [1, B, BLK])
        prod = sb("prod", [P, KD, B, BLK])
        att = sb("att", [P, KD, B])
        st1 = sb("st1", [P, T, 6])
        mv1 = sb("mv1", [P, T, 2])
        ve1 = sb("ve1", [P, T])
        rs1 = sb("rs1", [P, T])
        zsum = sb("zsum", [P, T])
        na = sb("na", [P, T, len(NEWTON)])
        nb = sb("nb", [P, T, len(NEWTON)])
        nt = sb("nt", [P, T, len(NEWTON) + 1])
        ne = sb("ne", [P, T])
        signs = sb("signs", [P, T, len(NEWTON)])
        tpos = sb("tpos", [P, T])
        cnt = sb("cnt", [P, T])
        rank = sb("rank", [P, T])
        m8 = sb("m8", [P, T, 8])
        j8 = sb("j8", [P, 8])
        j8b = sb("j8b", [P, 8])
        thresh = sb("thresh", [P, T])
        found = sb("found", [P, T])
        worst = sb("worst", [1, B])
        flag = sb("flag", [1, B], I32)
        st2 = sb("st2", [P, T, 6])
        mv2 = sb("mv2", [P, T, 2])
        ve2 = sb("ve2", [P, T])
        rs2 = sb("rs2", [P, T])

        ld_x = [sem(f"ld_x{b}") for b in range(B)]
        (ld_col, ld_row, ld_emb, ld_qkv, ld_out, ld_w1, ld_w2, ld_wk, ld_wo, ld_syn, ld_fin) = [
            sem("ld_" + n) for n in "col row emb qkv out w1 w2 wk wo syn fin".split()]
        consts = sem("consts")
        casts = sem("casts")
        pool_step = sem("pool_step")
        dve_step = sem("dve_step")
        x_squared = sem("x_squared")
        x_rstd = sem("x_rstd")
        x_scaled = sem("x_scaled")
        xT_ready = sem("xT_ready")
        xT_moved = sem("xT_moved")
        cond_ready = sem("cond_ready")
        mod_ready = sem("mod_ready")
        qk_ready = sem("qk_ready")
        v_ready = sem("v_ready")
        v_moved = sem("v_moved")
        qk_squared = sem("qk_squared")
        qk_summed = sem("qk_summed")
        qk_rstd = sem("qk_rstd")
        qk_normed = sem("qk_normed")
        gg_ready = sem("gg_ready")
        ggt_ready = sem("ggt_ready")
        k_gained = sem("k_gained")
        q_hi = sem("q_hi")
        k_hi = sem("k_hi")
        q_lo = sem("q_lo")
        k_lo = sem("k_lo")
        qT_ready = sem("qT_ready")
        kT_ready = sem("kT_ready")
        qT_moved = sem("qT_moved")
        kT_moved = sem("kT_moved")
        s_ready = sem("s_ready")
        exp_done = sem("exp_done")
        pv_done = sem("pv_done")
        o_moved = sem("o_moved")
        ot_ready = sem("ot_ready")
        o_normed = sem("o_normed")
        oTn_ready = sem("oTn_ready")
        oTn_moved = sem("oTn_moved")
        wout_ready = sem("wout_ready")
        y_ready = sem("y_ready")
        y_moved = sem("y_moved")
        w1_inv = sem("w1_inv")
        w2_inv = sem("w2_inv")
        w1_scaled = sem("w1_scaled")
        w2_scaled = sem("w2_scaled")
        w_quant = sem("w_quant")
        wT_ready = sem("wT_ready")
        wT_moved = sem("wT_moved")
        w_summed = sem("w_summed")
        w_total = sem("w_total")
        syn_inv = sem("syn_inv")
        tern_ready = sem("tern_ready")
        bsyn_ready = sem("bsyn_ready")
        xb2_ready = sem("xb2_ready")
        diag_ready = sem("diag_ready")
        s2row_ready = sem("s2row_ready")
        s2row_moved = sem("s2row_moved")
        am_col = sem("am_col")
        am_row = sem("am_row")
        am_one = sem("am_one")
        am_all = sem("am_all")
        sx_ready = sem("sx_ready")
        y_scaled = sem("y_scaled")
        yq_ready = sem("yq_ready")
        f1_ready = sem("f1_ready")
        gelu_done = sem("gelu_done")
        hq_pool = sem("hq_pool")
        h_scaled = sem("h_scaled")
        hq_dve = sem("hq_dve")
        f2_ready = sem("f2_ready")
        f2_scaled = sem("f2_scaled")
        x1_ready = sem("x1_ready")
        br_ready = sem("br_ready")
        br_moved = sem("br_moved")
        keys_ready = sem("keys_ready")
        keys_moved = sem("keys_moved")
        keys_sq = sem("keys_sq")
        keys_rstd = sem("keys_rstd")
        score_ready = sem("score_ready")
        score_row = sem("score_row")
        score_dif = sem("score_dif")
        score_exp = sem("score_exp")
        attn_ready = sem("attn_ready")
        attn_all = sem("attn_all")
        att_ready = sem("att_ready")
        pr_ready = sem("pr_ready")
        ln_stats = sem("ln_stats")
        ln_rstd = sem("ln_rstd")
        xhat_ready = sem("xhat_ready")
        x2T_ready = sem("x2T_ready")
        x2T_moved = sem("x2T_moved")
        x2_hi = sem("x2_hi")
        x2_lo = sem("x2_lo")
        lnbo_ready = sem("lnbo_ready")
        x2b_ready = sem("x2b_ready")
        x1b_ready = sem("x1b_ready")
        z_ready = sem("z_ready")
        z_relu = sem("z_relu")
        guess = [sem(f"guess{i}") for i in range(len(NEWTON) + 1)]
        counted = [sem(f"counted{i}") for i in range(len(NEWTON))]
        thresh_found = sem("thresh_found")
        found_sum = sem("found_sum")
        hid_ready = sem("hid_ready")
        hT_ready = sem("hT_ready")
        hT_act = sem("hT_act")
        hT_dve = sem("hT_dve")
        out_ready = sem("out_ready")
        x4_stats = sem("x4_stats")
        x4_rstd = sem("x4_rstd")
        x4_hat = sem("x4_hat")
        fin_ready = sem("fin_ready")
        stored = [sem("stored0"), sem("stored1")]

        N_CONST = 5
        POOL_F = (2, 6)
        ACT_F = (1, 3, 5, 7)
        steps = {"pool": 0, "dve": 0}

        def chain(eng, which, s, ins):
            steps[which] += 1
            ins.then_inc(s, 1)
            eng.wait_ge(s, steps[which])

        block = ctx.enter_context(nc.Block())

        @block.sync
        def _(sp):
            sp.dma_start(col[:, :], cols).then_inc(ld_col, 16)
            for b in range(B):
                sp.dma_start(xs[:, TPB * b:TPB * b + TPB, :],
                             x[S * b:S * b + S, :].rearrange("(t p) d -> p t d", p=P)).then_inc(ld_x[b], 16)
                if b == 0:
                    sp.dma_start(wemb[:, :, :], w_emb.rearrange("(k p) n -> p k n", p=P)).then_inc(ld_emb, 16)
                    sp.dma_start(wqkv[:, :, :], w_qkv.rearrange("(k p) n -> p k n", p=P)).then_inc(ld_qkv, 16)
                    sp.dma_start(row[:, :], rows.broadcast_to([P, NROWS])).then_inc(ld_row, 16)
            for dst, src, s in ((w1s, w1, ld_w1), (wout, w_out, ld_out), (w2s, w2, ld_w2), (wsyn, wsyn_t, ld_syn),
                                (wfin, wout_t, ld_fin), (wk, wk_t, ld_wk), (wo, wo_t, ld_wo)):
                sp.dma_start(dst[:, :, :], src.rearrange("(k p) n -> p k n", p=P)).then_inc(s, 16)
            for t in range(T):
                sp.wait_ge(fin_ready, t + 1)
                sp.dma_start(out[t * P:t * P + P, :], fin[:, t % 2, :]).then_inc(stored[t % 2], 16)
            for s in stored:
                sp.wait_ge(s, 16 * T // 2)

        @block.gpsimd
        def _(pool):
            def step(ins):
                chain(pool, "pool", pool_step, ins)

            def rstd(out_, mean_sq, sums, scale, eps):
                step(pool.tensor_scalar(mean_sq, sums, scale, eps, ALU.mult, ALU.add))
                return pool.tensor_tensor(out_, mean_sq, neg_half[0:out_.shape[0], 0:out_.shape[1]], ALU.pow)

            step(pool.memset(ident[:, :], 0.0))
            pool.affine_select(out=ident[:, :], in_=ident[:, :], compare_op=ALU.not_equal, fill=1.0, base=0,
                               pattern=[[-1, P]], channel_multiplier=1).then_inc(consts, 1)
            pool.memset(neg_half[:, :], -0.5)
            pool.memset(ones[:, :], 1.0).then_inc(consts, 1)
            step(pool.memset(block_of[:, :], 0.0))
            for j in range(P // BLK_TOKENS):
                step(pool.memset(block_of[BLK_TOKENS * j:BLK_TOKENS * (j + 1), j:j + 1], 1.0))
            pool.memset(round_col[:, :], ROUND)
            pool.memset(ones8[:, :], 1.0)
            for j in range(8):
                pool.memset(iota8[:, j:j + 1], float(j + 1))
            for j, f in enumerate(NEWTON):
                pool.memset(newton_c[:, j:j + 1], -0.5 * f * STEP)
            step(pool.memset(sel3[:, :], 0.0))
            for j in range(3):
                step(pool.memset(sel3[32 * j:32 * j + 1, :], 1.0))
            pool.memset(vaug[:, :, :, DH:2 * DH], 1.0).then_inc(consts, 3)

            for b in range(B):
                pool.wait_ge(x_squared, TPB * (b + 1))
                t = slice(TPB * b, TPB * b + TPB)
                rstd(rx[:, t], msx[:, t], ssx[:, t], 1.0 / D, 1e-6).then_inc(x_rstd, 1)
                if b == 0:
                    pool.wait_ge(gg_ready, 1)
                    pool.tensor_copy(ggt[:, :].rearrange("p (h d) -> p h d", h=HEADS),
                                     gg[:, :].unsqueeze(1).broadcast_to([P, HEADS, DH])).then_inc(ggt_ready, 1)
            pool.wait_ge(ggt_ready, 1)
            for t in range(T):
                i = t % 2
                pool.wait_ge(qk_summed, t + 1)
                rstd(rqk[:, i, :], msq[:, i, :], ssq[:, i, :], 1.0 / (DH * QK_SCALE ** 2),
                     1e-6 / QK_SCALE ** 2).then_inc(qk_rstd, 1)
                pool.wait_ge(qk_normed, t + 1)
                pool.tensor_tensor(qkn[:, i, 1, :], qkn[:, i, 1, :], ggt[:, :], ALU.mult).then_inc(k_gained, 1)
                pool.wait_ge(k_gained, t + 1)
                if t >= 2:
                    pool.wait_ge(kT_ready, t - 1)
                pool.tensor_scalar(kst[:, i, :, 0::2, :],
                                   qkn[:, i, 1, :].rearrange("p (h d) -> p h d", h=HEADS).unsqueeze(2)
                                   .broadcast_to([P, HEADS, 2, DH]), 1.0, 1.0, ALU.mult, ALU.mult).then_inc(k_hi, 1)
            pool.wait_ge(w1_inv, 1)
            pool.tensor_tensor(w1s[:, :, :], w1s[:, :, :], s1i[:, :].unsqueeze(2).broadcast_to([P, FT, D]),
                               ALU.mult).then_inc(w1_scaled, 1)
            pool.wait_ge(w2_inv, 1)
            pool.tensor_tensor(w2s[:, :, :], w2s[:, :, :], s2i[:, :].unsqueeze(2).broadcast_to([P, KD, HID]),
                               ALU.mult).then_inc(w2_scaled, 1)
            pool.wait_ge(w_summed, 1)
            pool.partition_all_reduce(wtot[:, :], wsum[:, :], P, bass.bass_isa.ReduceOp.add).then_inc(w_total, 1)
            pool.wait_ge(ld_x[B - 1], 16)
            for t in range(T):
                pool.tensor_tensor(xb2[:, t, :], xs[:, t, :], r("b2"), ALU.add).then_inc(xb2_ready, 1)
            pool.wait_ge(syn_inv, 1)
            step(pool.tensor_scalar(bs, r("b_syn"), ssyn_inv[:, 0:1], 1.0, ALU.mult, ALU.mult))
            for j in range(3):
                step(pool.tensor_scalar(bsyn3[32 * j:32 * j + 32, :], bs[32 * j:32 * j + 32, :], 1.0, 1.0, ALU.mult,
                                        ALU.mult))
                if j < 2:
                    step(pool.tensor_scalar(bsb, bs, 1.0, 1.0, ALU.mult, ALU.mult))
                    step(pool.tensor_tensor(bs, bs, bsb, ALU.subtract))
            pool.tensor_tensor(lnbo, r("ln_beta"), r("b_out"), ALU.add).then_inc(bsyn_ready, 1)
            pool.wait_ge(bsyn_ready, 1)
            pool.tensor_tensor(wq, row[0:B * BLK, ROWS["rms_w"][0]:ROWS["rms_w"][1]],
                               row[0:B * BLK, ROWS["query"][0]:ROWS["query"][1]], ALU.mult).then_inc(lnbo_ready, 1)

            pool.wait_ge(sx_ready, 2)
            for f in POOL_F:
                step(pool.tensor_scalar(hid[:, f, :], hid[:, f, :], sx_inv[:, 1:2], ROUND, ALU.mult, ALU.add))
                pool.tensor_scalar(hq[:, f, :], hid[:, f, :], 1.0, -ROUND, ALU.mult, ALU.add).then_inc(hq_pool, 1)
            for t in range(T):
                pool.wait_ge(f2_scaled, t + 1)
                pool.tensor_tensor(x1[:, t, :], xr[:, t, :], xb2[:, t, :], ALU.add).then_inc(x1_ready, 1)
            pool.wait_ge(keys_sq, 1)
            rstd(rk[:, :], kms[:, :], kss[:, :], 1.0 / D, 1e-6).then_inc(keys_rstd, 1)

            def x2_bias(t):
                pool.wait_ge(xhat_ready, t + 1)
                pool.tensor_tensor(xb2[:, t, :], xr[:, t, :], r("ln_gamma"), ALU.mult).then_inc(pool_step, 1)
                steps["pool"] += 1
                pool.wait_ge(pool_step, steps["pool"])
                pool.tensor_tensor(xb2[:, t, :], xb2[:, t, :], lnbo, ALU.add).then_inc(x2b_ready, 1)
                pool.tensor_tensor(x1b[:, t, :], x1[:, t, :], r("beta"), ALU.add).then_inc(x1b_ready, 1)

            def x2_split(b):
                pool.wait_ge(x2T_moved, KD * (b + 1))
                pool.tensor_scalar(x2h[:, :, S * b:S * b + S], x2f[:, b % 2, :, :], 1.0, 1.0, ALU.mult,
                                   ALU.mult).then_inc(x2_hi, 1)

            def ln1(b):
                pool.wait_ge(ln_stats, TPB * (b + 1))
                t = slice(TPB * b, TPB * b + TPB)
                rstd(rs1[:, t], ve1[:, t], mv1[:, t, 1], 1.0, 1e-6).then_inc(ln_rstd, 1)

            def guess0(t):
                pool.wait_ge(z_relu, t + 1)
                pool.tensor_scalar(nt[:, t, 0:1], zsum[:, t:t + 1], -START, 0.0, ALU.mult, ALU.add).then_inc(guess[0], 1)
                step(pool.tensor_scalar(na[:, t, :], newton_c[:, :], zsum[:, t:t + 1], 1.0, ALU.mult, ALU.mult))
                pool.tensor_scalar(nb[:, t, :], na[:, t, :], float(HID - 2 * AIM), 0.0, ALU.mult, ALU.add)

            def newton(i, t):
                pool.wait_ge(counted[i], t + 1)
                step(pool.tensor_scalar(ne[:, t:t + 1], signs[:, t, i:i + 1], na[:, t, i:i + 1], nb[:, t, i:i + 1],
                                        ALU.mult, ALU.add))
                ins = pool.tensor_tensor(nt[:, t, i + 1:i + 2], nt[:, t, i:i + 1], ne[:, t:t + 1], ALU.add)
                if i + 1 < len(NEWTON):
                    ins.then_inc(guess[i + 1], 1)
                else:
                    step(ins)
                    pool.tensor_scalar(tpos[:, t:t + 1], nt[:, t, i + 1:i + 2], -1.0, 0.0, ALU.mult,
                                       ALU.add).then_inc(guess[i + 1], 1)

            def final_rstd(t):
                pool.wait_ge(x4_stats, t + 1)
                rstd(rs2[:, t:t + 1], ve2[:, t:t + 1], mv2[:, t, 1:2], 1.0, 1e-5).then_inc(x4_rstd, 1)

            def final(t):
                pool.wait_ge(x4_hat, t + 1)
                step(pool.tensor_tensor(fin_g[:, t % 2, :], xh[:, t % 2, :], r("gamma"), ALU.mult))
                if t >= 2:
                    pool.wait_ge(stored[t % 2], 16 * (t // 2))
                pool.tensor_tensor(fin[:, t % 2, :], fin_g[:, t % 2, :], x1b[:, t, :], ALU.add).then_inc(fin_ready, 1)

            for b in range(B):
                ln1(b)
                if b >= 1:
                    x2_split(b - 1)
            pool.wait_ge(lnbo_ready, 1)
            for i in range(T + 5):
                if i < T:
                    guess0(i)
                if 0 <= i - 1 < T:
                    newton(0, i - 1)
                if 0 <= i - 2 < T:
                    newton(2, i - 2)
                if 0 <= i - 1 < T:
                    newton(1, i - 1)
                if 0 <= i - 2 < T:
                    newton(3, i - 2)
                if i == 0:
                    x2_split(B - 1)
                if i < T:
                    x2_bias(i)
                if 0 <= i - 5 < T:
                    final_rstd(i - 5)
                    final(i - 5)

        @block.scalar
        def _(act):
            def evac_xT(b):
                act.wait_ge(xT_ready, b + 1)
                for k in range(KD):
                    nc.scalar.activation(xnT[:, k, S * b:S * b + S], bank(0)[:, S * k:S * k + S], ACT.Identity,
                                         bias=mod_b[:, k, b:b + 1], scale=mod_a[:, k, b:b + 1]).then_inc(xT_moved, 1)

            for t in range(T):
                act.wait_ge(ld_x[t // TPB], 16)
                nc.scalar.activation(early[:, t // 4, D * (t % 4):D * (t % 4) + D], xs[:, t, :], ACT.Square,
                                     accum_out=ssx[:, t:t + 1]).then_inc(x_squared, 1)
            act.wait_ge(mod_ready, 1)
            evac_xT(0)
            act.wait_ge(x_squared, T)
            for t in range(T + 2):
                i = t % 2
                if t < T:
                    act.wait_ge(qk_ready, t + 1)
                    if t >= 2:
                        act.wait_ge(qk_summed, t - 1)
                    nc.scalar.activation(sq[:, i, :], bank(1 + i), ACT.Square).then_inc(qk_squared, 1)
                    act.wait_ge(v_ready, t + 1)
                    nc.scalar.activation(vaug[:, t, :, 0:DH],
                                         bank(3 + i)[:, 0:D].rearrange("p (h d) -> p h d", h=HEADS),
                                         ACT.Copy).then_inc(v_moved, 1)
                    if i == 0 and t // TPB + 1 < B:
                        evac_xT(t // TPB + 1)
                if 1 <= t <= T:
                    j = (t - 1) % 2
                    act.wait_ge(qk_normed, t)
                    if t >= 3:
                        act.wait_ge(qT_ready, t - 2)
                    nc.scalar.activation(qst[:, j, :, 0:2, :],
                                         qkn[:, j, 0, :].rearrange("p (h d) -> p h d", h=HEADS).unsqueeze(2)
                                         .broadcast_to([P, HEADS, 2, DH]), ACT.Copy).then_inc(q_hi, 1)
                if 2 <= t:
                    act.wait_ge(kT_ready, t - 1)
                    nc.scalar.activation(kT[:, :, P * (t - 2):P * (t - 1)],
                                         bank(6).bitcast(FP16).rearrange("p (a n) -> p a n", a=PAIRS),
                                         ACT.Copy).then_inc(kT_moved, 1)

            act.wait_ge(gg_ready, 2)
            for u in range(B * PAIRS):
                act.wait_ge(s_ready, u + 1)
                if u >= 4:
                    act.wait_ge(pv_done, (u - 4) // 2 + 1)
                nc.scalar.activation(probs[:, u % 4, :], pairs[u % 2][:, :], ACT.Exp, bias=nbound[:, 0:1],
                                     scale=DH ** -0.5 / QK_SCALE ** 2).then_inc(exp_done, 1)

            act.wait_ge(sx_ready, 1)
            nc.scalar.activation(tmp[:, :], yT[:, 1, :], ACT.Identity, bias=round_col[:, 0:1],
                                 scale=sx_inv[:, 0:1]).then_inc(y_scaled, 1)
            act.wait_ge(ld_col, 16)
            for f in range(FT):
                act.wait_ge(f1_ready, f + 1)
                nc.scalar.activation(hid[:, f, :], pairs[f % 2][:, :], ACT.Gelu,
                                     bias=col[:, COLS["b1"][0] + f:COLS["b1"][0] + f + 1],
                                     scale=sc1[:, f:f + 1]).then_inc(gelu_done, 1)
            act.wait_ge(sx_ready, 2)
            act.wait_ge(gelu_done, FT)
            for f in ACT_F:
                nc.scalar.activation(hid[:, f, :], hid[:, f, :], ACT.Identity, bias=round_col[:, 0:1],
                                     scale=sx_inv[:, 1:2]).then_inc(h_scaled, 1)

            act.wait_ge(keys_moved, 1)
            nc.scalar.activation(keys_j, keys, ACT.Square, accum_out=kss[:, :]).then_inc(keys_sq, 1)
            act.wait_ge(score_dif, 1)
            nc.scalar.activation(sexp[:, :, :], sdif[:, :, :], ACT.Exp).then_inc(score_exp, 1)

            def evac_x2T(b):
                act.wait_ge(x2T_ready, b + 1)
                if b >= 2:
                    act.wait_ge(x2_lo, b - 1)
                for k in range(KD):
                    nc.scalar.activation(x2f[:, b % 2, k, :], bank(6)[:, S * k:S * k + S], ACT.Identity,
                                         bias=col[:, COLS["ln_beta"][0] + k:COLS["ln_beta"][0] + k + 1],
                                         scale=col[:, COLS["ln_gamma"][0] + k:COLS["ln_gamma"][0] + k + 1]
                                         ).then_inc(x2T_moved, 1)

            counts = []

            def relu(t):
                act.wait_ge(z_ready, t + 1)
                if t >= 4:
                    act.wait_ge(hid_ready, t - 3)
                nc.scalar.activation(zp[:, t % 4, :], pairs[t % 2][:, :], ACT.Relu,
                                     accum_out=zsum[:, t:t + 1]).then_inc(z_relu, 1)

            def count(i, t):
                act.wait_ge(guess[i], t + 1)
                if len(counts) >= 2:
                    act.wait_ge(*counts[-2])
                counts.append((counted[i], t + 1))
                nc.scalar.activation(junk[len(counts) % 2], zp[:, t % 4, :], ACT.Sign, bias=nt[:, t, i:i + 1],
                                     accum_out=signs[:, t, i:i + 1]).then_inc(counted[i], 1)

            def move_hT(t):
                act.wait_ge(hT_ready, t + 1)
                if t >= 2:
                    act.wait_ge(out_ready, t - 1)
                nc.scalar.activation(hT[:, t % 2, 0:512], bank(4), ACT.Copy).then_inc(hT_act, 1)

            evac_x2T(0)
            evac_x2T(1)
            act.wait_ge(z_ready, 1)
            for i in range(T + 5):
                if i < T:
                    relu(i)
                if i == 0:
                    evac_x2T(2)
                    evac_x2T(3)
                if 0 <= i - 1 < T:
                    count(0, i - 1)
                if 0 <= i - 2 < T:
                    count(2, i - 2)
                if 0 <= i - 1 < T:
                    count(1, i - 1)
                if 0 <= i - 2 < T:
                    count(3, i - 2)
                if 0 <= i - 4 < T:
                    move_hT(i - 4)

        @block.vector
        def _(dve):
            def step(ins):
                chain(dve, "dve", dve_step, ins)

            dve.wait_ge(consts, 1)
            dve.tensor_copy(ident_h[:, :], ident[:, :]).then_inc(casts, 1)
            for b in range(B):
                dve.wait_ge(x_rstd, b + 1)
                for t in range(TPB * b, TPB * b + TPB):
                    dve.tensor_scalar(xr[:, t, :], xs[:, t, :], rx[:, t:t + 1], None, ALU.mult).then_inc(x_scaled, 1)
                if b == 0:
                    dve.wait_ge(ld_col, 16)
                    step(dve.tensor_scalar(bemb1[:, :], col[:, COLS["b_emb"][0]:COLS["b_emb"][0] + KD], 1.0, None, ALU.add))
                    dve.wait_ge(cond_ready, 1)
                    for k in range(KD):
                        dve.tensor_scalar(mod_a[:, k, :], bank(7)[:, B * k:B * k + B], bemb1[:, k:k + 1],
                                          col[:, COLS["g_norm"][0] + k:COLS["g_norm"][0] + k + 1], ALU.add, ALU.mult)
                        bk = COLS["b_emb"][0] + KD + k
                        ins = dve.tensor_scalar(mod_b[:, k, :], bank(7)[:, B * (KD + k):B * (KD + k) + B],
                                                col[:, bk:bk + 1], None, ALU.add)
                    ins.then_inc(mod_ready, 1)
                    dve.wait_ge(ld_row, 16)
                    dve.tensor_tensor(gg[:, :], r("g_q"), r("g_k"), ALU.mult).then_inc(gg_ready, 1)
                    dve.wait_ge(gg_ready, 1)
                    step(dve.tensor_reduce(ggmax[:, :], gg[:, :], AX.X, ALU.max, apply_absolute_value=True))
                    dve.tensor_scalar(nbound[:, :], ggmax[:, :], -(float(DH) ** 0.5), None, ALU.mult).then_inc(gg_ready, 1)

            def move_qT(t):
                dve.wait_ge(qT_ready, t + 1)
                dve.tensor_copy(qT[:, :, P * t:P * t + P],
                                bank(5).bitcast(FP16).rearrange("p (a n) -> p a n", a=PAIRS)).then_inc(qT_moved, 1)

            def split_low(t):
                i = t % 2
                dve.wait_ge(q_hi, t + 1)
                dve.tensor_tensor(qst[:, i, :, 2:4, :],
                                  qkn[:, i, 0, :].rearrange("p (h d) -> p h d", h=HEADS).unsqueeze(2)
                                  .broadcast_to([P, HEADS, 2, DH]), qst[:, i, :, 0:2, :], ALU.subtract).then_inc(q_lo, 1)
                dve.wait_ge(k_hi, t + 1)
                dve.tensor_tensor(kst[:, i, :, 1::2, :],
                                  qkn[:, i, 1, :].rearrange("p (h d) -> p h d", h=HEADS).unsqueeze(2)
                                  .broadcast_to([P, HEADS, 2, DH]), kst[:, i, :, 0::2, :], ALU.subtract).then_inc(k_lo, 1)

            for t in range(T + 2):
                i = t % 2
                if t < T:
                    dve.wait_ge(qk_squared, t + 1)
                    if t >= 2:
                        dve.wait_ge(qk_rstd, t - 1)
                    dve.tensor_reduce(ssq[:, i, :], sq[:, i, :].rearrange("p (h d) -> p h d", d=DH), AX.X,
                                      ALU.add).then_inc(qk_summed, 1)
                if 2 <= t:
                    move_qT(t - 2)
                if 1 <= t <= T:
                    split_low(t - 1)
                if t < T:
                    dve.wait_ge(qk_rstd, t + 1)
                    if t >= 2:
                        dve.wait_ge(q_lo, t - 1)
                        dve.wait_ge(k_lo, t - 1)
                    dve.tensor_tensor(qkn[:, i, :, :].rearrange("p a (h d) -> p (a h) d", d=DH),
                                      bank(1 + i).rearrange("p (h d) -> p h d", d=DH),
                                      rqk[:, i, :].unsqueeze(2).broadcast_to([P, 2 * HEADS, DH]),
                                      ALU.mult).then_inc(qk_normed, 1)

            def scales(w, ld, s, s_inv, ready):
                dve.wait_ge(ld, 16)
                step(dve.tensor_reduce(s[:, :], w[:, :, :], AX.X, ALU.max, apply_absolute_value=True))
                step(dve.tensor_scalar(s[:, :], s[:, :], 1.0 / QMAX, 1e-8, ALU.mult, ALU.max))
                dve.reciprocal(s_inv[:, :], s[:, :]).then_inc(ready, 1)

            def quantise(w, q, scaled):
                dve.wait_ge(scaled, 1)
                dve.tensor_scalar(q[:, :, :], w[:, :, :], ROUND, -ROUND, ALU.add, ALU.add).then_inc(w_quant, 1)

            def weight_sums():
                dve.wait_ge(ld_syn, 16)
                dve.tensor_reduce(wsum[:, 0:1], wsyn[:, :, :], AX.XY, ALU.add, apply_absolute_value=True)
                dve.wait_ge(ld_fin, 16)
                dve.tensor_reduce(wsum[:, 1:2], wfin[:, :, :], AX.XY, ALU.add,
                                  apply_absolute_value=True).then_inc(w_summed, 1)

            def ternary_scales():
                dve.wait_ge(w_total, 1)
                step(dve.tensor_scalar(wsc[:, :], wtot[:, :], 1.0 / (HID * D), None, ALU.mult))
                step(dve.tensor_scalar(th[:, :], wsc[:, :], 1e-8, 0.5, ALU.add, ALU.mult))
                step(dve.tensor_scalar(nth[:, :], th[:, :], -1.0, None, ALU.mult))
                step(dve.tensor_scalar(ssyn[:, :], wsc[:, 0:1], 1e-30, None, ALU.max))
                dve.reciprocal(ssyn_inv[:, :], ssyn[:, :]).then_inc(syn_inv, 1)
                dve.tensor_tensor(sfin[:, :], ssyn[:, :], wsc[:, 1:2], ALU.mult)

            def ternary(w, q, i):
                flat_w = w[:, :, :].rearrange("p a n -> p (a n)")
                flat_q = q[:, :, :].rearrange("p a n -> p (a n)")
                minus = w1s[:, :, :].rearrange("p f d -> p (f d)")
                step(dve.tensor_scalar(minus, flat_w, nth[:, i:i + 1], None, ALU.is_lt))
                dve.scalar_tensor_tensor(out=flat_q, in0=flat_w, scalar=th[:, i:i + 1], in1=minus, op0=ALU.is_gt,
                                         op1=ALU.subtract).then_inc(tern_ready, 1)

            def out_weights():
                dve.wait_ge(ld_out, 16)
                for k in range(KD):
                    ins = dve.tensor_tensor(wout[:, k, P * k:P * k + P], wout[:, k, P * k:P * k + P], ident[:, :], ALU.add)
                ins.then_inc(wout_ready, 1)

            def move_o(q):
                dve.wait_ge(pv_done, 2 * q + 2)
                if q >= 2:
                    dve.wait_ge(ot_ready, TPB * (q // 2))
                dve.tensor_copy(oT[:, q % 2, :], bank(4 + q % 2)).then_inc(o_moved, 1)

            def norm_o(t):
                i = t % TPB
                dve.wait_ge(ot_ready, t + 1)
                if t >= TPB:
                    dve.wait_ge(oTn_ready, t // TPB)
                view = bank(6 + i).rearrange("p (h d) -> p h d", h=HEADS)
                step(dve.reciprocal(rsum[:, i, :], view[:, :, DH]))
                dve.tensor_tensor(otm[:, i, :].rearrange("p (h d) -> p h d", h=HEADS), view[:, :, 0:DH],
                                  rsum[:, i, :].unsqueeze(2).broadcast_to([P, HEADS, DH]), ALU.mult).then_inc(o_normed, 1)

            def move_oTn(b):
                dve.wait_ge(oTn_ready, b + 1)
                if b >= 1:
                    dve.wait_ge(y_ready, b)
                dve.tensor_copy(oTn[:, :], bank(6)).then_inc(oTn_moved, 1)

            def move_y(b):
                dve.wait_ge(y_ready, b + 1)
                dve.tensor_reduce(ymax[:, b:b + 1], bank(7), AX.X, ALU.max, apply_absolute_value=True)
                dve.tensor_copy(yT[:, :, S * b:S * b + S],
                                bank(7).rearrange("p (m n) -> p m n", m=KD)).then_inc(y_moved, 1)

            def move_wT(i):
                dve.wait_ge(wT_ready, i + 1)
                src = bank(6).bitcast(FP16)
                if i < KD:
                    dve.tensor_copy(w1qT[:, i, :], src).then_inc(wT_moved, 1)
                else:
                    m = i - KD
                    dve.tensor_copy(w2qT[:, :, P * m:P * m + P], src.rearrange("p (f n) -> p f n", f=FT)).then_inc(wT_moved, 1)

            scales(w1s, ld_w1, s1, s1i, w1_inv)
            out_weights()
            for b in range(B):
                move_o(2 * b)
                if b == 0:
                    quantise(w1s, w1q, w1_scaled)
                    scales(w2s, ld_w2, s2, s2i, w2_inv)
                if b == 1:
                    weight_sums()
                if b == 2:
                    ternary_scales()
                    ternary(wsyn, tsyn, 0)
                if b == 3:
                    ternary(wfin, tfin, 1)
                move_o(2 * b + 1)
                norm_o(TPB * b)
                norm_o(TPB * b + 1)
                move_oTn(b)
                move_y(b)
                move_wT(b)
                if b == 0:
                    quantise(w2s, w2q, w2_scaled)
                    for m in range(KD):
                        ins = dve.tensor_scalar(diag[:, m, :], ident[:, :], s2[:, m:m + 1], None, ALU.mult)
                    ins.then_inc(diag_ready, 1)

            def scale_from(src, n):
                dve.tensor_reduce(amax[:, n:n + 1], src, AX.X, ALU.max).then_inc(am_col, 1)
                dve.wait_ge(am_row, n + 1)
                dve.tensor_reduce(amax1[0:1, n:n + 1], bank(4 - 4 * n)[0:1, 0:P], AX.X, ALU.max).then_inc(am_one, 1)
                dve.wait_ge(am_all, n + 1)
                step(dve.tensor_scalar(sx[:, n:n + 1], bank(4 - 4 * n)[:, P:P + 1], 1.0 / QMAX, 1e-8, ALU.mult, ALU.max))
                return dve.reciprocal(sx_inv[:, n:n + 1], sx[:, n:n + 1])

            dve.wait_ge(y_moved, B)
            scale_from(ymax[:, :], 0).then_inc(sx_ready, 1)
            dve.wait_ge(sx_ready, 1)
            step(dve.tensor_scalar(yT[:, 0, :], yT[:, 0, :], sx_inv[:, 0:1], ROUND, ALU.mult, ALU.add))
            dve.tensor_scalar(yq[:, 0, :], yT[:, 0, :], -ROUND, None, ALU.add).then_inc(yq_ready, 1)
            dve.wait_ge(y_scaled, 1)
            dve.tensor_scalar(yq[:, 1, :], tmp[:, :], -ROUND, None, ALU.add).then_inc(yq_ready, 1)
            dve.tensor_scalar(sc1[:, :], s1[:, :], sx[:, 0:1], None, ALU.mult).then_inc(yq_ready, 1)
            dve.wait_ge(s2row_ready, 1)
            dve.tensor_copy(s2row[:, :], bank(5)[:, 0:D]).then_inc(s2row_moved, 1)
            for f in range(FT):
                dve.wait_ge(gelu_done, f + 1)
                ins = dve.tensor_reduce(gmax[:, f:f + 1], hid[:, f, :], AX.X, ALU.max, apply_absolute_value=True)
            step(ins)
            scale_from(gmax[:, :], 1).then_inc(sx_ready, 1)
            dve.wait_ge(sx_ready, 2)
            dve.wait_ge(s2row_moved, 1)
            scaled = 0
            for f in range(FT):
                if f in POOL_F:
                    continue
                if f in ACT_F:
                    scaled += 1
                    dve.wait_ge(h_scaled, scaled)
                else:
                    step(dve.tensor_scalar(hid[:, f, :], hid[:, f, :], sx_inv[:, 1:2], ROUND, ALU.mult, ALU.add))
                dve.tensor_scalar(hq[:, f, :], hid[:, f, :], -ROUND, None, ALU.add).then_inc(hq_dve, 1)
            step(dve.tensor_scalar(scale2[:, :], s2row[:, :], sx[:, 1:2], None, ALU.mult))
            for t in range(T):
                dve.wait_ge(f2_ready, t // TPB + 1)
                dve.tensor_tensor(xr[:, t, :], bank(4 + t // TPB)[:, D * (t % TPB):D * (t % TPB) + D], scale2[:, :],
                                  ALU.mult).then_inc(f2_scaled, 1)

            dve.wait_ge(br_ready, 1)
            dve.tensor_copy(brT[:, :, :].rearrange("p k n -> p (k n)"), bank(0)[:, 0:KD * B * BLK]).then_inc(br_moved, 1)
            dve.wait_ge(keys_ready, 1)
            dve.tensor_copy(keys, bank(1)[0:B * BLK, 0:D]).then_inc(keys_moved, 1)
            dve.wait_ge(keys_moved, 1)
            dve.wait_ge(lnbo_ready, 1)
            dve.scalar_tensor_tensor(out=keys_k, in0=keys, scalar=1.0, in1=wq, op0=ALU.mult,
                                     op1=ALU.mult, accum_out=raw[:, :]).then_inc(dve_step, 1)
            steps["dve"] += 1
            dve.wait_ge(dve_step, steps["dve"])
            dve.wait_ge(keys_rstd, 1)
            dve.tensor_tensor(score[:, :], raw[:, :], rk[:, :], ALU.mult).then_inc(score_ready, 1)
            dve.wait_ge(score_row, 1)
            srow = bank(2)[0:1, 0:B * BLK].rearrange("p (b n) -> p b n", b=B)
            step(dve.tensor_reduce(smax[:, :], srow, AX.X, ALU.max))
            dve.tensor_tensor(sdif[:, :, :], srow, smax[:, :].unsqueeze(2).broadcast_to([1, B, BLK]),
                              ALU.subtract).then_inc(score_dif, 1)
            dve.wait_ge(score_exp, 1)
            step(dve.tensor_reduce(ssum[:, :], sexp[:, :, :], AX.X, ALU.add))
            step(dve.reciprocal(srec[:, :], ssum[:, :]))
            dve.tensor_tensor(attn[:, :, :], sexp[:, :, :], srec[:, :].unsqueeze(2).broadcast_to([1, B, BLK]),
                              ALU.mult).then_inc(attn_ready, 1)
            dve.wait_ge(attn_all, 1)
            for k in range(KD):
                ins = dve.tensor_tensor(prod[:, k, :, :].rearrange("p b n -> p (b n)"), brT[:, k, :],
                                        bank(2)[:, 64:64 + B * BLK], ALU.mult)
            step(ins)
            dve.tensor_reduce(att[:, :, :].rearrange("p k b -> p (k b)"),
                              prod[:, :, :, :].rearrange("p k b n -> p (k b) n"), AX.X, ALU.add).then_inc(att_ready, 1)

            def ln1_stats(b):
                dve.wait_ge(pr_ready, 2 * (b // 2) + 2)
                for t in range(TPB * b, TPB * b + TPB):
                    step(dve.tensor_tensor(xr[:, t, :], x1[:, t, :], pairs[2][:, D * b:D * b + D], ALU.add))
                    step(dve.bn_stats(st1[:, t, :], xr[:, t, :]))
                    dve.bn_aggr(mv1[:, t, :], st1[:, t, :]).then_inc(ln_stats, 1)

            def ln1_hat(b):
                dve.wait_ge(ln_rstd, b + 1)
                for t in range(TPB * b, TPB * b + TPB):
                    dve.tensor_scalar(xr[:, t, :], xr[:, t, :], mv1[:, t, 0:1], rs1[:, t:t + 1], ALU.subtract,
                                      ALU.mult).then_inc(xhat_ready, 1)

            def x2_low(b):
                dve.wait_ge(x2_hi, b + 1)
                dve.tensor_tensor(x2l[:, :, S * b:S * b + S], x2f[:, b % 2, :, :], x2h[:, :, S * b:S * b + S],
                                  ALU.subtract).then_inc(x2_lo, 1)

            for b in range(B + 2):
                if b < B:
                    ln1_stats(b)
                if 1 <= b <= B:
                    ln1_hat(b - 1)
                if 2 <= b:
                    x2_low(b - 2)

            def threshold(t):
                z = zp[:, t % 4, :]
                dve.wait_ge(guess[len(NEWTON)], t + 1)
                dve.tensor_scalar(junk_v, z, tpos[:, t:t + 1], None, ALU.is_ge, ALU.add,
                                  accum_out=cnt[:, t:t + 1]).then_inc(dve_step, 1)
                step(dve.scalar_tensor_tensor(out=below, in0=z, scalar=tpos[:, t:t + 1], in1=z, op0=ALU.is_lt,
                                              op1=ALU.mult))
                steps["dve"] += 1
                dve.wait_ge(dve_step, steps["dve"])
                dve.tensor_scalar(rank[:, t:t + 1], cnt[:, t:t + 1], -1.0, float(TOPK), ALU.mult, ALU.add)
                step(dve.max(m8[:, t, :], below))
                dve.scalar_tensor_tensor(out=j8[:, :], in0=iota8[:, :], scalar=rank[:, t:t + 1], in1=m8[:, t, :],
                                         op0=ALU.is_equal, op1=ALU.mult, accum_out=thresh[:, t:t + 1])
                dve.scalar_tensor_tensor(out=j8b[:, :], in0=iota8[:, :], scalar=rank[:, t:t + 1], in1=ones8[:, :],
                                         op0=ALU.is_equal, op1=ALU.mult,
                                         accum_out=found[:, t:t + 1]).then_inc(thresh_found, 1)

            def any_row(b):
                dve.wait_ge(found_sum, b + 1)
                step(dve.tensor_reduce(worst[0:1, b:b + 1], bank(6)[0:1, TPB * b:TPB * b + TPB], AX.X, ALU.min))
                step(dve.tensor_scalar(flag[0:1, b:b + 1], worst[0:1, b:b + 1], P - 0.5, None, ALU.is_lt))
                missing = dve.value_load(flag[0:1, b:b + 1], min_val=0, max_val=1)
                with dve.If(missing):
                    for t in range(TPB * b, TPB * b + TPB):
                        dve.tensor_copy(below, zp[:, t % 4, :])
                        dve.drain()
                        with dve.Fori(0, FLAT_ROUNDS - 1):
                            dve.max(m8[:, t, :], below)
                            dve.drain()
                            dve.match_replace(below, m8[:, t, :], below, 0.0)
                            dve.drain()
                        dve.max(m8[:, t, :], below)
                        dve.drain()
                        last = TOPK - 8 * (FLAT_ROUNDS - 1) - 1
                        dve.tensor_copy(thresh[:, t:t + 1], m8[:, t, last:last + 1])
                        dve.drain()

            def keep(t):
                z = zp[:, t % 4, :]
                if t >= 2:
                    dve.wait_ge(hT_ready, t - 1)
                dve.scalar_tensor_tensor(out=hidden[:, t % 2, :], in0=z, scalar=thresh[:, t:t + 1], in1=z,
                                         op0=ALU.is_ge, op1=ALU.mult).then_inc(hid_ready, 1)

            def move_hT(t):
                dve.wait_ge(hT_ready, t + 1)
                if t >= 2:
                    dve.wait_ge(out_ready, t - 1)
                dve.tensor_copy(hT[:, t % 2, 512:1024], bank(5)).then_inc(hT_dve, 1)

            def last_stats(t):
                dve.wait_ge(out_ready, t + 1)
                dve.wait_ge(x2b_ready, t + 1)
                step(dve.scalar_tensor_tensor(out=x4[:, t % 2, :], in0=bank(7)[:, 0:D], scalar=sfin[:, 0:1],
                                              in1=xb2[:, t, :], op0=ALU.mult, op1=ALU.add))
                step(dve.bn_stats(st2[:, t, :], x4[:, t % 2, :]))
                dve.bn_aggr(mv2[:, t, :], st2[:, t, :]).then_inc(x4_stats, 1)

            def last_hat(t):
                dve.wait_ge(x4_rstd, t + 1)
                if t >= 2:
                    dve.wait_ge(fin_ready, t - 1)
                dve.tensor_scalar(xh[:, t % 2, :], x4[:, t % 2, :], mv2[:, t, 0:1], rs2[:, t:t + 1], ALU.subtract,
                                  ALU.mult).then_inc(x4_hat, 1)

            for i in range(T + 4):
                if i < T:
                    threshold(i)
                if 0 <= i - 2 < T:
                    move_hT(i - 2)
                if 0 <= i - 3 < T:
                    last_stats(i - 3)
                    last_hat(i - 3)
                if i % TPB == TPB - 1 and i < T:
                    any_row(i // TPB)
                    for t in range(i - TPB + 1, i + 1):
                        keep(t)

        @block.tensor
        def _(pe):
            pe.wait_ge(ld_emb, 16)
            pe.wait_ge(ld_col, 16)
            for m in range(2 * KD):
                for k in range(KD):
                    ins = nc.tensor.matmul(bank(7)[:, B * m:B * m + B], wemb[:, k, P * m:P * m + P],
                                           col[:, B * k:B * k + B], start=(k == 0), stop=(k == KD - 1))
            ins.then_inc(cond_ready, 1)

            def transpose_x(b):
                pe.wait_ge(x_scaled, TPB * (b + 1))
                if b >= 1:
                    pe.wait_ge(xT_moved, KD * b)
                for k in range(KD):
                    for i in range(TPB):
                        ins = nc.tensor.transpose(bank(0)[:, S * k + P * i:S * k + P * i + P],
                                                  xr[:, TPB * b + i, P * k:P * k + P], ident[:, :])
                ins.then_inc(xT_ready, 1)

            def project(t):
                i = t % 2
                pe.wait_ge(xT_moved, KD * (t // TPB + 1))
                if t >= 2:
                    pe.wait_ge(qk_normed, t - 1)
                    pe.wait_ge(v_moved, t - 1)
                for k in range(KD):
                    ins = nc.tensor.matmul(bank(1 + i), xnT[:, k, P * t:P * t + P], wqkv[:, k, 0:2 * D],
                                           start=(k == 0), stop=(k == KD - 1))
                ins.then_inc(qk_ready, 1)
                for k in range(KD):
                    ins = nc.tensor.matmul(bank(3 + i)[:, 0:D], xnT[:, k, P * t:P * t + P], wqkv[:, k, 2 * D:3 * D],
                                           start=(k == 0), stop=(k == KD - 1))
                ins.then_inc(v_ready, 1)

            def transpose_qk(t):
                i = t % 2
                for st, low, moved, ready, bk in ((qst, q_lo, qT_moved, qT_ready, 5), (kst, k_lo, kT_moved, kT_ready, 6)):
                    pe.wait_ge(low, t + 1)
                    if t >= 1:
                        pe.wait_ge(moved, t)
                    dst = bank(bk).bitcast(FP16)
                    for a in range(PAIRS):
                        ins = nc.tensor.transpose(dst[:, P * a:P * a + P],
                                                  st[:, i, 2 * a:2 * a + 2, :, :].rearrange("p h s d -> p (h s d)"),
                                                  ident_h[:, :])
                    ins.then_inc(ready, 1)

            pe.wait_ge(consts, 1)
            transpose_x(0)
            pe.wait_ge(ld_qkv, 16)
            pe.wait_ge(casts, 1)
            for t in range(T + 1):
                if t < T and t % TPB == 0 and t // TPB + 1 < B:
                    transpose_x(t // TPB + 1)
                if t < T:
                    project(t)
                if t >= 1:
                    transpose_qk(t - 1)

            def scores(u):
                b, a = u // PAIRS, u % PAIRS
                pe.wait_ge(qT_moved, TPB * (b + 1))
                pe.wait_ge(kT_moved, TPB * (b + 1))
                if u >= 2:
                    pe.wait_ge(exp_done, u - 1)
                for h in range(2):
                    rows_ = slice(64 * h, 64 * h + 64)
                    for k in range(TPB):
                        at = 512 * h + S * k
                        ins = nc.tensor.matmul(pairs[u % 2][:, at:at + S],
                                               kT[rows_, a, S * b + P * k:S * b + P * k + P],
                                               qT[rows_, a, S * b:S * b + S], start=True, stop=True)
                ins.then_inc(s_ready, 1)

            def weigh(g):
                b, q = g // 4, g // 2
                pe.wait_ge(exp_done, 2 * g + 2)
                if g % 2 == 0 and q >= 2:
                    pe.wait_ge(o_moved, q - 1)
                if g == 2:
                    pe.wait_ge(qT_moved, T)
                for k in range(TPB):
                    for j in range(4):
                        at = 512 * (j % 2) + S * k
                        ins = nc.tensor.matmul(bank(4 + q % 2)[32 * j:32 * j + 32, S * (g % 2):S * (g % 2) + S],
                                               vaug[:, TPB * b + k, 4 * (g % 4) + j, :],
                                               probs[:, (2 * g + j // 2) % 4, at:at + S],
                                               start=(k == 0), stop=(k == TPB - 1), tile_position=(0, 32 * j))
                ins.then_inc(pv_done, 1)

            def tokens_first(b):
                pe.wait_ge(o_moved, 2 * b + 2)
                if b == 0:
                    pe.wait_ge(kT_moved, T)
                else:
                    pe.wait_ge(wT_moved, b)
                    pe.wait_ge(y_moved, b)
                for i in range(TPB):
                    for g in range(4):
                        ins = nc.tensor.transpose(bank(6 + i)[:, P * g:P * g + P],
                                                  oT[:, g // 2, S * (g % 2) + P * i:S * (g % 2) + P * i + P], ident[:, :])
                    ins.then_inc(ot_ready, 1)

            def features_first(b):
                pe.wait_ge(o_normed, TPB * (b + 1))
                for k in range(KD):
                    for i in range(TPB):
                        ins = nc.tensor.transpose(bank(6)[:, S * k + P * i:S * k + P * i + P],
                                                  otm[:, i, P * k:P * k + P], ident[:, :])
                ins.then_inc(oTn_ready, 1)

            def project_out(b):
                pe.wait_ge(oTn_moved, b + 1)
                pe.wait_ge(wout_ready, 1)
                for m in range(KD):
                    for k in range(KD):
                        ins = nc.tensor.matmul(bank(7)[:, S * m:S * m + S], wout[:, k, P * m:P * m + P],
                                               oTn[:, S * k:S * k + S], start=(k == 0), stop=(k == KD - 1))
                ins.then_inc(y_ready, 1)

            def transpose_w(i):
                pe.wait_ge(w_quant, i // KD + 1)
                pe.wait_ge(oTn_moved, i + 1)
                dst = bank(6).bitcast(FP16)
                for f in range(FT):
                    src = w1q[:, f, P * i:P * i + P] if i < KD else w2q[:, i - KD, P * f:P * f + P]
                    ins = nc.tensor.transpose(dst[:, P * f:P * f + P], src, ident_h[:, :])
                ins.then_inc(wT_ready, 1)

            pe.wait_ge(consts, 5)
            pe.wait_ge(qk_normed, T)
            pe.wait_ge(v_moved, T)
            for u in range(B * PAIRS + 7):
                if u < B * PAIRS:
                    scores(u)
                if u >= 2 and u % 2 == 0 and u // 2 - 1 < 4 * B:
                    weigh(u // 2 - 1)
                b, d = u // PAIRS - 1, u % PAIRS
                if b >= 0:
                    if d == 2:
                        tokens_first(b)
                    if d == 4:
                        features_first(b)
                    if d == 5:
                        project_out(b)
                    if d == 6:
                        transpose_w(b)

            pe.wait_ge(diag_ready, 1)
            for m in range(KD):
                ins = nc.tensor.matmul(bank(5)[:, P * m:P * m + P], ones[:, :], diag[:, m, :], start=True, stop=True)
            ins.then_inc(s2row_ready, 1)

            def spread_max(n):
                bk = bank(4 - 4 * n)
                pe.wait_ge(am_col, n + 1)
                nc.tensor.transpose(bk[0:1, 0:P], amax[:, n:n + 1], ident[:, :]).then_inc(am_row, 1)
                pe.wait_ge(am_one, n + 1)
                nc.tensor.matmul(bk[:, P:P + 1], ones[0:1, :], amax1[0:1, n:n + 1], start=True,
                                 stop=True).then_inc(am_all, 1)

            spread_max(0)
            pe.wait_ge(wT_moved, 4)
            pe.wait_ge(yq_ready, 3)
            for f in range(FT):
                if f >= 2:
                    pe.wait_ge(gelu_done, f - 1)
                for n in range(2):
                    for k in range(KD):
                        ins = nc.tensor.matmul(pairs[f % 2][:, 512 * n:512 * n + 512], w1qT[:, k, P * f:P * f + P],
                                               yq[:, k, 512 * n:512 * n + 512], start=(k == 0), stop=(k == KD - 1))
                ins.then_inc(f1_ready, 1)
            spread_max(1)
            pe.wait_ge(s2row_moved, 1)
            of_pool = of_dve = 0
            for f in range(FT):
                if f in POOL_F:
                    of_pool += 1
                    pe.wait_ge(hq_pool, of_pool)
                else:
                    of_dve += 1
                    pe.wait_ge(hq_dve, of_dve)
                for t in range(T):
                    ins = nc.tensor.matmul(bank(4 + t // TPB)[:, D * (t % TPB):D * (t % TPB) + D],
                                           hq[:, f, P * t:P * t + P], w2qT[:, f, :],
                                           start=(f == 0 and t % TPB == 0), stop=(f == FT - 1), skip_group_check=True)
                    if f == FT - 1 and t % TPB == TPB - 1:
                        ins.then_inc(f2_ready, 1)

            for t in range(T):
                pe.wait_ge(x1_ready, t + 1)
                for k in range(KD):
                    at = B * BLK * k + P // BLK_TOKENS * t
                    ins = nc.tensor.matmul(bank(0)[:, at:at + P // BLK_TOKENS], x1[:, t, P * k:P * k + P],
                                           block_of[:, :], start=True, stop=True)
            ins.then_inc(br_ready, 1)
            pe.wait_ge(br_moved, 1)
            pe.wait_ge(ld_wk, 16)
            for k in range(KD):
                ins = nc.tensor.matmul(bank(1)[0:B * BLK, 0:D], brT[:, k, :], wk[:, k, :], start=(k == 0), stop=(k == KD - 1))
            ins.then_inc(keys_ready, 1)
            pe.wait_ge(score_ready, 1)
            nc.tensor.matmul(bank(2)[0:1, 0:B * BLK], score[:, :], ident[0:B * BLK, 0:B * BLK], start=True,
                             stop=True).then_inc(score_row, 1)
            pe.wait_ge(attn_ready, 1)
            nc.tensor.matmul(bank(2)[:, 64:64 + B * BLK], ones[0:1, :], attn[:, :, :].rearrange("p b n -> p (b n)"),
                             start=True, stop=True).then_inc(attn_all, 1)
            pe.wait_ge(att_ready, 1)
            pe.wait_ge(ld_wo, 16)
            for b in range(B):
                for k in range(KD):
                    ins = nc.tensor.matmul(pairs[2][:, D * b:D * b + D], att[:, k, b:b + 1].broadcast_to([P, P]),
                                           wo[:, k, :], start=(k == 0), stop=(k == KD - 1))
                ins.then_inc(pr_ready, 1)

            def transpose_x2(b):
                pe.wait_ge(xhat_ready, TPB * (b + 1))
                if b >= 1:
                    pe.wait_ge(x2T_moved, KD * b)
                for k in range(KD):
                    for i in range(TPB):
                        ins = nc.tensor.transpose(bank(6)[:, S * k + P * i:S * k + P * i + P],
                                                  xr[:, TPB * b + i, P * k:P * k + P], ident[:, :])
                ins.then_inc(x2T_ready, 1)

            def synapse(t):
                pe.wait_ge(x2_lo, t // TPB + 1)
                if t >= 2:
                    pe.wait_ge(z_relu, t - 1)
                for n in range(2):
                    cols_ = slice(512 * n, 512 * n + 512)
                    nc.tensor.matmul(pairs[t % 2][:, cols_], sel3[:, :], bsyn3[:, cols_], start=True, stop=False)
                    for k in range(KD):
                        for part in (x2h, x2l):
                            ins = nc.tensor.matmul(pairs[t % 2][:, cols_], part[:, k, P * t:P * t + P], tsyn[:, k, cols_],
                                                   start=False, stop=(k == KD - 1 and part is x2l))
                ins.then_inc(z_ready, 1)

            def sum_found(b):
                pe.wait_ge(thresh_found, TPB * (b + 1))
                pe.wait_ge(x2T_moved, KD * B)
                nc.tensor.matmul(bank(6)[0:1, TPB * b:TPB * b + TPB], ones[:, 0:1], found[:, TPB * b:TPB * b + TPB],
                                 start=True, stop=True).then_inc(found_sum, 1)

            def transpose_hidden(t):
                pe.wait_ge(hid_ready, t + 1)
                if t == 0:
                    pe.wait_ge(ln_stats, T)
                else:
                    pe.wait_ge(hT_act, t)
                    pe.wait_ge(hT_dve, t)
                for f in range(FT):
                    ins = nc.tensor.transpose(pairs[2][:, P * f:P * f + P], hidden[:, t % 2, P * f:P * f + P], ident[:, :])
                ins.then_inc(hT_ready, 1)

            def last_product(t):
                pe.wait_ge(hT_act, t + 1)
                pe.wait_ge(hT_dve, t + 1)
                if t >= 1:
                    pe.wait_ge(x4_stats, t)
                for f in range(FT):
                    ins = nc.tensor.matmul(bank(7)[:, 0:D], hT[:, t % 2, P * f:P * f + P], tfin[:, f, :],
                                           start=(f == 0), stop=(f == FT - 1))
                ins.then_inc(out_ready, 1)

            pe.wait_ge(tern_ready, 2)
            pe.wait_ge(bsyn_ready, 1)
            transpose_x2(0)
            transpose_x2(1)
            for i in range(T + 4):
                if i < T:
                    synapse(i)
                if i == 0:
                    transpose_x2(2)
                    transpose_x2(3)
                if 0 <= i - 3 < T and (i - 3) % TPB == TPB - 1:
                    sum_found((i - 3) // TPB)
                if 0 <= i - 4 < T:
                    transpose_hidden(i - 4)
                    last_product(i - 4)


def kernel(**inputs):
    import numpy as _np
    import concourse.bacc as _bacc
    from concourse import mybir as _mybir
    from concourse.bass_utils import run_bass_kernel_spmd as _run

    a = {k: _np.asarray(v) for k, v in inputs.items()}

    def by_column(v):
        return v.reshape(-1, P).T

    cond_t = a["cond_2048"].T.reshape(KD, P, B).transpose(1, 0, 2).reshape(P, KD * B)
    cols = _np.concatenate([cond_t, by_column(a["L0_cond_b_emb"]), by_column(a["L0_cond_g_norm"]),
                            by_column(a["L0_ffn_b1"]), by_column(a["L1_cond_ln_gamma"]),
                            by_column(a["L1_cond_ln_beta"])], axis=1)
    rows = _np.concatenate([a["L0_cond_g_q"], a["L0_cond_g_k"], a["L0_ffn_b2"], a["L1_ffn_b_out"], a["L1_ffn_gamma"],
                            a["L1_ffn_beta"], a["L1_cond_ln_gamma"], a["L1_cond_ln_beta"], a["L1_cond_rms_weight"],
                            a["cond_2048"][1], a["L1_ffn_b_syn"]])[None, :]
    feed = {
        "x": a["x"].reshape(B * S, D), "cols": cols, "rows": rows, "w_emb": a["L0_cond_W_emb"],
        "w_qkv": a["L0_cond_W_qkv"], "w_out": a["L0_cond_W_out"], "w1": a["L0_ffn_w1"], "w2": a["L0_ffn_w2"],
        "wk_t": a["L1_cond_Wk"].T, "wo_t": a["L1_cond_Wo"].T, "wsyn_t": a["L1_ffn_W_syn"].T,
        "wout_t": a["L1_ffn_W_out"].T,
    }
    nc = _bacc.Bacc("TRN2", target_bir_lowering=False, num_devices=1)
    arrays, args = {}, []
    for name, v in feed.items():
        v = _np.ascontiguousarray(v)
        arrays[f"in_{name}"] = v
        args.append(nc.dram_tensor(f"in_{name}", v.shape, _mybir.dt.from_np(v.dtype), kind="ExternalInput").ap())
    args.append(nc.dram_tensor("out_x", (B * S, D), F32, kind="ExternalOutput").ap())
    build(nc, *args)
    res = _run(nc, [arrays], core_ids=[0])
    return res.results[0]["out_x"].reshape(B, S, D)
```

```python
from contextlib import ExitStack

import concourse.bass as bass
from concourse import mybir

F32 = mybir.dt.float32
BF16 = mybir.dt.bfloat16
FP16 = mybir.dt.float16
I32 = mybir.dt.int32
ALU = mybir.AluOpType
ACT = mybir.ActivationFunctionType
AX = mybir.AxisListType

P = 128
B, S, D = 4, 256, 256
T = B * S // P
TPB = S // P
KD = D // P
HEADS = 16
DH = D // HEADS
PAIRS = HEADS // 2
HID = 1024
FT = HID // P
BLK = 8
BLK_TOKENS = S // BLK
TOPK = max(1, int(HID * (1.0 - 0.9)))
ROUND = 1.5 * 2.0 ** 23
QMAX = 127.0
QK_SCALE = 8.0

COLS = {}
ROWS = {}


def _lay(table, names):
    at = 0
    for name, n in names:
        table[name] = (at, at + n)
        at += n
    return at


NCOLS = _lay(COLS, [("cond", KD * B), ("b_emb", 2 * KD), ("g_norm", KD), ("b1", FT), ("ln_gamma", KD),
                    ("ln_beta", KD)])
NROWS = _lay(ROWS, [("g_q", DH), ("g_k", DH), ("b2", D), ("b_out", D), ("gamma", D), ("beta", D),
                    ("ln_gamma", D), ("ln_beta", D), ("rms_w", D), ("query", D), ("b_syn", HID)])

NEWTON = (1.0, 0.8, 0.6, 0.4)
AIM = TOPK - 4.5
START = 1.2816 / 0.3989 / HID
STEP = 1.0 / 0.3989 / HID / (HID * 0.1755)
FLAT_ROUNDS = -(-TOPK // 8)


def build(nc, x, cols, rows, w_emb, w_qkv, w_out, w1, w2, wk_t, wo_t, wsyn_t, wout_t, out):
    ctx = ExitStack()
    with ctx:
        def sb(name, shape, dt=F32):
            return ctx.enter_context(nc.sbuf_tensor(name, shape, dt))

        def sem(name):
            return ctx.enter_context(nc.semaphore(name))

        pairs = [ctx.enter_context(nc.psum_tensor(f"banks{2 * i}{2 * i + 1}", [P, 1024], F32)) for i in range(4)]

        def bank(i):
            return pairs[i // 2][:, (i % 2) * 512:(i % 2) * 512 + 512]

        def projection(b):
            return (bank(4), bank(5), bank(7), bank(7)[:, D:2 * D])[b][:, 0:D]

        ident = sb("ident", [P, P])
        ident_h = sb("ident_h", [P, P], FP16)
        ones = sb("ones", [P, P])
        neg_half = sb("neg_half", [P, TPB])
        eps_x = sb("eps_x", [P, 1])
        eps_qk = sb("eps_qk", [P, 1])
        round_col = sb("round_col", [P, 1])
        block_of = sb("block_of", [P, P // BLK_TOKENS])
        rank8 = sb("rank8", [P, 8])
        ones8 = sb("ones8", [P, 8])
        newton_c = sb("newton_c", [P, len(NEWTON)])
        sel3 = sb("sel3", [96, P], BF16)
        col = sb("col", [P, NCOLS])
        row = sb("row", [P, NROWS])

        def c(name):
            return col[:, COLS[name][0]:COLS[name][1]]

        def r(name):
            return row[:, ROWS[name][0]:ROWS[name][1]]

        wemb = sb("wemb", [P, KD, 2 * D])
        wqkv = sb("wqkv", [P, KD, 3 * D])
        wout = sb("wout", [P, KD, D])
        w1s = sb("w1s", [P, FT, D])
        w2s = sb("w2s", [P, KD, HID])
        w1q = sb("w1q", [P, FT, D], FP16)
        w2q = sb("w2q", [P, KD, HID], FP16)
        w1qT = sb("w1qT", [P, KD, HID], FP16)
        w2qT = sb("w2qT", [P, FT, D], FP16)
        wk = sb("wk", [P, KD, D])
        wo = sb("wo", [P, KD, D])
        wsyn = sb("wsyn", [P, KD, HID])
        wfin = sb("wfin", [P, FT, D])
        tsyn = sb("tsyn", [P, KD, HID], FP16)
        tfin = wfin
        bsyn3 = w2s[0:96, 0, 0:HID // 2].bitcast(BF16)

        xs = sb("xs", [P, T, D])
        xr = sb("xr", [P, T, D])
        xnT = sb("xnT", [P, KD, B * S])
        early = sb("early", [P, 4, 2 * 2 * D])
        qkn = early[:, 0, :].rearrange("p (i a n) -> p i a n", i=2, a=2)
        sq = early[:, 1, :].rearrange("p (i n) -> p i n", i=2)
        qst = early[:, 2, :].bitcast(FP16).rearrange("p (i h s d) -> p i h s d", i=2, h=HEADS, s=4)
        kst = early[:, 3, :].bitcast(FP16).rearrange("p (i h s d) -> p i h s d", i=2, h=HEADS, s=4)
        stacks = sb("stacks", [P, 2, PAIRS, B * S], FP16)
        qT, kT = stacks[:, 0], stacks[:, 1]
        vaug = sb("vaug", [P, T, HEADS, 2 * DH])
        probs = sb("probs", [P, 4, 1024])
        late = sb("late", [P, 4, 2 * D])
        oT = late[:, 0:2]
        otm = late[:, 2].rearrange("p (i d) -> p i d", i=TPB)
        oTn = late[:, 3]
        yT = xnT
        yq = wqkv[:, :, :].rearrange("p k n -> p (k n)")[:, 0:B * S].bitcast(FP16).rearrange("p (k n) -> p k n", k=KD)
        hid = stacks[:, :, :, :].rearrange("p a b n -> p (a b n)").bitcast(F32).rearrange("p (f n) -> p f n", f=FT)
        hq = early[:, :, :].rearrange("p a n -> p (a n)").bitcast(FP16).rearrange("p (f n) -> p f n", f=FT)
        x1 = xs
        xb2 = sb("xb2", [P, T, D])
        x1b = wsyn[:, :, :].rearrange("p k n -> p (k n)").rearrange("p (t d) -> p t d", t=T)
        x2f = wemb[:, :, :].rearrange("p k (b n) -> p b k n", b=2)
        x2h = w1q[:, :, :].rearrange("p f d -> p (f d)").rearrange("p (k n) -> p k n", k=KD)
        x2l = w2q
        zp = vaug[:, :, :, :].rearrange("p t h d -> p (t h d)").rearrange("p (i n) -> p i n", i=4)
        hidden = probs[:, 0:2]
        hT = probs[:, 2:4]
        below = w1s[:, :, :].rearrange("p f d -> p (f d)")[:, 0:HID]
        minus = w1s[:, :, :].rearrange("p f d -> p (f d)")
        junk = [early[:, 0, HID // 2 * j:HID // 2 * (j + 1)].bitcast(BF16) for j in range(2)]
        junk_v = yT[:, 0, 0:HID // 2].bitcast(BF16)
        tmp = w2s[:, 1, :]
        fin, fin_g, x4, xh = [late[:, j].rearrange("p (i d) -> p i d", i=2) for j in range(4)]

        ssx = sb("ssx", [P, T])
        msx = sb("msx", [P, T])
        rx = sb("rx", [P, T])
        mod_a = sb("mod_a", [P, KD, B])
        mod_b = sb("mod_b", [P, KD, B])
        bemb1 = sb("bemb1", [P, KD])
        gg = sb("gg", [P, DH])
        ggt = sb("ggt", [P, D])
        ggmax = sb("ggmax", [P, 1])
        nbound = sb("nbound", [P, 1])
        ssq = sb("ssq", [P, 2, 2 * HEADS])
        msq = sb("msq", [P, 2, 2 * HEADS])
        rqk = sb("rqk", [P, 2, 2 * HEADS])
        rsum = sb("rsum", [P, 2, HEADS])
        ymax = sb("ymax", [P, B])
        amax = sb("amax", [P, 2])
        amax1 = sb("amax1", [1, 2])
        sx = sb("sx", [P, 2])
        sx_inv = sb("sx_inv", [P, 2])
        s1 = sb("s1", [P, FT])
        s1i = sb("s1i", [P, FT])
        s2 = sb("s2", [P, KD])
        s2i = sb("s2i", [P, KD])
        sc1 = sb("sc1", [P, FT])
        diag = early[:, 1, 0:KD * P].rearrange("p (m n) -> p m n", m=KD)
        s2row = ggt
        scale2 = ggt
        gmax = sb("gmax", [P, FT])
        wsum = sb("wsum", [P, 2])
        wtot = sb("wtot", [P, 2])
        wsc = sb("wsc", [P, 2])
        th = sb("th", [P, 2])
        nth = sb("nth", [P, 2])
        ssyn = sb("ssyn", [P, 1])
        ssyn_inv = sb("ssyn_inv", [P, 1])
        sfin = sb("sfin", [P, 1])
        lnbo = r("b_out")
        bs = r("b_syn")
        bsb = wqkv[:, :, :].rearrange("p k n -> p (k n)")[:, B * S:3 * D * KD].bitcast(BF16)
        brT = sb("brT", [P, KD, B * BLK])
        keys, keys_j, keys_k = [yT[0:B * BLK, 1, D * j:D * j + D] for j in range(3)]
        wq = row[0:B * BLK, ROWS["rms_w"][0]:ROWS["rms_w"][1]]
        raw = sb("raw", [B * BLK, 1])
        kss = sb("kss", [B * BLK, 1])
        kms = sb("kms", [B * BLK, 1])
        rk = sb("rk", [B * BLK, 1])
        score = sb("score", [B * BLK, 1])
        smax = sb("smax", [1, B])
        sdif = sb("sdif", [1, B, BLK])
        sexp = sb("sexp", [1, B, BLK])
        ssum = sb("ssum", [1, B])
        srec = sb("srec", [1, B])
        attn = sb("attn", [1, B, BLK])
        prod = sb("prod", [P, KD, B, BLK])
        att = sb("att", [P, KD, B])
        st1 = sb("st1", [P, T, 6])
        mv1 = sb("mv1", [P, T, 2])
        ve1 = sb("ve1", [P, T])
        rs1 = sb("rs1", [P, T])
        zsum = sb("zsum", [P, T])
        na = sb("na", [P, T, len(NEWTON)])
        nb = sb("nb", [P, T, len(NEWTON)])
        nt = sb("nt", [P, T, len(NEWTON) + 1])
        ne = sb("ne", [P, T])
        signs = sb("signs", [P, T, len(NEWTON)])
        tpos = sb("tpos", [P, T])
        cnt = sb("cnt", [P, T])
        m8 = sb("m8", [P, T, 8])
        j8 = sb("j8", [P, 8])
        j8b = sb("j8b", [P, 8])
        thresh = sb("thresh", [P, T])
        found = sb("found", [P, T])
        worst = sb("worst", [1, B])
        flag = sb("flag", [1, B], I32)
        st2 = sb("st2", [P, T, 6])
        mv2 = sb("mv2", [P, T, 2])
        ve2 = sb("ve2", [P, T])
        rs2 = sb("rs2", [P, T])
        ne2 = sb("ne2", [P, T])

        ld_x = [sem(f"ld_x{b}") for b in range(B)]
        (ld_col, ld_gain, ld_row, ld_emb, ld_qkv, ld_out, ld_w1, ld_w2, ld_wk, ld_wo, ld_syn, ld_fin) = [
            sem("ld_" + n) for n in "col gain row emb qkv out w1 w2 wk wo syn fin".split()]
        consts = sem("consts")
        casts = sem("casts")
        pool_step = sem("pool_step")
        dve_step = sem("dve_step")
        x_squared = sem("x_squared")
        x_rms = sem("x_rms")
        x_rstd = sem("x_rstd")
        x_scaled = sem("x_scaled")
        xT_ready = sem("xT_ready")
        xT_moved = sem("xT_moved")
        cond_ready = sem("cond_ready")
        mod_ready = sem("mod_ready")
        qk_ready = sem("qk_ready")
        v_ready = sem("v_ready")
        v_moved = sem("v_moved")
        qk_squared = sem("qk_squared")
        qk_summed = sem("qk_summed")
        qk_rms = sem("qk_rms")
        qk_rstd = sem("qk_rstd")
        qk_normed = sem("qk_normed")
        gg_ready = sem("gg_ready")
        ggt_ready = sem("ggt_ready")
        k_gained = sem("k_gained")
        q_hi = sem("q_hi")
        k_hi = sem("k_hi")
        q_lo = sem("q_lo")
        k_lo = sem("k_lo")
        qT_ready = sem("qT_ready")
        kT_ready = sem("kT_ready")
        qT_moved = sem("qT_moved")
        kT_moved = sem("kT_moved")
        s_ready = sem("s_ready")
        exp_done = sem("exp_done")
        pv_done = sem("pv_done")
        o_moved = sem("o_moved")
        ot_ready = sem("ot_ready")
        o_normed = sem("o_normed")
        oTn_ready = sem("oTn_ready")
        oTn_moved = sem("oTn_moved")
        wout_ready = sem("wout_ready")
        y_ready = sem("y_ready")
        y_moved = sem("y_moved")
        w1_inv = sem("w1_inv")
        w2_inv = sem("w2_inv")
        w1_scaled = sem("w1_scaled")
        w2_scaled = sem("w2_scaled")
        w_quant = sem("w_quant")
        wT_ready = sem("wT_ready")
        wT_moved = sem("wT_moved")
        w_summed = sem("w_summed")
        w_total = sem("w_total")
        syn_inv = sem("syn_inv")
        tern_low = sem("tern_low")
        tern_ready = sem("tern_ready")
        bsyn_ready = sem("bsyn_ready")
        xb2_ready = sem("xb2_ready")
        diag_ready = sem("diag_ready")
        s2row_ready = sem("s2row_ready")
        s2row_moved = sem("s2row_moved")
        am_col = sem("am_col")
        am_row = sem("am_row")
        am_one = sem("am_one")
        am_all = sem("am_all")
        sx_ready = sem("sx_ready")
        y_scaled = sem("y_scaled")
        yq_ready = sem("yq_ready")
        f1_ready = sem("f1_ready")
        gelu_done = sem("gelu_done")
        hq_pool = sem("hq_pool")
        h_scaled = sem("h_scaled")
        hq_dve = sem("hq_dve")
        f2_ready = sem("f2_ready")
        f2_scaled = sem("f2_scaled")
        x1_even = sem("x1_even")
        x1_odd = sem("x1_odd")
        br_ready = sem("br_ready")
        br_moved = sem("br_moved")
        keys_ready = sem("keys_ready")
        keys_moved = sem("keys_moved")
        keys_sq = sem("keys_sq")
        keys_rstd = sem("keys_rstd")
        score_ready = sem("score_ready")
        score_row = sem("score_row")
        score_dif = sem("score_dif")
        score_exp = sem("score_exp")
        attn_ready = sem("attn_ready")
        attn_all = sem("attn_all")
        att_ready = sem("att_ready")
        pr_ready = sem("pr_ready")
        ln_stats = sem("ln_stats")
        ln_rstd = sem("ln_rstd")
        xhat_ready = sem("xhat_ready")
        x2T_ready = sem("x2T_ready")
        x2T_moved = sem("x2T_moved")
        x2_hi = sem("x2_hi")
        x2_lo = sem("x2_lo")
        lnbo_ready = sem("lnbo_ready")
        x2g_ready = sem("x2g_ready")
        x2b_ready = sem("x2b_ready")
        x1b_ready = sem("x1b_ready")
        z_ready = sem("z_ready")
        z_relu = sem("z_relu")
        guess = [sem(f"guess{i}") for i in range(len(NEWTON) + 1)]
        counted = [sem(f"counted{i}") for i in range(len(NEWTON))]
        thresh_found = sem("thresh_found")
        found_sum = sem("found_sum")
        hid_ready = sem("hid_ready")
        hT_ready = sem("hT_ready")
        hT_moved = sem("hT_moved")
        out_ready = sem("out_ready")
        x4_stats = sem("x4_stats")
        x4_rstd = sem("x4_rstd")
        x4_shift = sem("x4_shift")
        x4_hat = sem("x4_hat")
        x4_gained = sem("x4_gained")
        fin_ready = sem("fin_ready")
        stored = [sem("stored0"), sem("stored1")]

        N_CONST = 5
        POOL_F = (2, 6)
        ACT_F = (1, 3, 5, 7)
        steps = {"pool": 0, "dve": 0}

        def chain(eng, which, s, ins):
            steps[which] += 1
            ins.then_inc(s, 1)
            eng.wait_ge(s, steps[which])

        block = ctx.enter_context(nc.Block())

        @block.sync
        def _(sp):
            sp.dma_start(col[:, :], cols).then_inc(ld_col, 16)
            for b in range(B):
                sp.dma_start(xs[:, TPB * b:TPB * b + TPB, :],
                             x[S * b:S * b + S, :].rearrange("(t p) d -> p t d", p=P)).then_inc(ld_x[b], 16)
                if b == 0:
                    sp.dma_start(wemb[:, :, :], w_emb.rearrange("(k p) n -> p k n", p=P)).then_inc(ld_emb, 16)
                    sp.dma_start(row[:, 0:2 * DH], rows[:, 0:2 * DH].broadcast_to([P, 2 * DH])).then_inc(ld_gain, 16)
                    sp.dma_start(wqkv[:, :, :], w_qkv.rearrange("(k p) n -> p k n", p=P)).then_inc(ld_qkv, 16)
            sp.dma_start(row[:, 2 * DH:NROWS], rows[:, 2 * DH:NROWS].broadcast_to([P, NROWS - 2 * DH])).then_inc(ld_row, 16)
            for dst, src, s in ((w1s, w1, ld_w1), (wout, w_out, ld_out), (w2s, w2, ld_w2), (wsyn, wsyn_t, ld_syn),
                                (wfin, wout_t, ld_fin), (wk, wk_t, ld_wk), (wo, wo_t, ld_wo)):
                sp.dma_start(dst[:, :, :], src.rearrange("(k p) n -> p k n", p=P)).then_inc(s, 16)
            for t in range(T):
                sp.wait_ge(fin_ready, t + 1)
                sp.dma_start(out[t * P:t * P + P, :], fin[:, t % 2, :]).then_inc(stored[t % 2], 16)
            for s in stored:
                sp.wait_ge(s, 16 * T // 2)

        @block.gpsimd
        def _(pool):
            def step(ins):
                chain(pool, "pool", pool_step, ins)

            def rstd(out_, mean_sq, sums, scale, eps):
                step(pool.tensor_scalar(mean_sq, sums, scale, eps, ALU.mult, ALU.add))
                return pool.tensor_tensor(out_, mean_sq, neg_half[0:out_.shape[0], 0:out_.shape[1]], ALU.pow)

            step(pool.memset(ident[:, :], 0.0))
            pool.affine_select(out=ident[:, :], in_=ident[:, :], compare_op=ALU.not_equal, fill=1.0, base=0,
                               pattern=[[-1, P]], channel_multiplier=1).then_inc(consts, 1)
            pool.memset(neg_half[:, :], -0.5)
            pool.memset(eps_x[:, :], 1e-6)
            pool.memset(eps_qk[:, :], 1e-6 / QK_SCALE ** 2)
            pool.memset(ones[:, :], 1.0).then_inc(consts, 1)
            step(pool.memset(block_of[:, :], 0.0))
            for j in range(P // BLK_TOKENS):
                step(pool.memset(block_of[BLK_TOKENS * j:BLK_TOKENS * (j + 1), j:j + 1], 1.0))
            pool.memset(round_col[:, :], ROUND)
            pool.memset(ones8[:, :], 1.0)
            for j in range(8):
                pool.memset(rank8[:, j:j + 1], float(TOPK - j - 1))
            for j, f in enumerate(NEWTON):
                pool.memset(newton_c[:, j:j + 1], -0.5 * f * STEP)
            step(pool.memset(sel3[:, :], 0.0))
            for j in range(3):
                step(pool.memset(sel3[32 * j:32 * j + 1, :], 1.0))
            pool.memset(vaug[:, :, :, DH:2 * DH], 1.0).then_inc(consts, 3)

            pool.wait_ge(gg_ready, 1)
            pool.tensor_copy(ggt[:, :].rearrange("p (h d) -> p h d", h=HEADS),
                             gg[:, :].unsqueeze(1).broadcast_to([P, HEADS, DH])).then_inc(ggt_ready, 1)
            pool.wait_ge(ggt_ready, 1)
            for t in range(T):
                i = t % 2
                pool.wait_ge(qk_normed, t + 1)
                pool.tensor_tensor(qkn[:, i, 1, :], qkn[:, i, 1, :], ggt[:, :], ALU.mult).then_inc(k_gained, 1)
                pool.wait_ge(k_gained, t + 1)
                if t >= 2:
                    pool.wait_ge(kT_ready, t - 1)
                pool.tensor_scalar(kst[:, i, :, 0::2, :],
                                   qkn[:, i, 1, :].rearrange("p (h d) -> p h d", h=HEADS).unsqueeze(2)
                                   .broadcast_to([P, HEADS, 2, DH]), 1.0, 1.0, ALU.mult, ALU.mult).then_inc(k_hi, 1)
                pool.wait_ge(k_hi, t + 1)
                pool.tensor_tensor(kst[:, i, :, 1::2, :],
                                   qkn[:, i, 1, :].rearrange("p (h d) -> p h d", h=HEADS).unsqueeze(2)
                                   .broadcast_to([P, HEADS, 2, DH]), kst[:, i, :, 0::2, :],
                                   ALU.subtract).then_inc(k_lo, 1)
            pool.wait_ge(w1_inv, 1)
            pool.tensor_tensor(w1s[:, :, :], w1s[:, :, :], s1i[:, :].unsqueeze(2).broadcast_to([P, FT, D]),
                               ALU.mult).then_inc(w1_scaled, 1)
            pool.wait_ge(w2_inv, 1)
            pool.tensor_tensor(w2s[:, :, :], w2s[:, :, :], s2i[:, :].unsqueeze(2).broadcast_to([P, KD, HID]),
                               ALU.mult).then_inc(w2_scaled, 1)
            pool.wait_ge(w_summed, 2)
            pool.partition_all_reduce(wtot[:, :], wsum[:, :], P, bass.bass_isa.ReduceOp.add).then_inc(w_total, 1)
            pool.wait_ge(ld_x[B - 1], 16)
            pool.wait_ge(ld_row, 16)
            for t in range(T):
                pool.tensor_tensor(xb2[:, t, :], xs[:, t, :], r("b2"), ALU.add).then_inc(xb2_ready, 1)
            pool.wait_ge(syn_inv, 1)
            step(pool.tensor_scalar(bs, r("b_syn"), ssyn_inv[:, 0:1], 1.0, ALU.mult, ALU.mult))
            for j in range(3):
                step(pool.tensor_scalar(bsyn3[32 * j:32 * j + 32, :], bs[32 * j:32 * j + 32, :], 1.0, 1.0, ALU.mult,
                                        ALU.mult))
                if j < 2:
                    step(pool.tensor_scalar(bsb, bs, 1.0, 1.0, ALU.mult, ALU.mult))
                    step(pool.tensor_tensor(bs, bs, bsb, ALU.subtract))
            pool.tensor_tensor(lnbo, r("ln_beta"), r("b_out"), ALU.add).then_inc(bsyn_ready, 1)
            pool.wait_ge(bsyn_ready, 1)
            pool.tensor_tensor(wq, row[0:B * BLK, ROWS["rms_w"][0]:ROWS["rms_w"][1]],
                               row[0:B * BLK, ROWS["query"][0]:ROWS["query"][1]], ALU.mult).then_inc(lnbo_ready, 1)

            pool.wait_ge(sx_ready, 2)
            for f in POOL_F:
                step(pool.tensor_scalar(hid[:, f, :], hid[:, f, :], sx_inv[:, 1:2], ROUND, ALU.mult, ALU.add))
                pool.tensor_scalar(hq[:, f, :], hid[:, f, :], 1.0, -ROUND, ALU.mult, ALU.add).then_inc(hq_pool, 1)
            for t in range(0, T, 2):
                pool.wait_ge(f2_scaled, t + 1)
                pool.tensor_tensor(x1[:, t, :], xr[:, t, :], xb2[:, t, :], ALU.add).then_inc(x1_even, 1)
            pool.wait_ge(keys_sq, 1)
            rstd(rk[:, :], kms[:, :], kss[:, :], 1.0 / D, 1e-6).then_inc(keys_rstd, 1)
            for t in range(T):
                pool.tensor_tensor(x1b[:, t, :], x1[:, t, :], r("beta"), ALU.add).then_inc(x1b_ready, 1)

            def x2_gain(t):
                pool.wait_ge(xhat_ready, t + 1)
                pool.tensor_tensor(xb2[:, t, :], xr[:, t, :], r("ln_gamma"), ALU.mult).then_inc(x2g_ready, 1)

            def x2_bias(t):
                pool.wait_ge(x2g_ready, t + 1)
                pool.tensor_tensor(xb2[:, t, :], xb2[:, t, :], lnbo, ALU.add).then_inc(x2b_ready, 1)

            def x2_split(b):
                pool.wait_ge(x2T_moved, KD * (b + 1))
                pool.tensor_scalar(x2h[:, :, S * b:S * b + S], x2f[:, b % 2, :, :], 1.0, 1.0, ALU.mult,
                                   ALU.mult).then_inc(x2_hi, 1)

            def ln1(b):
                pool.wait_ge(ln_stats, TPB * (b + 1))
                t = slice(TPB * b, TPB * b + TPB)
                rstd(rs1[:, t], ve1[:, t], mv1[:, t, 1], 1.0, 1e-6).then_inc(ln_rstd, 1)

            def guess0(t):
                pool.wait_ge(z_relu, t + 1)
                pool.tensor_scalar(nt[:, t, 0:1], zsum[:, t:t + 1], -START, 0.0, ALU.mult, ALU.add).then_inc(guess[0], 1)
                step(pool.tensor_scalar(na[:, t, :], newton_c[:, :], zsum[:, t:t + 1], 1.0, ALU.mult, ALU.mult))
                pool.tensor_scalar(nb[:, t, :], na[:, t, :], float(HID - 2 * AIM), 0.0, ALU.mult, ALU.add)

            def newton(i, t):
                pool.wait_ge(counted[i], t + 1)
                step(pool.tensor_scalar(ne[:, t:t + 1], signs[:, t, i:i + 1], na[:, t, i:i + 1], nb[:, t, i:i + 1],
                                        ALU.mult, ALU.add))
                ins = pool.tensor_tensor(nt[:, t, i + 1:i + 2], nt[:, t, i:i + 1], ne[:, t:t + 1], ALU.add)
                if i + 1 < len(NEWTON):
                    ins.then_inc(guess[i + 1], 1)
                else:
                    step(ins)
                    pool.tensor_scalar(tpos[:, t:t + 1], nt[:, t, i + 1:i + 2], -1.0, 0.0, ALU.mult,
                                       ALU.add).then_inc(guess[i + 1], 1)

            def final_rstd(t):
                pool.wait_ge(x4_stats, t + 1)
                rstd(rs2[:, t:t + 1], ve2[:, t:t + 1], mv2[:, t, 1:2], 1.0, 1e-5).then_inc(x4_rstd, 1)
                pool.wait_ge(x4_rstd, t + 1)
                pool.tensor_scalar(ne2[:, t:t + 1], mv2[:, t, 0:1], rs2[:, t:t + 1], -1.0, ALU.mult,
                                   ALU.mult).then_inc(x4_shift, 1)

            def final_hat(t):
                pool.wait_ge(x4_shift, t + 1)
                if t >= 2:
                    pool.wait_ge(fin_ready, t - 1)
                pool.tensor_scalar(xh[:, t % 2, :], x4[:, t % 2, :], rs2[:, t:t + 1], ne2[:, t:t + 1], ALU.mult,
                                   ALU.add).then_inc(x4_hat, 1)

            def final_gain(t):
                pool.wait_ge(x4_hat, t + 1)
                pool.tensor_tensor(fin_g[:, t % 2, :], xh[:, t % 2, :], r("gamma"), ALU.mult).then_inc(x4_gained, 1)

            def final(t):
                pool.wait_ge(x4_gained, t + 1)
                if t >= 2:
                    pool.wait_ge(stored[t % 2], 16 * (t // 2))
                pool.tensor_tensor(fin[:, t % 2, :], fin_g[:, t % 2, :], x1b[:, t, :], ALU.add).then_inc(fin_ready, 1)

            pool.wait_ge(lnbo_ready, 1)
            ln1(0)
            ln1(1)
            x2_split(0)
            ln1(2)
            x2_split(1)
            ln1(3)
            guess0(0)
            guess0(1)
            for b in range(B + 2):
                one, two = TPB * b, TPB * b + 1
                done, last = TPB * (b - 2), TPB * (b - 2) - 1
                if 1 <= b < B:
                    guess0(one)
                    guess0(two)
                for i in range(len(NEWTON)):
                    if b < B:
                        newton(i, one)
                    if 1 <= b <= B and i < TPB:
                        x2_gain(TPB * (b - 1) + i)
                    if b == 0 and i < 2:
                        x2_split(2 + i)
                    if b >= 3 and i == 2:
                        final_rstd(last)
                    if b >= 3 and i == 3:
                        final_hat(last)
                    if b < B:
                        newton(i, two)
                    if 1 <= b <= B and i < TPB:
                        x2_bias(TPB * (b - 1) + i)
                    if b >= 3 and i == 3:
                        final_gain(last)
                        final(last)
                if b >= 2:
                    final_rstd(done)
                    final_hat(done)
                    final_gain(done)
                    final(done)
            final_rstd(T - 1)
            final_hat(T - 1)
            final_gain(T - 1)
            final(T - 1)

        @block.scalar
        def _(act):
            def evac_xT(b):
                act.wait_ge(xT_ready, b + 1)
                for k in range(KD):
                    nc.scalar.activation(xnT[:, k, S * b:S * b + S], bank(0)[:, S * k:S * k + S], ACT.Identity,
                                         bias=mod_b[:, k, b:b + 1], scale=mod_a[:, k, b:b + 1]).then_inc(xT_moved, 1)

            def rms_x(b):
                act.wait_ge(ld_x[b], 16)
                for t in range(TPB * b, TPB * b + TPB):
                    nc.scalar.activation(early[:, t // 4, D * (t % 4):D * (t % 4) + D], xs[:, t, :], ACT.Square,
                                         accum_out=ssx[:, t:t + 1]).then_inc(x_squared, 1)
                act.wait_ge(x_squared, TPB * (b + 1))
                t = slice(TPB * b, TPB * b + TPB)
                nc.scalar.activation(msx[:, t], ssx[:, t], ACT.Sqrt, bias=eps_x[:, 0:1],
                                     scale=1.0 / D).then_inc(x_rms, 1)

            def rms_qk(t):
                act.wait_ge(qk_summed, t + 1)
                nc.scalar.activation(msq[:, t % 2, :], ssq[:, t % 2, :], ACT.Sqrt, bias=eps_qk[:, 0:1],
                                     scale=1.0 / (DH * QK_SCALE ** 2)).then_inc(qk_rms, 1)

            act.wait_ge(consts, 2)
            for b in range(B):
                rms_x(b)
            act.wait_ge(mod_ready, 1)
            evac_xT(0)
            def exponentiate(u):
                act.wait_ge(s_ready, u + 1)
                if u >= 4:
                    act.wait_ge(pv_done, (u - 4) // 2 + 1)
                nc.scalar.activation(probs[:, u % 4, :], pairs[u % 2][:, :], ACT.Exp, bias=nbound[:, 0:1],
                                     scale=DH ** -0.5 / QK_SCALE ** 2).then_inc(exp_done, 1)

            for t in range(T + 3):
                i = t % 2
                if t == T + 1:
                    act.wait_ge(gg_ready, 2)
                    exponentiate(0)
                if 3 <= t:
                    act.wait_ge(kT_ready, t - 2)
                    nc.scalar.activation(kT[:, :, P * (t - 3):P * (t - 2)],
                                         bank(6).bitcast(FP16).rearrange("p (a n) -> p a n", a=PAIRS),
                                         ACT.Copy).then_inc(kT_moved, 1)
                if t < T:
                    act.wait_ge(qk_ready, t + 1)
                    if t >= 2:
                        act.wait_ge(qk_summed, t - 1)
                    nc.scalar.activation(sq[:, i, :], bank(1 + i), ACT.Square).then_inc(qk_squared, 1)
                    act.wait_ge(v_ready, t + 1)
                    nc.scalar.activation(vaug[:, t, :, 0:DH],
                                         bank(3 + i)[:, 0:D].rearrange("p (h d) -> p h d", h=HEADS),
                                         ACT.Copy).then_inc(v_moved, 1)
                if 1 <= t <= T:
                    j = (t - 1) % 2
                    act.wait_ge(qk_normed, t)
                    if t >= 3:
                        act.wait_ge(qT_ready, t - 2)
                    nc.scalar.activation(qst[:, j, :, 0:2, :],
                                         qkn[:, j, 0, :].rearrange("p (h d) -> p h d", h=HEADS).unsqueeze(2)
                                         .broadcast_to([P, HEADS, 2, DH]), ACT.Copy).then_inc(q_hi, 1)
                if t < T:
                    rms_qk(t)
                    if i == 0 and t // TPB + 1 < B:
                        evac_xT(t // TPB + 1)

            for u in range(1, B * PAIRS):
                exponentiate(u)

            act.wait_ge(sx_ready, 1)
            nc.scalar.activation(tmp[:, :], yT[:, 1, :], ACT.Identity, bias=round_col[:, 0:1],
                                 scale=sx_inv[:, 0:1]).then_inc(y_scaled, 1)
            act.wait_ge(ld_col, 16)
            for f in range(FT):
                act.wait_ge(f1_ready, f + 1)
                nc.scalar.activation(hid[:, f, :], pairs[f % 2][:, :], ACT.Gelu,
                                     bias=col[:, COLS["b1"][0] + f:COLS["b1"][0] + f + 1],
                                     scale=sc1[:, f:f + 1]).then_inc(gelu_done, 1)
            act.wait_ge(sx_ready, 2)
            act.wait_ge(gelu_done, FT)
            for f in ACT_F:
                nc.scalar.activation(hid[:, f, :], hid[:, f, :], ACT.Identity, bias=round_col[:, 0:1],
                                     scale=sx_inv[:, 1:2]).then_inc(h_scaled, 1)

            act.wait_ge(keys_moved, 1)
            nc.scalar.activation(keys_j, keys, ACT.Square, accum_out=kss[:, :]).then_inc(keys_sq, 1)
            act.wait_ge(score_dif, 1)
            nc.scalar.activation(sexp[:, :, :], sdif[:, :, :], ACT.Exp).then_inc(score_exp, 1)

            def evac_x2T(b):
                act.wait_ge(x2T_ready, b + 1)
                if b >= 2:
                    act.wait_ge(x2_lo, b - 1)
                for k in range(KD):
                    nc.scalar.activation(x2f[:, b % 2, k, :], bank(6)[:, S * k:S * k + S], ACT.Identity,
                                         bias=col[:, COLS["ln_beta"][0] + k:COLS["ln_beta"][0] + k + 1],
                                         scale=col[:, COLS["ln_gamma"][0] + k:COLS["ln_gamma"][0] + k + 1]
                                         ).then_inc(x2T_moved, 1)

            counts = []

            def relu(t):
                act.wait_ge(z_ready, t + 1)
                if t >= 4:
                    act.wait_ge(hid_ready, t - 3)
                nc.scalar.activation(zp[:, t % 4, :], pairs[t % 2][:, :], ACT.Relu,
                                     accum_out=zsum[:, t:t + 1]).then_inc(z_relu, 1)

            def count(i, t):
                act.wait_ge(guess[i], t + 1)
                if len(counts) >= 2:
                    act.wait_ge(*counts[-2])
                counts.append((counted[i], t + 1))
                nc.scalar.activation(junk[len(counts) % 2], zp[:, t % 4, :], ACT.Sign, bias=nt[:, t, i:i + 1],
                                     accum_out=signs[:, t, i:i + 1]).then_inc(counted[i], 1)

            def move_hT(t):
                act.wait_ge(hT_ready, t + 1)
                if t >= 2:
                    act.wait_ge(out_ready, t - 1)
                nc.scalar.activation(hT[:, t % 2, :], pairs[2][:, :], ACT.Copy).then_inc(hT_moved, 1)

            evac_x2T(0)
            evac_x2T(1)
            act.wait_ge(z_ready, 1)
            for b in range(B + 2):
                if b < B:
                    relu(TPB * b)
                if b >= 2:
                    move_hT(TPB * (b - 2))
                if b < B:
                    relu(TPB * b + 1)
                for i in range(len(NEWTON)):
                    if b == 0 and i < 2:
                        evac_x2T(2 + i)
                    if b < B:
                        count(i, TPB * b)
                        count(i, TPB * b + 1)
                    if b >= 2 and i == 0:
                        move_hT(TPB * (b - 2) + 1)

        @block.vector
        def _(dve):
            def step(ins):
                chain(dve, "dve", dve_step, ins)

            dve.wait_ge(consts, 1)
            dve.tensor_copy(ident_h[:, :], ident[:, :]).then_inc(casts, 1)
            for b in range(B):
                dve.wait_ge(x_rms, b + 1)
                dve.reciprocal(rx[:, TPB * b:TPB * b + TPB], msx[:, TPB * b:TPB * b + TPB]).then_inc(x_rstd, 1)
                dve.wait_ge(x_rstd, b + 1)
                for t in range(TPB * b, TPB * b + TPB):
                    dve.tensor_scalar(xr[:, t, :], xs[:, t, :], rx[:, t:t + 1], None, ALU.mult).then_inc(x_scaled, 1)
                if b == 0:
                    dve.wait_ge(ld_col, 16)
                    step(dve.tensor_scalar(bemb1[:, :], col[:, COLS["b_emb"][0]:COLS["b_emb"][0] + KD], 1.0, None, ALU.add))
                    dve.wait_ge(cond_ready, 1)
                    for k in range(KD):
                        dve.tensor_scalar(mod_a[:, k, :], bank(7)[:, B * k:B * k + B], bemb1[:, k:k + 1],
                                          col[:, COLS["g_norm"][0] + k:COLS["g_norm"][0] + k + 1], ALU.add, ALU.mult)
                        bk = COLS["b_emb"][0] + KD + k
                        ins = dve.tensor_scalar(mod_b[:, k, :], bank(7)[:, B * (KD + k):B * (KD + k) + B],
                                                col[:, bk:bk + 1], None, ALU.add)
                    ins.then_inc(mod_ready, 1)
                    dve.wait_ge(ld_gain, 16)
                    dve.tensor_tensor(gg[:, :], r("g_q"), r("g_k"), ALU.mult).then_inc(gg_ready, 1)
                    dve.wait_ge(gg_ready, 1)
                    step(dve.tensor_reduce(ggmax[:, :], gg[:, :], AX.X, ALU.max, apply_absolute_value=True))
                    dve.tensor_scalar(nbound[:, :], ggmax[:, :], -(float(DH) ** 0.5), None, ALU.mult).then_inc(gg_ready, 1)

            def move_qT(t):
                dve.wait_ge(qT_ready, t + 1)
                dve.tensor_copy(qT[:, :, P * t:P * t + P],
                                bank(5).bitcast(FP16).rearrange("p (a n) -> p a n", a=PAIRS)).then_inc(qT_moved, 1)

            def split_low(t):
                i = t % 2
                dve.wait_ge(q_hi, t + 1)
                dve.tensor_tensor(qst[:, i, :, 2:4, :],
                                  qkn[:, i, 0, :].rearrange("p (h d) -> p h d", h=HEADS).unsqueeze(2)
                                  .broadcast_to([P, HEADS, 2, DH]), qst[:, i, :, 0:2, :], ALU.subtract).then_inc(q_lo, 1)

            for t in range(T + 3):
                i = t % 2
                if 3 <= t:
                    move_qT(t - 3)
                if t < T:
                    dve.wait_ge(qk_squared, t + 1)
                    if t >= 2:
                        dve.wait_ge(qk_rms, t - 1)
                    dve.tensor_reduce(ssq[:, i, :], sq[:, i, :].rearrange("p (h d) -> p h d", d=DH), AX.X,
                                      ALU.add).then_inc(qk_summed, 1)
                if 1 <= t <= T:
                    split_low(t - 1)
                if t < T:
                    dve.wait_ge(qk_rms, t + 1)
                    dve.reciprocal(rqk[:, i, :], msq[:, i, :]).then_inc(qk_rstd, 1)
                    dve.wait_ge(qk_rstd, t + 1)
                    if t >= 2:
                        dve.wait_ge(q_lo, t - 1)
                        dve.wait_ge(k_lo, t - 1)
                    dve.tensor_tensor(qkn[:, i, :, :].rearrange("p a (h d) -> p (a h) d", d=DH),
                                      bank(1 + i).rearrange("p (h d) -> p h d", d=DH),
                                      rqk[:, i, :].unsqueeze(2).broadcast_to([P, 2 * HEADS, DH]),
                                      ALU.mult).then_inc(qk_normed, 1)

            def scales(w, ld, s, s_inv, ready):
                dve.wait_ge(ld, 16)
                step(dve.tensor_reduce(s[:, :], w[:, :, :], AX.X, ALU.max, apply_absolute_value=True))
                step(dve.tensor_scalar(s[:, :], s[:, :], 1.0 / QMAX, 1e-8, ALU.mult, ALU.max))
                dve.reciprocal(s_inv[:, :], s[:, :]).then_inc(ready, 1)

            def quantise(w, q, scaled):
                dve.wait_ge(scaled, 1)
                dve.tensor_scalar(q[:, :, :], w[:, :, :], ROUND, -ROUND, ALU.add, ALU.add).then_inc(w_quant, 1)

            def weight_sum(i, w, ld):
                dve.wait_ge(ld, 16)
                dve.tensor_reduce(wsum[:, i:i + 1], w[:, :, :], AX.XY, ALU.add,
                                  apply_absolute_value=True).then_inc(w_summed, 1)

            def ternary_scales():
                dve.wait_ge(w_total, 1)
                step(dve.tensor_scalar(wsc[:, :], wtot[:, :], 1.0 / (HID * D), None, ALU.mult))
                step(dve.tensor_scalar(th[:, :], wsc[:, :], 1e-8, 0.5, ALU.add, ALU.mult))
                step(dve.tensor_scalar(nth[:, :], th[:, :], -1.0, None, ALU.mult))
                step(dve.tensor_scalar(ssyn[:, :], wsc[:, 0:1], 1e-30, None, ALU.max))
                dve.reciprocal(ssyn_inv[:, :], ssyn[:, :]).then_inc(syn_inv, 1)
                dve.tensor_tensor(sfin[:, :], ssyn[:, :], wsc[:, 1:2], ALU.mult)

            def ternary_low(w, i):
                if i == 1:
                    dve.wait_ge(tern_ready, 1)
                dve.tensor_scalar(minus, w[:, :, :].rearrange("p a n -> p (a n)"), nth[:, i:i + 1], None,
                                  ALU.is_lt).then_inc(tern_low, 1)

            def ternary(w, q, i):
                flat_w = w[:, :, :].rearrange("p a n -> p (a n)")
                flat_q = q[:, :, :].rearrange("p a n -> p (a n)")
                dve.wait_ge(tern_low, i + 1)
                dve.scalar_tensor_tensor(out=flat_q, in0=flat_w, scalar=th[:, i:i + 1], in1=minus, op0=ALU.is_gt,
                                         op1=ALU.subtract).then_inc(tern_ready, 1)

            def out_weights():
                dve.wait_ge(ld_out, 16)
                for k in range(KD):
                    ins = dve.tensor_tensor(wout[:, k, P * k:P * k + P], wout[:, k, P * k:P * k + P], ident[:, :], ALU.add)
                ins.then_inc(wout_ready, 1)

            def move_o(q):
                dve.wait_ge(pv_done, 2 * q + 2)
                if q >= 2:
                    dve.wait_ge(ot_ready, TPB * (q // 2))
                dve.tensor_copy(oT[:, q % 2, :], bank(4 + q % 2)).then_inc(o_moved, 1)

            def norm_o(t):
                i = t % TPB
                dve.wait_ge(ot_ready, t + 1)
                if t >= TPB:
                    dve.wait_ge(oTn_ready, t // TPB)
                view = bank(6 + i).rearrange("p (h d) -> p h d", h=HEADS)
                step(dve.reciprocal(rsum[:, i, :], view[:, :, DH]))
                dve.tensor_tensor(otm[:, i, :].rearrange("p (h d) -> p h d", h=HEADS), view[:, :, 0:DH],
                                  rsum[:, i, :].unsqueeze(2).broadcast_to([P, HEADS, DH]), ALU.mult).then_inc(o_normed, 1)

            def move_oTn(b):
                dve.wait_ge(oTn_ready, b + 1)
                if b >= 1:
                    dve.wait_ge(y_ready, b)
                dve.tensor_copy(oTn[:, :], bank(6)).then_inc(oTn_moved, 1)

            def move_y(b):
                dve.wait_ge(y_ready, b + 1)
                dve.tensor_reduce(ymax[:, b:b + 1], bank(7), AX.X, ALU.max, apply_absolute_value=True)
                dve.tensor_copy(yT[:, :, S * b:S * b + S],
                                bank(7).rearrange("p (m n) -> p m n", m=KD)).then_inc(y_moved, 1)

            def move_wT(i):
                dve.wait_ge(wT_ready, i + 1)
                src = bank(6).bitcast(FP16)
                if i < KD:
                    dve.tensor_copy(w1qT[:, i, :], src).then_inc(wT_moved, 1)
                else:
                    m = i - KD
                    dve.tensor_copy(w2qT[:, :, P * m:P * m + P], src.rearrange("p (f n) -> p f n", f=FT)).then_inc(wT_moved, 1)

            def scale_diagonals():
                for m in range(KD):
                    ins = dve.tensor_scalar(diag[:, m, :], ident[:, :], s2[:, m:m + 1], None, ALU.mult)
                ins.then_inc(diag_ready, 1)

            scales(w1s, ld_w1, s1, s1i, w1_inv)
            out_weights()
            scales(w2s, ld_w2, s2, s2i, w2_inv)
            move_o(0)
            scale_diagonals()
            weight_sum(0, wsyn, ld_syn)
            move_o(1)
            for b in range(B):
                norm_o(TPB * b)
                norm_o(TPB * b + 1)
                if b == 0:
                    quantise(w1s, w1q, w1_scaled)
                if b == 1:
                    weight_sum(1, wfin, ld_fin)
                if b == 2:
                    ternary_low(wsyn, 0)
                if b == 3:
                    ternary_low(wfin, 1)
                move_oTn(b)
                if b + 1 < B:
                    move_o(2 * b + 2)
                if b == 3:
                    ternary(wfin, tfin, 1)
                move_y(b)
                move_wT(b)
                if b == 0:
                    quantise(w2s, w2q, w2_scaled)
                if b == 1:
                    ternary_scales()
                if b == 2:
                    ternary(wsyn, tsyn, 0)
                if b + 1 < B:
                    move_o(2 * b + 3)

            def scale_from(src, n):
                dve.tensor_reduce(amax[:, n:n + 1], src, AX.X, ALU.max).then_inc(am_col, 1)
                dve.wait_ge(am_row, n + 1)
                dve.tensor_reduce(amax1[0:1, n:n + 1], bank(4 - 4 * n)[0:1, 0:P], AX.X, ALU.max).then_inc(am_one, 1)
                dve.wait_ge(am_all, n + 1)
                step(dve.tensor_scalar(sx[:, n:n + 1], bank(4 - 4 * n)[:, P:P + 1], 1.0 / QMAX, 1e-8, ALU.mult, ALU.max))
                return dve.reciprocal(sx_inv[:, n:n + 1], sx[:, n:n + 1])

            dve.wait_ge(y_moved, B)
            scale_from(ymax[:, :], 0).then_inc(sx_ready, 1)
            dve.wait_ge(sx_ready, 1)
            step(dve.tensor_scalar(yT[:, 0, :], yT[:, 0, :], sx_inv[:, 0:1], ROUND, ALU.mult, ALU.add))
            dve.tensor_scalar(yq[:, 0, :], yT[:, 0, :], -ROUND, None, ALU.add).then_inc(yq_ready, 1)
            dve.wait_ge(y_scaled, 1)
            dve.tensor_scalar(yq[:, 1, :], tmp[:, :], -ROUND, None, ALU.add).then_inc(yq_ready, 1)
            dve.tensor_scalar(sc1[:, :], s1[:, :], sx[:, 0:1], None, ALU.mult).then_inc(yq_ready, 1)
            dve.wait_ge(s2row_ready, 1)
            dve.tensor_copy(s2row[:, :], bank(5)[:, 0:D]).then_inc(s2row_moved, 1)
            for f in range(FT):
                dve.wait_ge(gelu_done, f + 1)
                ins = dve.tensor_reduce(gmax[:, f:f + 1], hid[:, f, :], AX.X, ALU.max, apply_absolute_value=True)
            step(ins)
            scale_from(gmax[:, :], 1).then_inc(sx_ready, 1)
            dve.wait_ge(sx_ready, 2)
            dve.wait_ge(s2row_moved, 1)
            scaled = 0
            for f in range(FT):
                if f in POOL_F:
                    continue
                if f in ACT_F:
                    scaled += 1
                    dve.wait_ge(h_scaled, scaled)
                else:
                    step(dve.tensor_scalar(hid[:, f, :], hid[:, f, :], sx_inv[:, 1:2], ROUND, ALU.mult, ALU.add))
                dve.tensor_scalar(hq[:, f, :], hid[:, f, :], -ROUND, None, ALU.add).then_inc(hq_dve, 1)
            step(dve.tensor_scalar(scale2[:, :], s2row[:, :], sx[:, 1:2], None, ALU.mult))
            for t in range(T):
                dve.wait_ge(f2_ready, t // TPB + 1)
                dve.tensor_tensor(xr[:, t, :], bank(4 + t // TPB)[:, D * (t % TPB):D * (t % TPB) + D], scale2[:, :],
                                  ALU.mult).then_inc(f2_scaled, 1)
                if t % 2:
                    dve.wait_ge(f2_scaled, t + 1)
                    dve.tensor_tensor(x1[:, t, :], xr[:, t, :], xb2[:, t, :], ALU.add).then_inc(x1_odd, 1)

            dve.wait_ge(br_ready, 1)
            dve.tensor_copy(brT[:, :, :].rearrange("p k n -> p (k n)"), bank(0)[:, 0:KD * B * BLK]).then_inc(br_moved, 1)
            dve.wait_ge(keys_ready, 1)
            dve.tensor_copy(keys, bank(1)[0:B * BLK, 0:D]).then_inc(keys_moved, 1)
            dve.wait_ge(keys_moved, 1)
            dve.wait_ge(lnbo_ready, 1)
            dve.scalar_tensor_tensor(out=keys_k, in0=keys, scalar=1.0, in1=wq, op0=ALU.mult,
                                     op1=ALU.mult, accum_out=raw[:, :]).then_inc(dve_step, 1)
            steps["dve"] += 1
            dve.wait_ge(dve_step, steps["dve"])
            dve.wait_ge(keys_rstd, 1)
            dve.tensor_tensor(score[:, :], raw[:, :], rk[:, :], ALU.mult).then_inc(score_ready, 1)
            dve.wait_ge(score_row, 1)
            srow = bank(2)[0:1, 0:B * BLK].rearrange("p (b n) -> p b n", b=B)
            step(dve.tensor_reduce(smax[:, :], srow, AX.X, ALU.max))
            dve.tensor_tensor(sdif[:, :, :], srow, smax[:, :].unsqueeze(2).broadcast_to([1, B, BLK]),
                              ALU.subtract).then_inc(score_dif, 1)
            dve.wait_ge(score_exp, 1)
            step(dve.tensor_reduce(ssum[:, :], sexp[:, :, :], AX.X, ALU.add))
            step(dve.reciprocal(srec[:, :], ssum[:, :]))
            dve.tensor_tensor(attn[:, :, :], sexp[:, :, :], srec[:, :].unsqueeze(2).broadcast_to([1, B, BLK]),
                              ALU.mult).then_inc(attn_ready, 1)
            dve.wait_ge(attn_all, 1)
            for k in range(KD):
                ins = dve.tensor_tensor(prod[:, k, :, :].rearrange("p b n -> p (b n)"), brT[:, k, :],
                                        bank(2)[:, 64:64 + B * BLK], ALU.mult)
            step(ins)
            dve.tensor_reduce(att[:, :, :].rearrange("p k b -> p (k b)"),
                              prod[:, :, :, :].rearrange("p k b n -> p (k b) n"), AX.X, ALU.add).then_inc(att_ready, 1)

            def ln1_stats(b):
                dve.wait_ge(pr_ready, b + 1 if b < 2 else B)
                for t in range(TPB * b, TPB * b + TPB):
                    step(dve.tensor_tensor(xr[:, t, :], x1[:, t, :], projection(b), ALU.add))
                    step(dve.bn_stats(st1[:, t, :], xr[:, t, :]))
                    dve.bn_aggr(mv1[:, t, :], st1[:, t, :]).then_inc(ln_stats, 1)

            def ln1_hat(b):
                dve.wait_ge(ln_rstd, b + 1)
                for t in range(TPB * b, TPB * b + TPB):
                    dve.tensor_scalar(xr[:, t, :], xr[:, t, :], mv1[:, t, 0:1], rs1[:, t:t + 1], ALU.subtract,
                                      ALU.mult).then_inc(xhat_ready, 1)

            def x2_low(b):
                dve.wait_ge(x2_hi, b + 1)
                dve.tensor_tensor(x2l[:, :, S * b:S * b + S], x2f[:, b % 2, :, :], x2h[:, :, S * b:S * b + S],
                                  ALU.subtract).then_inc(x2_lo, 1)

            ln1_stats(0)
            ln1_hat(0)
            ln1_stats(1)
            ln1_hat(1)
            x2_low(0)
            ln1_stats(2)
            x2_low(1)
            ln1_hat(2)
            ln1_stats(3)
            ln1_hat(3)
            x2_low(2)
            x2_low(3)

            def threshold(t):
                z = zp[:, t % 4, :]
                dve.wait_ge(guess[len(NEWTON)], t + 1)
                dve.tensor_scalar(junk_v, z, tpos[:, t:t + 1], None, ALU.is_ge, ALU.add,
                                  accum_out=cnt[:, t:t + 1]).then_inc(dve_step, 1)
                step(dve.scalar_tensor_tensor(out=below, in0=z, scalar=tpos[:, t:t + 1], in1=z, op0=ALU.is_lt,
                                              op1=ALU.mult))
                steps["dve"] += 1
                dve.wait_ge(dve_step, steps["dve"])
                step(dve.max(m8[:, t, :], below))
                dve.scalar_tensor_tensor(out=j8[:, :], in0=rank8[:, :], scalar=cnt[:, t:t + 1], in1=m8[:, t, :],
                                         op0=ALU.is_equal, op1=ALU.mult, accum_out=thresh[:, t:t + 1])
                dve.scalar_tensor_tensor(out=j8b[:, :], in0=rank8[:, :], scalar=cnt[:, t:t + 1], in1=ones8[:, :],
                                         op0=ALU.is_equal, op1=ALU.mult,
                                         accum_out=found[:, t:t + 1]).then_inc(thresh_found, 1)

            def any_row(b):
                dve.wait_ge(found_sum, b + 1)
                step(dve.tensor_reduce(worst[0:1, b:b + 1], bank(6)[0:1, TPB * b:TPB * b + TPB], AX.X, ALU.min))
                step(dve.tensor_scalar(flag[0:1, b:b + 1], worst[0:1, b:b + 1], P - 0.5, None, ALU.is_lt))
                missing = dve.value_load(flag[0:1, b:b + 1], min_val=0, max_val=1)
                with dve.If(missing):
                    for t in range(TPB * b, TPB * b + TPB):
                        dve.tensor_copy(below, zp[:, t % 4, :])
                        dve.drain()
                        with dve.Fori(0, FLAT_ROUNDS - 1):
                            dve.max(m8[:, t, :], below)
                            dve.drain()
                            dve.match_replace(below, m8[:, t, :], below, 0.0)
                            dve.drain()
                        dve.max(m8[:, t, :], below)
                        dve.drain()
                        last = TOPK - 8 * (FLAT_ROUNDS - 1) - 1
                        dve.tensor_copy(thresh[:, t:t + 1], m8[:, t, last:last + 1])
                        dve.drain()

            def keep(t):
                z = zp[:, t % 4, :]
                if t >= 2:
                    dve.wait_ge(hT_ready, t - 1)
                dve.scalar_tensor_tensor(out=hidden[:, t % 2, :], in0=z, scalar=thresh[:, t:t + 1], in1=z,
                                         op0=ALU.is_ge, op1=ALU.mult).then_inc(hid_ready, 1)

            def last_stats(t):
                dve.wait_ge(out_ready, t + 1)
                dve.wait_ge(x2b_ready, t + 1)
                if t >= 2:
                    dve.wait_ge(fin_ready, t - 1)
                step(dve.scalar_tensor_tensor(out=x4[:, t % 2, :], in0=bank(6 + t % 2)[:, 0:D], scalar=sfin[:, 0:1],
                                              in1=xb2[:, t, :], op0=ALU.mult, op1=ALU.add))
                step(dve.bn_stats(st2[:, t, :], x4[:, t % 2, :]))
                dve.bn_aggr(mv2[:, t, :], st2[:, t, :]).then_inc(x4_stats, 1)

            for b in range(1, B + 2):
                one, two = TPB * (b - 1), TPB * (b - 1) + 1
                done, last = TPB * (b - 2), TPB * (b - 2) + 1
                if b <= B:
                    threshold(one)
                    threshold(two)
                if b >= 2:
                    last_stats(done)
                if b <= B:
                    any_row(b - 1)
                    keep(one)
                    keep(two)
                if b >= 2:
                    last_stats(last)

        @block.tensor
        def _(pe):
            def keep_warm(n, bk):
                for _ in range(n):
                    nc.tensor.matmul(bank(bk), ident_h[:, :], ident_h[:, :].unsqueeze(1).broadcast_to([P, 4, P]),
                                     start=True, stop=True)

            pe.wait_ge(casts, 1)
            keep_warm(16, 6)
            pe.wait_ge(ld_emb, 16)
            pe.wait_ge(ld_col, 16)
            for m in range(2 * KD):
                for k in range(KD):
                    ins = nc.tensor.matmul(bank(7)[:, B * m:B * m + B], wemb[:, k, P * m:P * m + P],
                                           col[:, B * k:B * k + B], start=(k == 0), stop=(k == KD - 1))
            ins.then_inc(cond_ready, 1)

            def transpose_x(b):
                pe.wait_ge(x_scaled, TPB * (b + 1))
                if b >= 1:
                    pe.wait_ge(xT_moved, KD * b)
                for k in range(KD):
                    for i in range(TPB):
                        ins = nc.tensor.transpose(bank(0)[:, S * k + P * i:S * k + P * i + P],
                                                  xr[:, TPB * b + i, P * k:P * k + P], ident[:, :])
                ins.then_inc(xT_ready, 1)

            def project(t):
                i = t % 2
                pe.wait_ge(xT_moved, KD * (t // TPB + 1))
                if t >= 2:
                    pe.wait_ge(qk_normed, t - 1)
                    pe.wait_ge(v_moved, t - 1)
                for k in range(KD):
                    ins = nc.tensor.matmul(bank(1 + i), xnT[:, k, P * t:P * t + P], wqkv[:, k, 0:2 * D],
                                           start=(k == 0), stop=(k == KD - 1))
                ins.then_inc(qk_ready, 1)
                for k in range(KD):
                    ins = nc.tensor.matmul(bank(3 + i)[:, 0:D], xnT[:, k, P * t:P * t + P], wqkv[:, k, 2 * D:3 * D],
                                           start=(k == 0), stop=(k == KD - 1))
                ins.then_inc(v_ready, 1)

            def transpose_qk(t):
                i = t % 2
                for st, low, moved, ready, bk in ((qst, q_lo, qT_moved, qT_ready, 5), (kst, k_lo, kT_moved, kT_ready, 6)):
                    pe.wait_ge(low, t + 1)
                    if t >= 1:
                        pe.wait_ge(moved, t)
                    dst = bank(bk).bitcast(FP16)
                    for a in range(PAIRS):
                        ins = nc.tensor.transpose(dst[:, P * a:P * a + P],
                                                  st[:, i, 2 * a:2 * a + 2, :, :].rearrange("p h s d -> p (h s d)"),
                                                  ident_h[:, :])
                    ins.then_inc(ready, 1)

            def scores(u):
                b, a = u // PAIRS, u % PAIRS
                pe.wait_ge(qT_moved, TPB * (b + 1))
                pe.wait_ge(kT_moved, TPB * (b + 1))
                if u >= 2:
                    pe.wait_ge(exp_done, u - 1)
                for h in range(2):
                    rows_ = slice(64 * h, 64 * h + 64)
                    for k in range(TPB):
                        at = 512 * h + S * k
                        ins = nc.tensor.matmul(pairs[u % 2][:, at:at + S],
                                               kT[rows_, a, S * b + P * k:S * b + P * k + P],
                                               qT[rows_, a, S * b:S * b + S], start=True, stop=True)
                ins.then_inc(s_ready, 1)

            def weigh(g):
                b, q = g // 4, g // 2
                pe.wait_ge(exp_done, 2 * g + 2)
                if g % 2 == 0 and q >= 2:
                    pe.wait_ge(o_moved, q - 1)
                if g == 2:
                    pe.wait_ge(qT_moved, T)
                for k in range(TPB):
                    for j in range(4):
                        at = 512 * (j % 2) + S * k
                        ins = nc.tensor.matmul(bank(4 + q % 2)[32 * j:32 * j + 32, S * (g % 2):S * (g % 2) + S],
                                               vaug[:, TPB * b + k, 4 * (g % 4) + j, :],
                                               probs[:, (2 * g + j // 2) % 4, at:at + S],
                                               start=(k == 0), stop=(k == TPB - 1), tile_position=(0, 32 * j))
                ins.then_inc(pv_done, 1)

            def tokens_first(b):
                pe.wait_ge(o_moved, 2 * b + 2)
                if b == 0:
                    pe.wait_ge(kT_moved, T)
                else:
                    pe.wait_ge(wT_moved, b)
                    pe.wait_ge(y_moved, b)
                for i in range(TPB):
                    for g in range(4):
                        ins = nc.tensor.transpose(bank(6 + i)[:, P * g:P * g + P],
                                                  oT[:, g // 2, S * (g % 2) + P * i:S * (g % 2) + P * i + P], ident[:, :])
                    ins.then_inc(ot_ready, 1)

            def features_first(b):
                pe.wait_ge(o_normed, TPB * (b + 1))
                for k in range(KD):
                    for i in range(TPB):
                        ins = nc.tensor.transpose(bank(6)[:, S * k + P * i:S * k + P * i + P],
                                                  otm[:, i, P * k:P * k + P], ident[:, :])
                ins.then_inc(oTn_ready, 1)

            def project_out(b):
                pe.wait_ge(oTn_moved, b + 1)
                pe.wait_ge(wout_ready, 1)
                for m in range(KD):
                    for k in range(KD):
                        ins = nc.tensor.matmul(bank(7)[:, S * m:S * m + S], wout[:, k, P * m:P * m + P],
                                               oTn[:, S * k:S * k + S], start=(k == 0), stop=(k == KD - 1))
                ins.then_inc(y_ready, 1)

            def transpose_w(i):
                pe.wait_ge(w_quant, i // KD + 1)
                pe.wait_ge(oTn_moved, i + 1)
                dst = bank(6).bitcast(FP16)
                for f in range(FT):
                    src = w1q[:, f, P * i:P * i + P] if i < KD else w2q[:, i - KD, P * f:P * f + P]
                    ins = nc.tensor.transpose(dst[:, P * f:P * f + P], src, ident_h[:, :])
                ins.then_inc(wT_ready, 1)

            pe.wait_ge(consts, 1)
            transpose_x(0)
            pe.wait_ge(ld_qkv, 16)
            for t in range(T):
                if t % TPB == 0 and t // TPB + 1 < B:
                    transpose_x(t // TPB + 1)
                project(t)
                if t >= 2:
                    transpose_qk(t - 2)
            keep_warm(4, 7)
            pe.wait_ge(qk_normed, T)
            pe.wait_ge(v_moved, T)
            scores(0)
            scores(1)
            transpose_qk(T - 2)
            keep_warm(4, 7)
            transpose_qk(T - 1)
            pe.wait_ge(consts, 5)
            keep_warm(4, 7)
            for u in range(2, B * PAIRS + 7):
                if u < B * PAIRS:
                    scores(u)
                if u >= 3 and u % 2 == 1 and u // 2 - 1 < 4 * B:
                    weigh(u // 2 - 1)
                b, d = u // PAIRS - 1, u % PAIRS
                if b >= 0:
                    if d == 2:
                        tokens_first(b)
                    if d == 4:
                        if b == B - 1:
                            keep_warm(6, 0)
                        features_first(b)
                    if d == 6:
                        if b == B - 1:
                            keep_warm(6, 0)
                        project_out(b)
                        transpose_w(b)

            pe.wait_ge(diag_ready, 1)
            for m in range(KD):
                ins = nc.tensor.matmul(bank(5)[:, P * m:P * m + P], ones[:, :], diag[:, m, :], start=True, stop=True)
            ins.then_inc(s2row_ready, 1)

            def spread_max(n):
                bk = bank(4 - 4 * n)
                pe.wait_ge(am_col, n + 1)
                nc.tensor.transpose(bk[0:1, 0:P], amax[:, n:n + 1], ident[:, :]).then_inc(am_row, 1)
                pe.wait_ge(am_one, n + 1)
                nc.tensor.matmul(bk[:, P:P + 1], ones[0:1, :], amax1[0:1, n:n + 1], start=True,
                                 stop=True).then_inc(am_all, 1)

            keep_warm(12, 0)
            spread_max(0)
            keep_warm(12, 0)
            pe.wait_ge(wT_moved, 4)
            pe.wait_ge(yq_ready, 3)
            for f in range(FT):
                if f >= 2:
                    pe.wait_ge(gelu_done, f - 1)
                for n in range(2):
                    for k in range(KD):
                        ins = nc.tensor.matmul(pairs[f % 2][:, 512 * n:512 * n + 512], w1qT[:, k, P * f:P * f + P],
                                               yq[:, k, 512 * n:512 * n + 512], start=(k == 0), stop=(k == KD - 1))
                ins.then_inc(f1_ready, 1)
            pe.wait_ge(gelu_done, FT)
            keep_warm(6, 1)
            spread_max(1)
            keep_warm(6, 1)
            pe.wait_ge(s2row_moved, 1)
            of_pool = of_dve = 0
            for f in range(FT):
                if f in POOL_F:
                    of_pool += 1
                    pe.wait_ge(hq_pool, of_pool)
                else:
                    of_dve += 1
                    pe.wait_ge(hq_dve, of_dve)
                for t in range(T):
                    ins = nc.tensor.matmul(bank(4 + t // TPB)[:, D * (t % TPB):D * (t % TPB) + D],
                                           hq[:, f, P * t:P * t + P], w2qT[:, f, :],
                                           start=(f == 0 and t % TPB == 0), stop=(f == FT - 1), skip_group_check=True)
                    if f == FT - 1 and t % TPB == TPB - 1:
                        ins.then_inc(f2_ready, 1)

            for t in range(T):
                pe.wait_ge(x1_odd if t % 2 else x1_even, t // 2 + 1)
                for k in range(KD):
                    at = B * BLK * k + P // BLK_TOKENS * t
                    ins = nc.tensor.matmul(bank(0)[:, at:at + P // BLK_TOKENS], x1[:, t, P * k:P * k + P],
                                           block_of[:, :], start=True, stop=True)
            ins.then_inc(br_ready, 1)
            pe.wait_ge(br_moved, 1)
            pe.wait_ge(ld_wk, 16)
            for k in range(KD):
                ins = nc.tensor.matmul(bank(1)[0:B * BLK, 0:D], brT[:, k, :], wk[:, k, :], start=(k == 0), stop=(k == KD - 1))
            ins.then_inc(keys_ready, 1)
            pe.wait_ge(score_ready, 1)
            nc.tensor.matmul(bank(2)[0:1, 0:B * BLK], score[:, :], ident[0:B * BLK, 0:B * BLK], start=True,
                             stop=True).then_inc(score_row, 1)
            pe.wait_ge(attn_ready, 1)
            nc.tensor.matmul(bank(2)[:, 64:64 + B * BLK], ones[0:1, :], attn[:, :, :].rearrange("p b n -> p (b n)"),
                             start=True, stop=True).then_inc(attn_all, 1)
            pe.wait_ge(att_ready, 1)
            pe.wait_ge(ld_wo, 16)
            for b in range(B):
                for k in range(KD):
                    ins = nc.tensor.matmul(projection(b), att[:, k, b:b + 1].broadcast_to([P, P]),
                                           wo[:, k, :], start=(k == 0), stop=(k == KD - 1))
                ins.then_inc(pr_ready, 1)

            keep_warm(6, 0)

            def transpose_x2(b):
                pe.wait_ge(xhat_ready, TPB * (b + 1))
                if b >= 1:
                    pe.wait_ge(x2T_moved, KD * b)
                for k in range(KD):
                    for i in range(TPB):
                        ins = nc.tensor.transpose(bank(6)[:, S * k + P * i:S * k + P * i + P],
                                                  xr[:, TPB * b + i, P * k:P * k + P], ident[:, :])
                ins.then_inc(x2T_ready, 1)

            def synapse(t):
                pe.wait_ge(x2_lo, t // TPB + 1)
                if t >= 2:
                    pe.wait_ge(z_relu, t - 1)
                for n in range(2):
                    cols_ = slice(512 * n, 512 * n + 512)
                    nc.tensor.matmul(pairs[t % 2][:, cols_], sel3[:, :], bsyn3[:, cols_], start=True, stop=False)
                    for k in range(KD):
                        for part in (x2h, x2l):
                            ins = nc.tensor.matmul(pairs[t % 2][:, cols_], part[:, k, P * t:P * t + P], tsyn[:, k, cols_],
                                                   start=False, stop=(k == KD - 1 and part is x2l))
                ins.then_inc(z_ready, 1)

            def sum_found(b):
                pe.wait_ge(thresh_found, TPB * (b + 1))
                pe.wait_ge(x2T_moved, KD * B)
                if b >= 1:
                    pe.wait_ge(x4_stats, TPB * (b - 1) + 1)
                nc.tensor.matmul(bank(6)[0:1, TPB * b:TPB * b + TPB], ones[:, 0:1], found[:, TPB * b:TPB * b + TPB],
                                 start=True, stop=True).then_inc(found_sum, 1)

            def transpose_hidden(t):
                pe.wait_ge(hid_ready, t + 1)
                if t == 0:
                    pe.wait_ge(ln_stats, T)
                else:
                    pe.wait_ge(hT_moved, t)
                for f in range(FT):
                    ins = nc.tensor.transpose(pairs[2][:, P * f:P * f + P], hidden[:, t % 2, P * f:P * f + P], ident[:, :])
                ins.then_inc(hT_ready, 1)

            def last_product(t):
                pe.wait_ge(hT_moved, t + 1)
                if t >= 2:
                    pe.wait_ge(x4_stats, t - 1)
                for f in range(FT):
                    ins = nc.tensor.matmul(bank(6 + t % 2)[:, 0:D], hT[:, t % 2, P * f:P * f + P], tfin[:, f, :],
                                           start=(f == 0), stop=(f == FT - 1))
                ins.then_inc(out_ready, 1)

            pe.wait_ge(tern_ready, 2)
            pe.wait_ge(bsyn_ready, 1)
            transpose_x2(0)
            keep_warm(6, 0)
            transpose_x2(1)
            keep_warm(6, 0)
            synapse(0)
            synapse(1)
            transpose_x2(2)
            transpose_x2(3)
            for b in range(B + 2):
                one, two = TPB * (b - 2), TPB * (b - 2) + 1
                if b >= 2:
                    transpose_hidden(one)
                if b + 1 < B:
                    synapse(TPB * (b + 1))
                if b >= 2:
                    transpose_hidden(two)
                    last_product(one)
                    last_product(two)
                if 1 <= b <= B:
                    sum_found(b - 1)
                if b + 1 < B:
                    synapse(TPB * (b + 1) + 1)


def kernel(**inputs):
    import numpy as _np
    import concourse.bacc as _bacc
    from concourse import mybir as _mybir
    from concourse.bass_utils import run_bass_kernel_spmd as _run

    a = {k: _np.asarray(v) for k, v in inputs.items()}

    def by_column(v):
        return v.reshape(-1, P).T

    cond_t = a["cond_2048"].T.reshape(KD, P, B).transpose(1, 0, 2).reshape(P, KD * B)
    cols = _np.concatenate([cond_t, by_column(a["L0_cond_b_emb"]), by_column(a["L0_cond_g_norm"]),
                            by_column(a["L0_ffn_b1"]), by_column(a["L1_cond_ln_gamma"]),
                            by_column(a["L1_cond_ln_beta"])], axis=1)
    rows = _np.concatenate([a["L0_cond_g_q"], a["L0_cond_g_k"], a["L0_ffn_b2"], a["L1_ffn_b_out"], a["L1_ffn_gamma"],
                            a["L1_ffn_beta"], a["L1_cond_ln_gamma"], a["L1_cond_ln_beta"], a["L1_cond_rms_weight"],
                            a["cond_2048"][1], a["L1_ffn_b_syn"]])[None, :]
    feed = {
        "x": a["x"].reshape(B * S, D), "cols": cols, "rows": rows, "w_emb": a["L0_cond_W_emb"],
        "w_qkv": a["L0_cond_W_qkv"], "w_out": a["L0_cond_W_out"], "w1": a["L0_ffn_w1"], "w2": a["L0_ffn_w2"],
        "wk_t": a["L1_cond_Wk"].T, "wo_t": a["L1_cond_Wo"].T, "wsyn_t": a["L1_ffn_W_syn"].T,
        "wout_t": a["L1_ffn_W_out"].T,
    }
    nc = _bacc.Bacc("TRN2", target_bir_lowering=False, num_devices=1)
    arrays, args = {}, []
    for name, v in feed.items():
        v = _np.ascontiguousarray(v)
        arrays[f"in_{name}"] = v
        args.append(nc.dram_tensor(f"in_{name}", v.shape, _mybir.dt.from_np(v.dtype), kind="ExternalInput").ap())
    args.append(nc.dram_tensor("out_x", (B * S, D), F32, kind="ExternalOutput").ap())
    build(nc, *args)
    res = _run(nc, [arrays], core_ids=[0])
    return res.results[0]["out_x"].reshape(B, S, D)
```

```python
from contextlib import ExitStack

import concourse.bass as bass
from concourse import mybir

F32 = mybir.dt.float32
BF16 = mybir.dt.bfloat16
FP16 = mybir.dt.float16
I32 = mybir.dt.int32
ALU = mybir.AluOpType
ACT = mybir.ActivationFunctionType
AX = mybir.AxisListType

P = 128
B, S, D = 4, 256, 256
T = B * S // P
TPB = S // P
KD = D // P
HEADS = 16
DH = D // HEADS
PAIRS = HEADS // 2
HID = 1024
FT = HID // P
BLK = 8
BLK_TOKENS = S // BLK
TOPK = max(1, int(HID * (1.0 - 0.9)))
ROUND = 1.5 * 2.0 ** 23
QMAX = 127.0
QK_SCALE = 8.0

COLS = {}
ROWS = {}


def _lay(table, names):
    at = 0
    for name, n in names:
        table[name] = (at, at + n)
        at += n
    return at


NCOLS = _lay(COLS, [("cond", KD * B), ("b_emb", 2 * KD), ("g_norm", KD), ("b1", FT), ("ln_gamma", KD),
                    ("ln_beta", KD)])
NROWS = _lay(ROWS, [("g_q", DH), ("g_k", DH), ("b2", D), ("b_out", D), ("gamma", D), ("beta", D),
                    ("ln_gamma", D), ("ln_beta", D), ("rms_w", D), ("query", D), ("b_syn", HID)])

NEWTON = (1.0, 0.8, 0.6, 0.4)
AIM = TOPK - 4.5
START = 1.2816 / 0.3989 / HID
STEP = 1.0 / 0.3989 / HID / (HID * 0.1755)
WARM_FOUND = (10, 0, 12, 0)
FLAT_ROUNDS = -(-TOPK // 8)


def build(nc, x, cols, rows, w_emb, w_qkv, w_out, w1, w2, wk_t, wo_t, wsyn_t, wout_t, out):
    ctx = ExitStack()
    with ctx:
        def sb(name, shape, dt=F32):
            return ctx.enter_context(nc.sbuf_tensor(name, shape, dt))

        def sem(name):
            return ctx.enter_context(nc.semaphore(name))

        pairs = [ctx.enter_context(nc.psum_tensor(f"banks{2 * i}{2 * i + 1}", [P, 1024], F32)) for i in range(4)]

        def bank(i):
            return pairs[i // 2][:, (i % 2) * 512:(i % 2) * 512 + 512]

        def projection(b):
            return (bank(4), bank(5), bank(7), bank(7)[:, D:2 * D])[b][:, 0:D]

        def hidden_banks(t):
            return pairs[2] if t < T - 1 else pairs[1]

        def found_at(b):
            return (bank(7) if b < B - 1 else bank(0))[0:1, 0:1]

        ident = sb("ident", [P, P])
        ident_h = sb("ident_h", [P, P], FP16)
        ones = sb("ones", [P, P])
        neg_half = sb("neg_half", [P, TPB])
        eps_x = sb("eps_x", [P, 1])
        eps_qk = sb("eps_qk", [P, 1])
        table_in = sb("table_in", [P, 1])
        round_col = sb("round_col", [P, 1])
        block_of = sb("block_of", [P, P // BLK_TOKENS])
        rank8 = sb("rank8", [P, 8])
        newton_c = sb("newton_c", [P, len(NEWTON)])
        sel3 = sb("sel3", [96, P], BF16)
        col = sb("col", [P, NCOLS])
        row = sb("row", [P, NROWS])

        def c(name):
            return col[:, COLS[name][0]:COLS[name][1]]

        def r(name):
            return row[:, ROWS[name][0]:ROWS[name][1]]

        wemb = sb("wemb", [P, KD, 2 * D])
        wqkv = sb("wqkv", [P, KD, 3 * D])
        wout = sb("wout", [P, KD, D])
        w1s = sb("w1s", [P, FT, D])
        w2s = sb("w2s", [P, KD, HID])
        w1q = sb("w1q", [P, FT, D], FP16)
        w2q = sb("w2q", [P, KD, HID], FP16)
        w1qT = sb("w1qT", [P, KD, HID], FP16)
        w2qT = sb("w2qT", [P, FT, D], FP16)
        wk = sb("wk", [P, KD, D])
        wo = sb("wo", [P, KD, D])
        wsyn = sb("wsyn", [P, KD, HID])
        wfin = sb("wfin", [P, FT, D])
        tsyn = sb("tsyn", [P, KD, HID], FP16)
        tfin = wfin
        tfin_h = w1qT[:, :, :].rearrange("p k n -> p (k n)").rearrange("p (f d) -> p f d", f=FT)
        bsyn3 = w2s[0:96, 0, 0:HID // 2].bitcast(BF16)

        xs = sb("xs", [P, T, D])
        xr = sb("xr", [P, T, D])
        xnT = sb("xnT", [P, KD, B * S])
        early = sb("early", [P, 4, 2 * 2 * D])
        qkn = early[:, 0, :].rearrange("p (i a n) -> p i a n", i=2, a=2)
        sq = early[:, 1, :].rearrange("p (i n) -> p i n", i=2)
        qst = early[:, 2, :].bitcast(FP16).rearrange("p (i h s d) -> p i h s d", i=2, h=HEADS, s=4)
        kst = early[:, 3, :].bitcast(FP16).rearrange("p (i h s d) -> p i h s d", i=2, h=HEADS, s=4)
        stacks = sb("stacks", [P, 2, PAIRS, B * S], FP16)
        qT, kT = stacks[:, 0], stacks[:, 1]
        vaug = sb("vaug", [P, T, HEADS, 2 * DH])
        probs = sb("probs", [P, 4, 1024])
        late = sb("late", [P, 4, 2 * D])
        oT = late[:, 0:2]
        otm = late[:, 2].rearrange("p (i d) -> p i d", i=TPB)
        oTn = late[:, 3]
        yT = xnT
        yq = wqkv[:, :, :].rearrange("p k n -> p (k n)")[:, 0:B * S].bitcast(FP16).rearrange("p (k n) -> p k n", k=KD)
        hid = stacks[:, :, :, :].rearrange("p a b n -> p (a b n)").bitcast(F32).rearrange("p (f n) -> p f n", f=FT)
        hq = early[:, :, :].rearrange("p a n -> p (a n)").bitcast(FP16).rearrange("p (f n) -> p f n", f=FT)
        x1 = xs
        xb2 = sb("xb2", [P, T, D])
        x1b = wsyn[:, :, :].rearrange("p k n -> p (k n)").rearrange("p (t d) -> p t d", t=T)
        x2f = wemb[:, :, :].rearrange("p k (b n) -> p b k n", b=2)
        x2h = w1q[:, :, :].rearrange("p f d -> p (f d)").rearrange("p (k n) -> p k n", k=KD)
        x2l = w2q
        zp = vaug[:, :, :, :].rearrange("p t h d -> p (t h d)").rearrange("p (i n) -> p i n", i=4)
        hidden = probs[:, 0:2]
        hT = probs[:, 2:4]
        hT_hi, hT_lo = [probs[:, 2:4, 512 * j:512 * j + 512].bitcast(FP16) for j in range(2)]
        below = w1s[:, :, :].rearrange("p f d -> p (f d)")[:, 0:HID]
        minus = w1s[:, :, :].rearrange("p f d -> p (f d)")
        junk = [early[:, 0, HID // 2 * j:HID // 2 * (j + 1)].bitcast(BF16) for j in range(2)]
        junk_v = yT[:, 0, 0:HID // 2].bitcast(BF16)
        tmp = w2s[:, 1, :]
        fin, fin_g, x4, xh = [late[:, j].rearrange("p (i d) -> p i d", i=2) for j in range(4)]

        ssx = sb("ssx", [P, T])
        msx = sb("msx", [P, T])
        rx = sb("rx", [P, T])
        mod_a = sb("mod_a", [P, KD, B])
        mod_b = sb("mod_b", [P, KD, B])
        bemb1 = sb("bemb1", [P, KD])
        gg = sb("gg", [P, DH])
        ggt = sb("ggt", [P, D])
        ggmax = sb("ggmax", [P, 1])
        nbound = sb("nbound", [P, 1])
        ssq = sb("ssq", [P, 2, 2 * HEADS])
        msq = sb("msq", [P, 2, 2 * HEADS])
        rqk = sb("rqk", [P, 2, 2 * HEADS])
        rsum = sb("rsum", [P, 2, HEADS])
        ymax = sb("ymax", [P, B])
        amax = sb("amax", [P, 2])
        amax1 = sb("amax1", [1, 2])
        sx = sb("sx", [P, 2])
        sx_inv = sb("sx_inv", [P, 2])
        s1 = sb("s1", [P, FT])
        s1i = sb("s1i", [P, FT])
        s2 = sb("s2", [P, KD])
        s2i = sb("s2i", [P, KD])
        sc1 = sb("sc1", [P, FT])
        diag = early[:, 1, 0:KD * P].rearrange("p (m n) -> p m n", m=KD)
        s2row = ggt
        scale2 = ggt
        gmax = sb("gmax", [P, FT])
        wsum = sb("wsum", [P, 2])
        wtot = sb("wtot", [P, 2])
        wsc = sb("wsc", [P, 2])
        th = sb("th", [P, 2])
        nth = sb("nth", [P, 2])
        ssyn = sb("ssyn", [P, 1])
        ssyn_inv = sb("ssyn_inv", [P, 1])
        sfin = sb("sfin", [P, 1])
        lnbo = r("b_out")
        bs = r("b_syn")
        bsb = wqkv[:, :, :].rearrange("p k n -> p (k n)")[:, B * S:3 * D * KD].bitcast(BF16)
        brT = sb("brT", [P, KD, B * BLK])
        keys, keys_j, keys_k = [yT[0:B * BLK, 1, D * j:D * j + D] for j in range(3)]
        wq = row[0:B * BLK, ROWS["rms_w"][0]:ROWS["rms_w"][1]]
        raw = sb("raw", [B * BLK, 1])
        kss = sb("kss", [B * BLK, 1])
        kms = sb("kms", [B * BLK, 1])
        rk = sb("rk", [B * BLK, 1])
        score = sb("score", [B * BLK, 1])
        smax = sb("smax", [1, B])
        sdif = sb("sdif", [1, B, BLK])
        sexp = sb("sexp", [1, B, BLK])
        ssum = sb("ssum", [1, B])
        srec = sb("srec", [1, B])
        attn = sb("attn", [1, B, BLK])
        prod = sb("prod", [P, KD, B, BLK])
        att = sb("att", [P, KD, B])
        st1 = sb("st1", [P, T, 6])
        mv1 = sb("mv1", [P, T, 2])
        ve1 = sb("ve1", [P, T])
        rs1 = sb("rs1", [P, T])
        zsum = sb("zsum", [P, T])
        na = sb("na", [P, T, len(NEWTON)])
        nb = sb("nb", [P, T, len(NEWTON)])
        nt = sb("nt", [P, T, len(NEWTON) + 1])
        ne = sb("ne", [P, T])
        signs = sb("signs", [P, T, len(NEWTON) + 1])
        tpos = sb("tpos", [P, T])
        m8 = sb("m8", [P, T, 8])
        j8 = sb("j8", [P, 8])
        j8b = sb("j8b", [P, 8])
        clear = sb("clear", [P, T])
        thresh = sb("thresh", [P, T])
        found = sb("found", [P, T])
        flag = sb("flag", [1, B], I32)
        st2 = sb("st2", [P, T, 6])
        mv2 = sb("mv2", [P, T, 2])
        ve2 = sb("ve2", [P, T])
        rs2 = sb("rs2", [P, T])
        ne2 = sb("ne2", [P, T])

        ld_x = [sem(f"ld_x{b}") for b in range(B)]
        (ld_col, ld_gain, ld_row, ld_emb, ld_qkv, ld_out, ld_w1, ld_w2, ld_wk, ld_wo, ld_syn, ld_fin) = [
            sem("ld_" + n) for n in "col gain row emb qkv out w1 w2 wk wo syn fin".split()]
        consts = sem("consts")
        casts = sem("casts")
        pool_step = sem("pool_step")
        act_step = sem("act_step")
        dve_step = sem("dve_step")
        x_squared = sem("x_squared")
        x_rms = sem("x_rms")
        x_rstd = sem("x_rstd")
        x_scaled = sem("x_scaled")
        xT_ready = sem("xT_ready")
        xT_moved = sem("xT_moved")
        cond_ready = sem("cond_ready")
        mod_ready = sem("mod_ready")
        qk_ready = sem("qk_ready")
        v_ready = sem("v_ready")
        v_moved = sem("v_moved")
        qk_squared = sem("qk_squared")
        qk_summed = sem("qk_summed")
        qk_rms = sem("qk_rms")
        qk_rstd = sem("qk_rstd")
        qk_normed = sem("qk_normed")
        gg_ready = sem("gg_ready")
        ggt_ready = sem("ggt_ready")
        k_gained = sem("k_gained")
        q_hi = sem("q_hi")
        k_hi = sem("k_hi")
        q_lo = sem("q_lo")
        k_lo = sem("k_lo")
        qT_ready = sem("qT_ready")
        kT_ready = sem("kT_ready")
        qT_moved = sem("qT_moved")
        kT_moved = sem("kT_moved")
        s_ready = sem("s_ready")
        exp_done = sem("exp_done")
        pv_done = sem("pv_done")
        o_moved = sem("o_moved")
        ot_ready = sem("ot_ready")
        o_normed = sem("o_normed")
        oTn_ready = sem("oTn_ready")
        oTn_moved = sem("oTn_moved")
        wout_ready = sem("wout_ready")
        y_ready = sem("y_ready")
        y_moved = sem("y_moved")
        w1_inv = sem("w1_inv")
        w2_inv = sem("w2_inv")
        w1_scaled = sem("w1_scaled")
        w2_scaled = sem("w2_scaled")
        w_quant = sem("w_quant")
        wT_ready = sem("wT_ready")
        wT_moved = sem("wT_moved")
        wT_last = sem("wT_last")
        w_summed = sem("w_summed")
        w_total = sem("w_total")
        syn_inv = sem("syn_inv")
        tern_low = sem("tern_low")
        tern_ready = sem("tern_ready")
        bsyn_ready = sem("bsyn_ready")
        xb2_ready = sem("xb2_ready")
        diag_ready = sem("diag_ready")
        s2row_ready = sem("s2row_ready")
        s2row_moved = sem("s2row_moved")
        am_col = sem("am_col")
        am_row = sem("am_row")
        am_one = sem("am_one")
        am_all = sem("am_all")
        sx_ready = sem("sx_ready")
        y_scaled = sem("y_scaled")
        yq_ready = sem("yq_ready")
        f1_ready = sem("f1_ready")
        gelu_done = sem("gelu_done")
        hq_pool = sem("hq_pool")
        h_scaled = sem("h_scaled")
        hq_dve = sem("hq_dve")
        f2_ready = sem("f2_ready")
        f2_scaled = sem("f2_scaled")
        x1_even = sem("x1_even")
        x1_odd = sem("x1_odd")
        br_ready = sem("br_ready")
        br_moved = sem("br_moved")
        keys_ready = sem("keys_ready")
        keys_moved = sem("keys_moved")
        keys_sq = sem("keys_sq")
        keys_rstd = sem("keys_rstd")
        score_ready = sem("score_ready")
        score_row = sem("score_row")
        score_dif = sem("score_dif")
        score_exp = sem("score_exp")
        attn_ready = sem("attn_ready")
        attn_all = sem("attn_all")
        att_ready = sem("att_ready")
        pr_ready = sem("pr_ready")
        ln_stats = sem("ln_stats")
        ln_rstd = sem("ln_rstd")
        xhat_ready = sem("xhat_ready")
        x2T_ready = sem("x2T_ready")
        x2T_moved = sem("x2T_moved")
        x2T_moved_late = sem("x2T_moved_late")
        x2_hi = sem("x2_hi")
        x2_lo = sem("x2_lo")
        lnbo_ready = sem("lnbo_ready")
        x2g_ready = sem("x2g_ready")
        x2b_ready = sem("x2b_ready")
        x1b_ready = sem("x1b_ready")
        z_ready = sem("z_ready")
        z_relu = sem("z_relu")
        guess = [sem(f"guess{i}") for i in range(len(NEWTON) + 1)]
        counted = [sem(f"counted{i}") for i in range(len(NEWTON) + 1)]
        thresh_found = sem("thresh_found")
        found_sum = sem("found_sum")
        flag_read = sem("flag_read")
        hid_ready = sem("hid_ready")
        hT_ready = sem("hT_ready")
        hT_act = sem("hT_act")
        hT_dve = sem("hT_dve")
        hT_head = sem("hT_head")
        hT_rest = sem("hT_rest")
        out_ready = sem("out_ready")
        x4_stats = sem("x4_stats")
        x4_rstd = sem("x4_rstd")
        x4_shift = sem("x4_shift")
        x4_hat = sem("x4_hat")
        x4_gained = sem("x4_gained")
        fin_ready = sem("fin_ready")
        fin_last = sem("fin_last")
        stored = [sem("stored0"), sem("stored1")]

        N_CONST = 5
        POOL_F = (2, 6)
        F2_LATE = 5
        ACT_F = (1, 3, 5, 7)
        steps = {"pool": 0, "dve": 0}

        def chain(eng, which, s, ins):
            steps[which] += 1
            ins.then_inc(s, 1)
            eng.wait_ge(s, steps[which])

        block = ctx.enter_context(nc.Block())

        @block.sync
        def _(sp):
            sp.dma_start(col[:, :], cols).then_inc(ld_col, 16)
            for b in range(B):
                sp.dma_start(xs[:, TPB * b:TPB * b + TPB, :],
                             x[S * b:S * b + S, :].rearrange("(t p) d -> p t d", p=P)).then_inc(ld_x[b], 16)
                if b == 0:
                    sp.dma_start(wemb[:, :, :], w_emb.rearrange("(k p) n -> p k n", p=P)).then_inc(ld_emb, 16)
                    sp.dma_start(row[:, 0:2 * DH], rows[:, 0:2 * DH].broadcast_to([P, 2 * DH])).then_inc(ld_gain, 16)
                    sp.dma_start(wqkv[:, :, :], w_qkv.rearrange("(k p) n -> p k n", p=P)).then_inc(ld_qkv, 16)
            sp.dma_start(row[:, 2 * DH:NROWS], rows[:, 2 * DH:NROWS].broadcast_to([P, NROWS - 2 * DH])).then_inc(ld_row, 16)
            for dst, src, s in ((w1s, w1, ld_w1), (wout, w_out, ld_out), (w2s, w2, ld_w2), (wsyn, wsyn_t, ld_syn),
                                (wfin, wout_t, ld_fin), (wk, wk_t, ld_wk), (wo, wo_t, ld_wo)):
                sp.dma_start(dst[:, :, :], src.rearrange("(k p) n -> p k n", p=P)).then_inc(s, 16)
            for t in range(T):
                if t < T - 1:
                    sp.wait_ge(fin_ready, t + 1)
                else:
                    sp.wait_ge(fin_last, 1)
                sp.dma_start(out[t * P:t * P + P, :], fin[:, t % 2, :]).then_inc(stored[t % 2], 16)
            for s in stored:
                sp.wait_ge(s, 16 * T // 2)

        @block.gpsimd
        def _(pool):
            def step(ins):
                chain(pool, "pool", pool_step, ins)

            def rstd(out_, mean_sq, sums, scale, eps):
                step(pool.tensor_scalar(mean_sq, sums, scale, eps, ALU.mult, ALU.add))
                return pool.tensor_tensor(out_, mean_sq, neg_half[0:out_.shape[0], 0:out_.shape[1]], ALU.pow)

            step(pool.memset(ident[:, :], 0.0))
            pool.affine_select(out=ident[:, :], in_=ident[:, :], compare_op=ALU.not_equal, fill=1.0, base=0,
                               pattern=[[-1, P]], channel_multiplier=1).then_inc(consts, 1)
            pool.memset(neg_half[:, :], -0.5)
            pool.memset(eps_x[:, :], 1e-6)
            pool.memset(eps_qk[:, :], 1e-6 / QK_SCALE ** 2)
            pool.memset(ones[:, :], 1.0).then_inc(consts, 1)
            step(pool.memset(block_of[:, :], 0.0))
            for j in range(P // BLK_TOKENS):
                step(pool.memset(block_of[BLK_TOKENS * j:BLK_TOKENS * (j + 1), j:j + 1], 1.0))
            pool.memset(round_col[:, :], ROUND)
            for j in range(8):
                pool.memset(rank8[:, j:j + 1], float(2 * (TOPK - j - 1) - HID))
            for j, f in enumerate(NEWTON):
                pool.memset(newton_c[:, j:j + 1], -0.5 * f * STEP)
            step(pool.memset(sel3[:, :], 0.0))
            for j in range(3):
                step(pool.memset(sel3[32 * j:32 * j + 1, :], 1.0))
            pool.memset(vaug[:, :, :, DH:2 * DH], 1.0).then_inc(consts, 3)

            pool.wait_ge(gg_ready, 1)
            pool.tensor_copy(ggt[:, :].rearrange("p (h d) -> p h d", h=HEADS),
                             gg[:, :].unsqueeze(1).broadcast_to([P, HEADS, DH])).then_inc(ggt_ready, 1)
            pool.wait_ge(ggt_ready, 1)
            for t in range(T):
                i = t % 2
                pool.wait_ge(qk_normed, t + 1)
                pool.tensor_tensor(qkn[:, i, 1, :], qkn[:, i, 1, :], ggt[:, :], ALU.mult).then_inc(k_gained, 1)
                pool.wait_ge(k_gained, t + 1)
                if t >= 2:
                    pool.wait_ge(kT_ready, t - 1)
                pool.tensor_scalar(kst[:, i, :, 0::2, :],
                                   qkn[:, i, 1, :].rearrange("p (h d) -> p h d", h=HEADS).unsqueeze(2)
                                   .broadcast_to([P, HEADS, 2, DH]), 1.0, 1.0, ALU.mult, ALU.mult).then_inc(k_hi, 1)
                pool.wait_ge(k_hi, t + 1)
                pool.tensor_tensor(kst[:, i, :, 1::2, :],
                                   qkn[:, i, 1, :].rearrange("p (h d) -> p h d", h=HEADS).unsqueeze(2)
                                   .broadcast_to([P, HEADS, 2, DH]), kst[:, i, :, 0::2, :],
                                   ALU.subtract).then_inc(k_lo, 1)
            pool.wait_ge(w1_inv, 1)
            pool.tensor_tensor(w1s[:, :, :], w1s[:, :, :], s1i[:, :].unsqueeze(2).broadcast_to([P, FT, D]),
                               ALU.mult).then_inc(w1_scaled, 1)
            pool.wait_ge(w2_inv, 1)
            pool.tensor_tensor(w2s[:, :, :], w2s[:, :, :], s2i[:, :].unsqueeze(2).broadcast_to([P, KD, HID]),
                               ALU.mult).then_inc(w2_scaled, 1)
            pool.wait_ge(w_summed, 2)
            pool.partition_all_reduce(wtot[:, :], wsum[:, :], P, bass.bass_isa.ReduceOp.add).then_inc(w_total, 1)
            pool.wait_ge(ld_x[B - 1], 16)
            pool.wait_ge(ld_row, 16)
            for t in range(T):
                pool.tensor_tensor(xb2[:, t, :], xs[:, t, :], r("b2"), ALU.add).then_inc(xb2_ready, 1)
            pool.wait_ge(syn_inv, 1)
            step(pool.tensor_scalar(bs, r("b_syn"), ssyn_inv[:, 0:1], 1.0, ALU.mult, ALU.mult))
            for j in range(3):
                step(pool.tensor_scalar(bsyn3[32 * j:32 * j + 32, :], bs[32 * j:32 * j + 32, :], 1.0, 1.0, ALU.mult,
                                        ALU.mult))
                if j < 2:
                    step(pool.tensor_scalar(bsb, bs, 1.0, 1.0, ALU.mult, ALU.mult))
                    step(pool.tensor_tensor(bs, bs, bsb, ALU.subtract))
            pool.tensor_tensor(lnbo, r("ln_beta"), r("b_out"), ALU.add).then_inc(bsyn_ready, 1)
            pool.wait_ge(bsyn_ready, 1)
            pool.tensor_tensor(wq, row[0:B * BLK, ROWS["rms_w"][0]:ROWS["rms_w"][1]],
                               row[0:B * BLK, ROWS["query"][0]:ROWS["query"][1]], ALU.mult).then_inc(lnbo_ready, 1)

            pool.wait_ge(sx_ready, 2)
            for f in POOL_F:
                step(pool.tensor_scalar(hid[:, f, :], hid[:, f, :], sx_inv[:, 1:2], ROUND, ALU.mult, ALU.add))
                pool.tensor_scalar(hq[:, f, :], hid[:, f, :], 1.0, -ROUND, ALU.mult, ALU.add).then_inc(hq_pool, 1)
            for t in range(0, T, 2):
                pool.wait_ge(f2_scaled, t + 1)
                pool.tensor_tensor(x1[:, t, :], xr[:, t, :], xb2[:, t, :], ALU.add).then_inc(x1_even, 1)
            pool.wait_ge(keys_sq, 1)
            rstd(rk[:, :], kms[:, :], kss[:, :], 1.0 / D, 1e-6).then_inc(keys_rstd, 1)
            for t in range(T):
                pool.tensor_tensor(x1b[:, t, :], x1[:, t, :], r("beta"), ALU.add).then_inc(x1b_ready, 1)

            def x2_gain(t):
                pool.wait_ge(xhat_ready, t + 1)
                pool.tensor_tensor(xb2[:, t, :], xr[:, t, :], r("ln_gamma"), ALU.mult).then_inc(x2g_ready, 1)

            def x2_bias(t):
                pool.wait_ge(x2g_ready, t + 1)
                pool.tensor_tensor(xb2[:, t, :], xb2[:, t, :], lnbo, ALU.add).then_inc(x2b_ready, 1)

            def x2_split(b):
                if b < 2:
                    pool.wait_ge(x2T_moved, KD * (b + 1))
                else:
                    pool.wait_ge(x2T_moved_late, KD * (b - 1))
                pool.tensor_scalar(x2h[:, :, S * b:S * b + S], x2f[:, b % 2, :, :], 1.0, 1.0, ALU.mult,
                                   ALU.mult).then_inc(x2_hi, 1)

            def ln1(b):
                pool.wait_ge(ln_stats, TPB * (b + 1))
                t = slice(TPB * b, TPB * b + TPB)
                rstd(rs1[:, t], ve1[:, t], mv1[:, t, 1], 1.0, 1e-6).then_inc(ln_rstd, 1)

            def guess0(t):
                pool.wait_ge(z_relu, t + 1)
                pool.tensor_scalar(nt[:, t, 0:1], zsum[:, t:t + 1], -START, 0.0, ALU.mult, ALU.add).then_inc(guess[0], 1)
                step(pool.tensor_scalar(na[:, t, :], newton_c[:, :], zsum[:, t:t + 1], 1.0, ALU.mult, ALU.mult))
                pool.tensor_scalar(nb[:, t, :], na[:, t, :], float(HID - 2 * AIM), 0.0, ALU.mult, ALU.add)

            def newton(i, t):
                pool.wait_ge(counted[i], t + 1)
                step(pool.tensor_scalar(ne[:, t:t + 1], signs[:, t, i:i + 1], na[:, t, i:i + 1], nb[:, t, i:i + 1],
                                        ALU.mult, ALU.add))
                ins = pool.tensor_tensor(nt[:, t, i + 1:i + 2], nt[:, t, i:i + 1], ne[:, t:t + 1], ALU.add)
                if i + 1 < len(NEWTON):
                    ins.then_inc(guess[i + 1], 1)
                else:
                    step(ins)
                    pool.tensor_scalar(tpos[:, t:t + 1], nt[:, t, i + 1:i + 2], -1.0, 0.0, ALU.mult,
                                       ALU.add).then_inc(guess[i + 1], 1)

            def final_rstd(t):
                pool.wait_ge(x4_stats, t + 1)
                rstd(rs2[:, t:t + 1], ve2[:, t:t + 1], mv2[:, t, 1:2], 1.0, 1e-5).then_inc(x4_rstd, 1)
                pool.wait_ge(x4_rstd, t + 1)
                pool.tensor_scalar(ne2[:, t:t + 1], mv2[:, t, 0:1], rs2[:, t:t + 1], -1.0, ALU.mult,
                                   ALU.mult).then_inc(x4_shift, 1)

            def final_hat(t):
                pool.wait_ge(x4_shift, t + 1)
                if t >= 2:
                    pool.wait_ge(fin_ready, t - 1)
                pool.tensor_scalar(xh[:, t % 2, :], x4[:, t % 2, :], rs2[:, t:t + 1], ne2[:, t:t + 1], ALU.mult,
                                   ALU.add).then_inc(x4_hat, 1)

            def final_gain(t):
                pool.wait_ge(x4_hat, t + 1)
                pool.tensor_tensor(fin_g[:, t % 2, :], xh[:, t % 2, :], r("gamma"), ALU.mult).then_inc(x4_gained, 1)

            def final(t):
                pool.wait_ge(x4_gained, t + 1)
                if t >= 2:
                    pool.wait_ge(stored[t % 2], 16 * (t // 2))
                pool.tensor_tensor(fin[:, t % 2, :], fin_g[:, t % 2, :], x1b[:, t, :], ALU.add).then_inc(fin_ready, 1)

            pool.wait_ge(lnbo_ready, 1)
            ln1(0)
            ln1(1)
            x2_split(0)
            ln1(2)
            x2_split(1)
            guess0(0)
            ln1(3)
            guess0(1)
            for b in range(B + 2):
                one, two = TPB * b, TPB * b + 1
                done, last = TPB * (b - 2), TPB * (b - 2) - 1
                if 1 <= b < B:
                    guess0(one)
                    guess0(two)
                for i in range(len(NEWTON)):
                    x2_tile = 3 * b + i - 1
                    if b < B:
                        newton(i, one)
                    if i < 3 and 0 <= x2_tile < T:
                        x2_gain(x2_tile)
                    if b == 0 and i == 0:
                        x2_split(2)
                    if b >= 3 and i == 0:
                        final_rstd(last)
                    if b >= 3 and i == 1:
                        final_gain(last)
                    if b < B:
                        newton(i, two)
                    if i < 3 and 0 <= x2_tile < T:
                        x2_bias(x2_tile)
                    if b >= 3 and i == 0:
                        final_hat(last)
                    if b >= 3 and i == 1:
                        final(last)
                if b == 0:
                    x2_split(3)
                if b >= 2:
                    final_rstd(done)
                    final_hat(done)
                    if b == B + 1:
                        final_rstd(T - 1)
                    final_gain(done)
                    final(done)

        @block.scalar
        def _(act):
            def evac_xT(b):
                act.wait_ge(xT_ready, b + 1)
                for k in range(KD):
                    nc.scalar.activation(xnT[:, k, S * b:S * b + S], bank(0)[:, S * k:S * k + S], ACT.Identity,
                                         bias=mod_b[:, k, b:b + 1], scale=mod_a[:, k, b:b + 1]).then_inc(xT_moved, 1)

            def rms_x(b):
                act.wait_ge(ld_x[b], 16)
                for t in range(TPB * b, TPB * b + TPB):
                    nc.scalar.activation(early[:, t // 4, D * (t % 4):D * (t % 4) + D], xs[:, t, :], ACT.Square,
                                         accum_out=ssx[:, t:t + 1]).then_inc(x_squared, 1)
                act.wait_ge(x_squared, TPB * (b + 1))
                t = slice(TPB * b, TPB * b + TPB)
                nc.scalar.activation(msx[:, t], ssx[:, t], ACT.Sqrt, bias=eps_x[:, 0:1],
                                     scale=1.0 / D).then_inc(x_rms, 1)

            def rms_qk(t):
                act.wait_ge(qk_summed, t + 1)
                nc.scalar.activation(msq[:, t % 2, :], ssq[:, t % 2, :], ACT.Sqrt, bias=eps_qk[:, 0:1],
                                     scale=1.0 / (DH * QK_SCALE ** 2)).then_inc(qk_rms, 1)

            def load_table(function):
                nc.scalar.activation(table_in[:, :], eps_x[:, :], function).then_inc(act_step, 1)

            act.wait_ge(consts, 2)
            load_table(ACT.Sqrt)
            rms_x(0)
            rms_x(1)
            act.wait_ge(mod_ready, 1)
            evac_xT(0)
            for b in range(2, B):
                rms_x(b)
            def exponentiate(u):
                act.wait_ge(s_ready, u + 1)
                if u >= 4:
                    act.wait_ge(pv_done, (u - 4) // 2 + 1)
                nc.scalar.activation(probs[:, u % 4, :], pairs[u % 2][:, :], ACT.Exp, bias=nbound[:, 0:1],
                                     scale=DH ** -0.5 / QK_SCALE ** 2).then_inc(exp_done, 1)

            for t in range(T + 3):
                i = t % 2
                if t > T:
                    exponentiate(2 * (t - T) - 1)
                if 3 <= t:
                    act.wait_ge(kT_ready, t - 2)
                    nc.scalar.activation(kT[:, :, P * (t - 3):P * (t - 2)],
                                         bank(6).bitcast(FP16).rearrange("p (a n) -> p a n", a=PAIRS),
                                         ACT.Copy).then_inc(kT_moved, 1)
                if t == T:
                    act.wait_ge(gg_ready, 2)
                if t in (T, T + 1):
                    exponentiate(2 * (t - T))
                if t < T:
                    act.wait_ge(qk_ready, t + 1)
                    if t >= 2:
                        act.wait_ge(qk_summed, t - 1)
                    nc.scalar.activation(sq[:, i, :], bank(1 + i), ACT.Square).then_inc(qk_squared, 1)
                    act.wait_ge(v_ready, t + 1)
                    nc.scalar.activation(vaug[:, t, :, 0:DH],
                                         bank(3 + i)[:, 0:D].rearrange("p (h d) -> p h d", h=HEADS),
                                         ACT.Copy).then_inc(v_moved, 1)
                if 1 <= t <= T:
                    j = (t - 1) % 2
                    act.wait_ge(qk_normed, t)
                    if t >= 3:
                        act.wait_ge(qT_ready, t - 2)
                    nc.scalar.activation(qst[:, j, :, 0:2, :],
                                         qkn[:, j, 0, :].rearrange("p (h d) -> p h d", h=HEADS).unsqueeze(2)
                                         .broadcast_to([P, HEADS, 2, DH]), ACT.Copy).then_inc(q_hi, 1)
                if t < T:
                    rms_qk(t)
                    if t == T - 1:
                        act.wait_ge(act_step, 1)
                        load_table(ACT.Exp)
                    if i == 0 and t // TPB + 1 < B:
                        evac_xT(t // TPB + 1)

            for u in range(4, B * PAIRS):
                exponentiate(u)

            act.wait_ge(wT_ready, B)
            nc.scalar.activation(w2qT[:, :, P:2 * P], bank(6).bitcast(FP16).rearrange("p (f n) -> p f n", f=FT),
                                 ACT.Copy).then_inc(wT_last, 1)

            act.wait_ge(act_step, 2)
            load_table(ACT.Gelu)
            act.wait_ge(sx_ready, 1)
            nc.scalar.activation(tmp[:, :], yT[:, 1, :], ACT.Identity, bias=round_col[:, 0:1],
                                 scale=sx_inv[:, 0:1]).then_inc(y_scaled, 1)
            act.wait_ge(ld_col, 16)
            for f in range(FT):
                act.wait_ge(f1_ready, f + 1)
                nc.scalar.activation(hid[:, f, :], pairs[f % 2][:, :], ACT.Gelu,
                                     bias=col[:, COLS["b1"][0] + f:COLS["b1"][0] + f + 1],
                                     scale=sc1[:, f:f + 1]).then_inc(gelu_done, 1)
            act.wait_ge(sx_ready, 2)
            act.wait_ge(gelu_done, FT)
            for f in ACT_F:
                nc.scalar.activation(hid[:, f, :], hid[:, f, :], ACT.Identity, bias=round_col[:, 0:1],
                                     scale=sx_inv[:, 1:2]).then_inc(h_scaled, 1)

            act.wait_ge(act_step, 3)
            load_table(ACT.Exp)
            act.wait_ge(keys_moved, 1)
            nc.scalar.activation(keys_j, keys, ACT.Square, accum_out=kss[:, :]).then_inc(keys_sq, 1)
            act.wait_ge(score_dif, 1)
            nc.scalar.activation(sexp[:, :, :], sdif[:, :, :], ACT.Exp).then_inc(score_exp, 1)

            def evac_x2T(b):
                act.wait_ge(x2T_ready, b + 1)
                for k in range(KD):
                    nc.scalar.activation(x2f[:, b % 2, k, :], bank(6)[:, S * k:S * k + S], ACT.Identity,
                                         bias=col[:, COLS["ln_beta"][0] + k:COLS["ln_beta"][0] + k + 1],
                                         scale=col[:, COLS["ln_gamma"][0] + k:COLS["ln_gamma"][0] + k + 1]
                                         ).then_inc(x2T_moved, 1)

            counts = []

            def relu(t):
                act.wait_ge(z_ready, t + 1)
                if t >= 4:
                    act.wait_ge(hid_ready, t - 3)
                nc.scalar.activation(zp[:, t % 4, :], pairs[t % 2][:, :], ACT.Relu,
                                     accum_out=zsum[:, t:t + 1]).then_inc(z_relu, 1)

            def count(i, t):
                act.wait_ge(guess[i], t + 1)
                if len(counts) >= 2:
                    act.wait_ge(*counts[-2])
                counts.append((counted[i], t + 1))
                nc.scalar.activation(junk[len(counts) % 2], zp[:, t % 4, :], ACT.Sign, bias=nt[:, t, i:i + 1],
                                     accum_out=signs[:, t, i:i + 1]).then_inc(counted[i], 1)

            def move_hT(t):
                act.wait_ge(hT_ready, t + 1)
                if t >= 2:
                    act.wait_ge(out_ready, t - 1)
                n = 512 if t < T - TPB - 1 else 1024
                nc.scalar.activation(hT[:, t % 2, 0:n], hidden_banks(t)[:, 0:n], ACT.Copy).then_inc(hT_act, 1)

            def head_hT(t):
                act.wait_ge(hT_ready, t + 1)
                act.wait_ge(out_ready, t - 1)
                nc.scalar.activation(hT_hi[:, t % 2, :], hidden_banks(t)[:, :], ACT.Copy).then_inc(hT_head, 1)

            evac_x2T(0)
            evac_x2T(1)
            act.wait_ge(z_ready, 1)
            for b in range(B + 2):
                if b < B:
                    relu(TPB * b)
                    relu(TPB * b + 1)
                for i in range(len(NEWTON) + 1):
                    if b < B:
                        count(i, TPB * b)
                        count(i, TPB * b + 1)
                    if 2 <= b <= B and i == 0:
                        move_hT(TPB * (b - 2) + 1)
            head_hT(T - 2)
            head_hT(T - 1)

        @block.vector
        def _(dve):
            def step(ins):
                chain(dve, "dve", dve_step, ins)

            dve.wait_ge(consts, 1)
            dve.tensor_copy(ident_h[:, :], ident[:, :]).then_inc(casts, 1)
            for b in range(B):
                dve.wait_ge(x_rms, b + 1)
                dve.reciprocal(rx[:, TPB * b:TPB * b + TPB], msx[:, TPB * b:TPB * b + TPB]).then_inc(x_rstd, 1)
                dve.wait_ge(x_rstd, b + 1)
                for t in range(TPB * b, TPB * b + TPB):
                    dve.tensor_scalar(xr[:, t, :], xs[:, t, :], rx[:, t:t + 1], None, ALU.mult).then_inc(x_scaled, 1)
                if b == 0:
                    dve.wait_ge(ld_col, 16)
                    step(dve.tensor_scalar(bemb1[:, :], col[:, COLS["b_emb"][0]:COLS["b_emb"][0] + KD], 1.0, None, ALU.add))
                    dve.wait_ge(cond_ready, 1)
                    for k in range(KD):
                        dve.tensor_scalar(mod_a[:, k, :], bank(7)[:, B * k:B * k + B], bemb1[:, k:k + 1],
                                          col[:, COLS["g_norm"][0] + k:COLS["g_norm"][0] + k + 1], ALU.add, ALU.mult)
                        bk = COLS["b_emb"][0] + KD + k
                        ins = dve.tensor_scalar(mod_b[:, k, :], bank(7)[:, B * (KD + k):B * (KD + k) + B],
                                                col[:, bk:bk + 1], None, ALU.add)
                    ins.then_inc(mod_ready, 1)
                    dve.wait_ge(ld_gain, 16)
                    dve.tensor_tensor(gg[:, :], r("g_q"), r("g_k"), ALU.mult).then_inc(gg_ready, 1)
                    dve.wait_ge(gg_ready, 1)
                    step(dve.tensor_reduce(ggmax[:, :], gg[:, :], AX.X, ALU.max, apply_absolute_value=True))
                    dve.tensor_scalar(nbound[:, :], ggmax[:, :], -(float(DH) ** 0.5), None, ALU.mult).then_inc(gg_ready, 1)

            def move_qT(t):
                dve.wait_ge(qT_ready, t + 1)
                dve.tensor_copy(qT[:, :, P * t:P * t + P],
                                bank(5).bitcast(FP16).rearrange("p (a n) -> p a n", a=PAIRS)).then_inc(qT_moved, 1)

            def split_low(t):
                i = t % 2
                dve.wait_ge(q_hi, t + 1)
                dve.tensor_tensor(qst[:, i, :, 2:4, :],
                                  qkn[:, i, 0, :].rearrange("p (h d) -> p h d", h=HEADS).unsqueeze(2)
                                  .broadcast_to([P, HEADS, 2, DH]), qst[:, i, :, 0:2, :], ALU.subtract).then_inc(q_lo, 1)

            for t in range(T + 2):
                i = t % 2
                if 3 <= t:
                    move_qT(t - 3)
                if t < T:
                    dve.wait_ge(qk_squared, t + 1)
                    if t >= 2:
                        dve.wait_ge(qk_rms, t - 1)
                    dve.tensor_reduce(ssq[:, i, :], sq[:, i, :].rearrange("p (h d) -> p h d", d=DH), AX.X,
                                      ALU.add).then_inc(qk_summed, 1)
                if 1 <= t <= T:
                    split_low(t - 1)
                if t < T:
                    dve.wait_ge(qk_rms, t + 1)
                    dve.reciprocal(rqk[:, i, :], msq[:, i, :]).then_inc(qk_rstd, 1)
                    dve.wait_ge(qk_rstd, t + 1)
                    if t >= 2:
                        dve.wait_ge(q_lo, t - 1)
                        dve.wait_ge(k_lo, t - 1)
                    dve.tensor_tensor(qkn[:, i, :, :].rearrange("p a (h d) -> p (a h) d", d=DH),
                                      bank(1 + i).rearrange("p (h d) -> p h d", d=DH),
                                      rqk[:, i, :].unsqueeze(2).broadcast_to([P, 2 * HEADS, DH]),
                                      ALU.mult).then_inc(qk_normed, 1)

            def scales(w, ld, s, s_inv, ready):
                dve.wait_ge(ld, 16)
                step(dve.tensor_reduce(s[:, :], w[:, :, :], AX.X, ALU.max, apply_absolute_value=True))
                step(dve.tensor_scalar(s[:, :], s[:, :], 1.0 / QMAX, 1e-8, ALU.mult, ALU.max))
                dve.reciprocal(s_inv[:, :], s[:, :]).then_inc(ready, 1)

            def quantise(w, q, scaled):
                dve.wait_ge(scaled, 1)
                dve.tensor_scalar(q[:, :, :], w[:, :, :], ROUND, -ROUND, ALU.add, ALU.add).then_inc(w_quant, 1)

            def weight_sum(i, w, ld):
                dve.wait_ge(ld, 16)
                dve.tensor_reduce(wsum[:, i:i + 1], w[:, :, :], AX.XY, ALU.add,
                                  apply_absolute_value=True).then_inc(w_summed, 1)

            def ternary_scales():
                dve.wait_ge(w_total, 1)
                step(dve.tensor_scalar(wsc[:, :], wtot[:, :], 1.0 / (HID * D), None, ALU.mult))
                step(dve.tensor_scalar(th[:, :], wsc[:, :], 1e-8, 0.5, ALU.add, ALU.mult))
                step(dve.tensor_scalar(nth[:, :], th[:, :], -1.0, None, ALU.mult))
                step(dve.tensor_scalar(ssyn[:, :], wsc[:, 0:1], 1e-30, None, ALU.max))
                dve.reciprocal(ssyn_inv[:, :], ssyn[:, :]).then_inc(syn_inv, 1)
                dve.tensor_tensor(sfin[:, :], ssyn[:, :], wsc[:, 1:2], ALU.mult)

            def ternary_low(w, i):
                if i == 1:
                    dve.wait_ge(tern_ready, 2)
                dve.tensor_scalar(minus, w[:, :, :].rearrange("p a n -> p (a n)"), nth[:, i:i + 1], None,
                                  ALU.is_lt).then_inc(tern_low, 1)

            def ternary(w, q, i, part=slice(0, 2 * HID)):
                flat_w = w[:, :, :].rearrange("p a n -> p (a n)")[:, part]
                flat_q = q[:, :, :].rearrange("p a n -> p (a n)")[:, part]
                dve.wait_ge(tern_low, i + 1)
                dve.scalar_tensor_tensor(out=flat_q, in0=flat_w, scalar=th[:, i:i + 1], in1=minus[:, part], op0=ALU.is_gt,
                                         op1=ALU.subtract).then_inc(tern_ready, 1)

            def out_weights():
                dve.wait_ge(ld_out, 16)
                for k in range(KD):
                    ins = dve.tensor_tensor(wout[:, k, P * k:P * k + P], wout[:, k, P * k:P * k + P], ident[:, :], ALU.add)
                ins.then_inc(wout_ready, 1)

            def move_o(q):
                dve.wait_ge(pv_done, 2 * q + 2)
                if q >= 2:
                    dve.wait_ge(ot_ready, TPB * (q // 2))
                dve.tensor_copy(oT[:, q % 2, :], bank(4 + q % 2)).then_inc(o_moved, 1)

            def norm_o(t):
                i = t % TPB
                dve.wait_ge(ot_ready, t + 1)
                if t >= TPB:
                    dve.wait_ge(oTn_ready, t // TPB)
                view = bank(6 + i).rearrange("p (h d) -> p h d", h=HEADS)
                step(dve.reciprocal(rsum[:, i, :], view[:, :, DH]))
                dve.tensor_tensor(otm[:, i, :].rearrange("p (h d) -> p h d", h=HEADS), view[:, :, 0:DH],
                                  rsum[:, i, :].unsqueeze(2).broadcast_to([P, HEADS, DH]), ALU.mult).then_inc(o_normed, 1)

            def move_oTn(b):
                dve.wait_ge(oTn_ready, b + 1)
                if b >= 1:
                    dve.wait_ge(y_ready, b)
                dve.tensor_copy(oTn[:, :], bank(6)).then_inc(oTn_moved, 1)

            def move_y(b):
                dve.wait_ge(y_ready, b + 1)
                dve.tensor_reduce(ymax[:, b:b + 1], bank(7), AX.X, ALU.max, apply_absolute_value=True)
                dve.tensor_copy(yT[:, :, S * b:S * b + S],
                                bank(7).rearrange("p (m n) -> p m n", m=KD)).then_inc(y_moved, 1)

            def move_wT(i):
                dve.wait_ge(wT_ready, i + 1)
                src = bank(6).bitcast(FP16)
                if i < KD:
                    dve.tensor_copy(w1qT[:, i, :], src).then_inc(wT_moved, 1)
                else:
                    dve.tensor_copy(w2qT[:, :, 0:P], src.rearrange("p (f n) -> p f n", f=FT)).then_inc(wT_moved, 1)

            def scale_diagonals():
                for m in range(KD):
                    ins = dve.tensor_scalar(diag[:, m, :], ident[:, :], s2[:, m:m + 1], None, ALU.mult)
                ins.then_inc(diag_ready, 1)

            scales(w1s, ld_w1, s1, s1i, w1_inv)
            move_qT(T - 1)
            out_weights()
            scales(w2s, ld_w2, s2, s2i, w2_inv)
            move_o(0)
            scale_diagonals()
            weight_sum(0, wsyn, ld_syn)
            move_o(1)
            for b in range(B):
                norm_o(TPB * b)
                norm_o(TPB * b + 1)
                if b == 0:
                    quantise(w1s, w1q, w1_scaled)
                if b == 1:
                    weight_sum(1, wfin, ld_fin)
                if b == 2:
                    ternary_low(wsyn, 0)
                move_oTn(b)
                if b + 1 < B:
                    move_o(2 * b + 2)
                if b == 3:
                    ternary(wsyn, tsyn, 0, slice(0, HID))
                move_y(b)
                if b + 1 < B:
                    move_wT(b)
                if b == 0:
                    quantise(w2s, w2q, w2_scaled)
                if b == 1:
                    ternary_scales()
                if b + 1 < B:
                    move_o(2 * b + 3)

            def scale_from(src, n):
                dve.tensor_reduce(amax[:, n:n + 1], src, AX.X, ALU.max).then_inc(am_col, 1)
                dve.wait_ge(am_row, n + 1)
                dve.tensor_reduce(amax1[0:1, n:n + 1], bank(4 - 4 * n)[0:1, 0:P], AX.X, ALU.max).then_inc(am_one, 1)
                dve.wait_ge(am_all, n + 1)
                step(dve.tensor_scalar(sx[:, n:n + 1], bank(4 - 4 * n)[:, P:P + 1], 1.0 / QMAX, 1e-8, ALU.mult, ALU.max))
                return dve.reciprocal(sx_inv[:, n:n + 1], sx[:, n:n + 1])

            dve.wait_ge(y_moved, B)
            scale_from(ymax[:, :], 0).then_inc(sx_ready, 1)
            dve.wait_ge(sx_ready, 1)
            step(dve.tensor_scalar(yT[:, 0, :], yT[:, 0, :], sx_inv[:, 0:1], ROUND, ALU.mult, ALU.add))
            dve.tensor_scalar(yq[:, 0, :], yT[:, 0, :], -ROUND, None, ALU.add).then_inc(yq_ready, 1)
            dve.wait_ge(y_scaled, 1)
            dve.tensor_scalar(yq[:, 1, :], tmp[:, :], -ROUND, None, ALU.add).then_inc(yq_ready, 1)
            dve.tensor_scalar(sc1[:, :], s1[:, :], sx[:, 0:1], None, ALU.mult).then_inc(yq_ready, 1)
            dve.wait_ge(s2row_ready, 1)
            dve.tensor_copy(s2row[:, :], bank(5)[:, 0:D]).then_inc(s2row_moved, 1)
            ternary(wsyn, tsyn, 0, slice(HID, 2 * HID))
            for f in range(FT):
                dve.wait_ge(gelu_done, f + 1)
                ins = dve.tensor_reduce(gmax[:, f:f + 1], hid[:, f, :], AX.X, ALU.max, apply_absolute_value=True)
            step(ins)
            scale_from(gmax[:, :], 1).then_inc(sx_ready, 1)
            dve.wait_ge(sx_ready, 2)
            dve.wait_ge(s2row_moved, 1)
            scaled = 0
            for f in range(FT):
                if f in POOL_F:
                    continue
                if f in ACT_F:
                    scaled += 1
                    dve.wait_ge(h_scaled, scaled)
                for cols_ in ([slice(0, 512), slice(512, 1024)] if f == 0 else [slice(0, 1024)]):
                    if f not in ACT_F:
                        step(dve.tensor_scalar(hid[:, f, cols_], hid[:, f, cols_], sx_inv[:, 1:2], ROUND, ALU.mult,
                                               ALU.add))
                    dve.tensor_scalar(hq[:, f, cols_], hid[:, f, cols_], -ROUND, None, ALU.add).then_inc(hq_dve, 1)
            step(dve.tensor_scalar(scale2[:, :], s2row[:, :], sx[:, 1:2], None, ALU.mult))
            for t in range(T):
                dve.wait_ge(f2_ready, t // TPB + 1)
                dve.tensor_tensor(xr[:, t, :], bank(4 + t // TPB)[:, D * (t % TPB):D * (t % TPB) + D], scale2[:, :],
                                  ALU.mult).then_inc(f2_scaled, 1)
                if t % 2:
                    dve.wait_ge(f2_scaled, t + 1)
                    dve.tensor_tensor(x1[:, t, :], xr[:, t, :], xb2[:, t, :], ALU.add).then_inc(x1_odd, 1)

            dve.wait_ge(br_ready, 1)
            dve.tensor_copy(brT[:, :, :].rearrange("p k n -> p (k n)"), bank(0)[:, 0:KD * B * BLK]).then_inc(br_moved, 1)
            dve.wait_ge(keys_ready, 1)
            dve.tensor_copy(keys, bank(1)[0:B * BLK, 0:D]).then_inc(keys_moved, 1)
            dve.wait_ge(keys_moved, 1)
            dve.wait_ge(lnbo_ready, 1)
            dve.scalar_tensor_tensor(out=keys_k, in0=keys, scalar=1.0, in1=wq, op0=ALU.mult,
                                     op1=ALU.mult, accum_out=raw[:, :]).then_inc(dve_step, 1)
            steps["dve"] += 1
            dve.wait_ge(dve_step, steps["dve"])
            dve.wait_ge(keys_rstd, 1)
            dve.tensor_tensor(score[:, :], raw[:, :], rk[:, :], ALU.mult).then_inc(score_ready, 1)
            dve.wait_ge(score_row, 1)
            srow = bank(2)[0:1, 0:B * BLK].rearrange("p (b n) -> p b n", b=B)
            step(dve.tensor_reduce(smax[:, :], srow, AX.X, ALU.max))
            dve.tensor_tensor(sdif[:, :, :], srow, smax[:, :].unsqueeze(2).broadcast_to([1, B, BLK]),
                              ALU.subtract).then_inc(score_dif, 1)
            dve.wait_ge(score_exp, 1)
            step(dve.tensor_reduce(ssum[:, :], sexp[:, :, :], AX.X, ALU.add))
            step(dve.reciprocal(srec[:, :], ssum[:, :]))
            dve.tensor_tensor(attn[:, :, :], sexp[:, :, :], srec[:, :].unsqueeze(2).broadcast_to([1, B, BLK]),
                              ALU.mult).then_inc(attn_ready, 1)
            dve.wait_ge(attn_all, 1)
            for k in range(KD):
                ins = dve.tensor_tensor(prod[:, k, :, :].rearrange("p b n -> p (b n)"), brT[:, k, :],
                                        bank(2)[:, 64:64 + B * BLK], ALU.mult)
            step(ins)
            dve.tensor_reduce(att[:, :, :].rearrange("p k b -> p (k b)"),
                              prod[:, :, :, :].rearrange("p k b n -> p (k b) n"), AX.X, ALU.add).then_inc(att_ready, 1)

            def ln1_stats(t):
                b = t // TPB
                dve.wait_ge(pr_ready, b + 1 if b < 2 else B)
                step(dve.tensor_tensor(xr[:, t, :], x1[:, t, :], projection(b), ALU.add))
                step(dve.bn_stats(st1[:, t, :], xr[:, t, :]))
                dve.bn_aggr(mv1[:, t, :], st1[:, t, :]).then_inc(ln_stats, 1)

            def ln1_hat(b):
                dve.wait_ge(ln_rstd, b + 1)
                for t in range(TPB * b, TPB * b + TPB):
                    dve.tensor_scalar(xr[:, t, :], xr[:, t, :], mv1[:, t, 0:1], rs1[:, t:t + 1], ALU.subtract,
                                      ALU.mult).then_inc(xhat_ready, 1)

            def evac_x2T(b):
                dve.wait_ge(x2T_ready, b + 1)
                dve.wait_ge(x2_lo, b - 1)
                for k in range(KD):
                    dve.tensor_scalar(x2f[:, b % 2, k, :], bank(6)[:, S * k:S * k + S],
                                      col[:, COLS["ln_gamma"][0] + k:COLS["ln_gamma"][0] + k + 1],
                                      col[:, COLS["ln_beta"][0] + k:COLS["ln_beta"][0] + k + 1], ALU.mult,
                                      ALU.add).then_inc(x2T_moved_late, 1)

            def x2_low(b):
                dve.wait_ge(x2_hi, b + 1)
                dve.tensor_tensor(x2l[:, :, S * b:S * b + S], x2f[:, b % 2, :, :], x2h[:, :, S * b:S * b + S],
                                  ALU.subtract).then_inc(x2_lo, 1)

            ln1_stats(0)
            ln1_stats(1)
            ln1_stats(2)
            ln1_hat(0)
            ln1_stats(3)
            ln1_stats(4)
            ln1_hat(1)
            x2_low(0)
            ln1_stats(5)
            ln1_stats(6)
            x2_low(1)
            ln1_hat(2)
            ln1_stats(7)
            evac_x2T(2)
            ln1_hat(3)
            x2_low(2)
            evac_x2T(3)
            ternary_low(wfin, 1)
            ternary(wfin, tfin, 1)
            dve.wait_ge(tern_ready, 3)
            dve.tensor_copy(tfin_h, tfin[:, :, :]).then_inc(tern_ready, 1)

            def eight_below(t):
                z = zp[:, t % 4, :]
                dve.wait_ge(guess[len(NEWTON)], t + 1)
                step(dve.scalar_tensor_tensor(out=below, in0=z, scalar=tpos[:, t:t + 1], in1=z, op0=ALU.is_le,
                                              op1=ALU.mult))
                step(dve.max(m8[:, t, :], below))
                step(dve.tensor_scalar(clear[:, t:t + 1], m8[:, t, 0:1], tpos[:, t:t + 1], None, ALU.is_lt))

            def threshold(t):
                dve.wait_ge(counted[len(NEWTON)], t + 1)
                sign_sum = signs[:, t, len(NEWTON):len(NEWTON) + 1]
                dve.scalar_tensor_tensor(out=j8[:, :], in0=rank8[:, :], scalar=sign_sum, in1=m8[:, t, :],
                                         op0=ALU.is_equal, op1=ALU.mult, accum_out=thresh[:, t:t + 1])
                dve.scalar_tensor_tensor(out=j8b[:, :], in0=rank8[:, :], scalar=sign_sum,
                                         in1=clear[:, t:t + 1].broadcast_to([P, 8]), op0=ALU.is_equal, op1=ALU.mult,
                                         accum_out=found[:, t:t + 1]).then_inc(thresh_found, 1)

            def any_row(b):
                dve.wait_ge(found_sum, b + 1)
                dve.tensor_scalar(flag[0:1, b:b + 1], found_at(b), TPB * P - 0.5, None,
                                  ALU.is_lt).then_inc(flag_read, 1)
                dve.wait_ge(flag_read, b + 1)
                missing = dve.value_load(flag[0:1, b:b + 1], min_val=0, max_val=1)
                with dve.If(missing):
                    for t in range(TPB * b, TPB * b + TPB):
                        dve.tensor_copy(below, zp[:, t % 4, :])
                        dve.drain()
                        with dve.Fori(0, FLAT_ROUNDS - 1):
                            dve.max(m8[:, t, :], below)
                            dve.drain()
                            dve.match_replace(below, m8[:, t, :], below, 0.0)
                            dve.drain()
                        dve.max(m8[:, t, :], below)
                        dve.drain()
                        last = TOPK - 8 * (FLAT_ROUNDS - 1) - 1
                        dve.tensor_copy(thresh[:, t:t + 1], m8[:, t, last:last + 1])
                        dve.drain()

            def keep(t):
                z = zp[:, t % 4, :]
                if t >= 2:
                    dve.wait_ge(hT_ready, t - 1)
                dve.scalar_tensor_tensor(out=hidden[:, t % 2, :], in0=z, scalar=thresh[:, t:t + 1], in1=z,
                                         op0=ALU.is_ge, op1=ALU.mult).then_inc(hid_ready, 1)

            def move_hT(t):
                dve.wait_ge(hT_ready, t + 1)
                if t >= 2:
                    dve.wait_ge(out_ready, t - 1)
                at = 512 * (t % TPB)
                dve.tensor_copy(hT[:, t % 2, at:1024], pairs[2][:, at:1024]).then_inc(hT_dve, 1)

            def rest_hT(t):
                dve.wait_ge(hT_head, t - (T - TPB) + 1)
                dve.tensor_tensor(hT_lo[:, t % 2, :], hidden_banks(t)[:, :], hT_hi[:, t % 2, :],
                                  ALU.subtract).then_inc(hT_rest, 1)

            def last_stats(t):
                dve.wait_ge(out_ready, t + 1)
                dve.wait_ge(x2b_ready, t + 1)
                if t >= 2:
                    dve.wait_ge(fin_ready, t - 1)
                step(dve.scalar_tensor_tensor(out=x4[:, t % 2, :], in0=bank(6 + t % 2)[:, 0:D], scalar=sfin[:, 0:1],
                                              in1=xb2[:, t, :], op0=ALU.mult, op1=ALU.add))
                step(dve.bn_stats(st2[:, t, :], x4[:, t % 2, :]))
                dve.bn_aggr(mv2[:, t, :], st2[:, t, :]).then_inc(x4_stats, 1)

            for b in range(B + 1):
                one, two = TPB * b, TPB * b + 1
                done, last = one - TPB, two - TPB
                if b < B:
                    eight_below(one)
                    threshold(one)
                if b == 0:
                    x2_low(3)
                if 1 <= b < B - 1:
                    move_hT(last)
                if b < B:
                    eight_below(two)
                    threshold(two)
                if b == B - 1:
                    last_stats(done)
                if b < B:
                    any_row(b)
                    keep(one)
                    keep(two)
                if 1 <= b < B - 1:
                    last_stats(done)
                if b < B - 1:
                    move_hT(one)
                if b == B:
                    last_stats(done)
                if b >= 1:
                    last_stats(last)
                if b == B - 1:
                    rest_hT(one)
                    rest_hT(two)
            dve.wait_ge(x4_rstd, T)
            step(dve.tensor_scalar(xh[:, 1, :], x4[:, 1, :], mv2[:, T - 1, 0:1], rs2[:, T - 1:T], ALU.subtract, ALU.mult))
            step(dve.tensor_tensor(fin_g[:, 1, :], xh[:, 1, :], r("gamma"), ALU.mult))
            dve.wait_ge(stored[1], 16 * (T // 2 - 1))
            dve.tensor_tensor(fin[:, 1, :], fin_g[:, 1, :], x1b[:, T - 1, :], ALU.add).then_inc(fin_last, 1)

        @block.tensor
        def _(pe):
            def keep_warm(n, bk):
                for _ in range(n):
                    nc.tensor.matmul(bank(bk), ident_h[:, :], ident_h[:, :].unsqueeze(1).broadcast_to([P, 4, P]),
                                     start=True, stop=True)

            pe.wait_ge(casts, 1)
            keep_warm(12, 6)
            pe.wait_ge(ld_emb, 16)
            pe.wait_ge(ld_col, 16)
            for m in range(2 * KD):
                for k in range(KD):
                    ins = nc.tensor.matmul(bank(7)[:, B * m:B * m + B], wemb[:, k, P * m:P * m + P],
                                           col[:, B * k:B * k + B], start=(k == 0), stop=(k == KD - 1))
            ins.then_inc(cond_ready, 1)

            def transpose_x(b):
                pe.wait_ge(x_scaled, TPB * (b + 1))
                if b >= 1:
                    pe.wait_ge(xT_moved, KD * b)
                for k in range(KD):
                    for i in range(TPB):
                        ins = nc.tensor.transpose(bank(0)[:, S * k + P * i:S * k + P * i + P],
                                                  xr[:, TPB * b + i, P * k:P * k + P], ident[:, :])
                ins.then_inc(xT_ready, 1)

            def project(t):
                i = t % 2
                pe.wait_ge(xT_moved, KD * (t // TPB + 1))
                if t >= 2:
                    pe.wait_ge(qk_normed, t - 1)
                    pe.wait_ge(v_moved, t - 1)
                for k in range(KD):
                    ins = nc.tensor.matmul(bank(1 + i), xnT[:, k, P * t:P * t + P], wqkv[:, k, 0:2 * D],
                                           start=(k == 0), stop=(k == KD - 1))
                ins.then_inc(qk_ready, 1)
                for k in range(KD):
                    ins = nc.tensor.matmul(bank(3 + i)[:, 0:D], xnT[:, k, P * t:P * t + P], wqkv[:, k, 2 * D:3 * D],
                                           start=(k == 0), stop=(k == KD - 1))
                ins.then_inc(v_ready, 1)

            def transpose_qk(t):
                i = t % 2
                for st, low, moved, ready, bk in ((qst, q_lo, qT_moved, qT_ready, 5), (kst, k_lo, kT_moved, kT_ready, 6)):
                    pe.wait_ge(low, t + 1)
                    if t >= 1:
                        pe.wait_ge(moved, t)
                    dst = bank(bk).bitcast(FP16)
                    for a in range(PAIRS):
                        ins = nc.tensor.transpose(dst[:, P * a:P * a + P],
                                                  st[:, i, 2 * a:2 * a + 2, :, :].rearrange("p h s d -> p (h s d)"),
                                                  ident_h[:, :])
                    ins.then_inc(ready, 1)

            def scores(u):
                b, a = u // PAIRS, u % PAIRS
                pe.wait_ge(qT_moved, TPB * (b + 1))
                pe.wait_ge(kT_moved, TPB * (b + 1))
                if u >= 2:
                    pe.wait_ge(exp_done, u - 1)
                for h in range(2):
                    rows_ = slice(64 * h, 64 * h + 64)
                    for k in range(TPB):
                        at = 512 * h + S * k
                        ins = nc.tensor.matmul(pairs[u % 2][:, at:at + S],
                                               kT[rows_, a, S * b + P * k:S * b + P * k + P],
                                               qT[rows_, a, S * b:S * b + S], start=True, stop=True)
                ins.then_inc(s_ready, 1)

            def weigh(g):
                b, q = g // 4, g // 2
                pe.wait_ge(exp_done, 2 * g + 2)
                if g % 2 == 0 and q >= 2:
                    pe.wait_ge(o_moved, q - 1)
                if g == 2:
                    pe.wait_ge(qT_moved, T)
                for k in range(TPB):
                    for j in range(4):
                        at = 512 * (j % 2) + S * k
                        ins = nc.tensor.matmul(bank(4 + q % 2)[32 * j:32 * j + 32, S * (g % 2):S * (g % 2) + S],
                                               vaug[:, TPB * b + k, 4 * (g % 4) + j, :],
                                               probs[:, (2 * g + j // 2) % 4, at:at + S],
                                               start=(k == 0), stop=(k == TPB - 1), tile_position=(0, 32 * j))
                ins.then_inc(pv_done, 1)

            def tokens_first(b):
                pe.wait_ge(o_moved, 2 * b + 2)
                if b == 0:
                    pe.wait_ge(kT_moved, T)
                else:
                    pe.wait_ge(wT_moved, b)
                    pe.wait_ge(y_moved, b)
                for i in range(TPB):
                    for g in range(4):
                        ins = nc.tensor.transpose(bank(6 + i)[:, P * g:P * g + P],
                                                  oT[:, g // 2, S * (g % 2) + P * i:S * (g % 2) + P * i + P], ident[:, :])
                    ins.then_inc(ot_ready, 1)

            def features_first(b):
                pe.wait_ge(o_normed, TPB * (b + 1))
                for k in range(KD):
                    for i in range(TPB):
                        ins = nc.tensor.transpose(bank(6)[:, S * k + P * i:S * k + P * i + P],
                                                  otm[:, i, P * k:P * k + P], ident[:, :])
                ins.then_inc(oTn_ready, 1)

            def project_out(b):
                pe.wait_ge(oTn_moved, b + 1)
                pe.wait_ge(wout_ready, 1)
                for m in range(KD):
                    for k in range(KD):
                        ins = nc.tensor.matmul(bank(7)[:, S * m:S * m + S], wout[:, k, P * m:P * m + P],
                                               oTn[:, S * k:S * k + S], start=(k == 0), stop=(k == KD - 1))
                ins.then_inc(y_ready, 1)

            def transpose_w(i):
                pe.wait_ge(w_quant, i // KD + 1)
                pe.wait_ge(oTn_moved, i + 1)
                dst = bank(6).bitcast(FP16)
                for f in range(FT):
                    src = w1q[:, f, P * i:P * i + P] if i < KD else w2q[:, i - KD, P * f:P * f + P]
                    ins = nc.tensor.transpose(dst[:, P * f:P * f + P], src, ident_h[:, :])
                ins.then_inc(wT_ready, 1)

            pe.wait_ge(consts, 1)
            transpose_x(0)
            keep_warm(7, 6)
            pe.wait_ge(ld_qkv, 16)
            for t in range(T):
                project(t)
                if t % TPB == 0 and t // TPB + 1 < B:
                    transpose_x(t // TPB + 1)
                if t >= 2:
                    transpose_qk(t - 2)
            pe.wait_ge(qk_normed, T - 1)
            scores(0)
            pe.wait_ge(qk_normed, T)
            pe.wait_ge(v_moved, T)
            scores(1)
            keep_warm(3, 7)
            transpose_qk(T - 2)
            keep_warm(3, 7)
            scores(2)
            pe.wait_ge(consts, 5)
            keep_warm(3, 7)
            scores(3)
            weigh(0)
            transpose_qk(T - 1)
            for u in range(4, B * PAIRS + 7):
                if u < B * PAIRS:
                    scores(u)
                if u >= 3 and u % 2 == 1 and u // 2 - 1 < 4 * B:
                    weigh(u // 2 - 1)
                b, d = u // PAIRS - 1, u % PAIRS
                if b >= 0:
                    if d == 2:
                        tokens_first(b)
                    if d == 4:
                        if b == B - 1:
                            keep_warm(4, 0)
                        features_first(b)
                    if d == 6:
                        if b == B - 1:
                            keep_warm(2, 0)
                        project_out(b)
                        transpose_w(b)

            pe.wait_ge(diag_ready, 1)
            for m in range(KD):
                ins = nc.tensor.matmul(bank(5)[:, P * m:P * m + P], ones[:, :], diag[:, m, :], start=True, stop=True)
            ins.then_inc(s2row_ready, 1)

            def spread_max(n):
                bk = bank(4 - 4 * n)
                pe.wait_ge(am_col, n + 1)
                nc.tensor.transpose(bk[0:1, 0:P], amax[:, n:n + 1], ident[:, :]).then_inc(am_row, 1)
                pe.wait_ge(am_one, n + 1)
                nc.tensor.matmul(bk[:, P:P + 1], ones[0:1, :], amax1[0:1, n:n + 1], start=True,
                                 stop=True).then_inc(am_all, 1)

            keep_warm(3, 0)
            spread_max(0)
            keep_warm(10, 0)
            pe.wait_ge(wT_moved, B - 1)
            pe.wait_ge(wT_last, 1)
            pe.wait_ge(yq_ready, 3)
            for f in range(FT):
                if f >= 2:
                    pe.wait_ge(gelu_done, f - 1)
                for n in range(2):
                    for k in range(KD):
                        ins = nc.tensor.matmul(pairs[f % 2][:, 512 * n:512 * n + 512], w1qT[:, k, P * f:P * f + P],
                                               yq[:, k, 512 * n:512 * n + 512], start=(k == 0), stop=(k == KD - 1))
                ins.then_inc(f1_ready, 1)
            pe.wait_ge(gelu_done, FT)
            keep_warm(6, 1)
            spread_max(1)
            keep_warm(6, 1)
            pe.wait_ge(s2row_moved, 1)
            of_pool = of_dve = 0

            def ffn2(f, t):
                return nc.tensor.matmul(bank(4 + t // TPB)[:, D * (t % TPB):D * (t % TPB) + D],
                                        hq[:, f, P * t:P * t + P], w2qT[:, f, :],
                                        start=(f == 0 and t % TPB == 0), stop=(f == FT - 1), skip_group_check=True)

            for f in range(FT):
                if f in POOL_F:
                    of_pool += 1
                    pe.wait_ge(hq_pool, of_pool)
                else:
                    of_dve += 1
                    pe.wait_ge(hq_dve, of_dve)
                if f < F2_LATE:
                    for t in range(T):
                        if f == 0 and t == T // 2:
                            of_dve += 1
                            pe.wait_ge(hq_dve, of_dve)
                        ffn2(f, t)
            for t in range(T):
                for f in range(F2_LATE, FT):
                    ins = ffn2(f, t)
                if t % TPB == TPB - 1:
                    ins.then_inc(f2_ready, 1)

            for t in range(T):
                pe.wait_ge(x1_odd if t % 2 else x1_even, t // 2 + 1)
                keep_warm(3 if t == 0 else 1, 1)
                for k in range(KD):
                    at = B * BLK * k + P // BLK_TOKENS * t
                    ins = nc.tensor.matmul(bank(0)[:, at:at + P // BLK_TOKENS], x1[:, t, P * k:P * k + P],
                                           block_of[:, :], start=True, stop=True)
            ins.then_inc(br_ready, 1)
            keep_warm(2, 3)
            pe.wait_ge(br_moved, 1)
            pe.wait_ge(ld_wk, 16)
            for k in range(KD):
                ins = nc.tensor.matmul(bank(1)[0:B * BLK, 0:D], brT[:, k, :], wk[:, k, :], start=(k == 0), stop=(k == KD - 1))
            ins.then_inc(keys_ready, 1)
            keep_warm(8, 3)
            pe.wait_ge(score_ready, 1)
            nc.tensor.matmul(bank(2)[0:1, 0:B * BLK], score[:, :], ident[0:B * BLK, 0:B * BLK], start=True,
                             stop=True).then_inc(score_row, 1)
            keep_warm(6, 3)
            pe.wait_ge(attn_ready, 1)
            nc.tensor.matmul(bank(2)[:, 64:64 + B * BLK], ones[0:1, :], attn[:, :, :].rearrange("p b n -> p (b n)"),
                             start=True, stop=True).then_inc(attn_all, 1)
            keep_warm(3, 3)
            pe.wait_ge(att_ready, 1)
            pe.wait_ge(ld_wo, 16)
            for b in range(B):
                for k in range(KD):
                    ins = nc.tensor.matmul(projection(b), att[:, k, b:b + 1].broadcast_to([P, P]),
                                           wo[:, k, :], start=(k == 0), stop=(k == KD - 1))
                ins.then_inc(pr_ready, 1)
            keep_warm(8, 3)

            def transpose_x2(b):
                pe.wait_ge(xhat_ready, TPB * (b + 1))
                if b in (1, 2):
                    pe.wait_ge(x2T_moved, KD * b)
                elif b == 3:
                    pe.wait_ge(x2T_moved_late, KD)
                for k in range(KD):
                    for i in range(TPB):
                        ins = nc.tensor.transpose(bank(6)[:, S * k + P * i:S * k + P * i + P],
                                                  xr[:, TPB * b + i, P * k:P * k + P], ident[:, :])
                ins.then_inc(x2T_ready, 1)

            def synapse(t):
                pe.wait_ge(x2_lo, t // TPB + 1)
                if t >= 2:
                    pe.wait_ge(z_relu, t - 1)
                for n in range(2):
                    cols_ = slice(512 * n, 512 * n + 512)
                    nc.tensor.matmul(pairs[t % 2][:, cols_], sel3[:, :], bsyn3[:, cols_], start=True, stop=False)
                    for k in range(KD):
                        for part in (x2h, x2l):
                            ins = nc.tensor.matmul(pairs[t % 2][:, cols_], part[:, k, P * t:P * t + P], tsyn[:, k, cols_],
                                                   start=False, stop=(k == KD - 1 and part is x2l))
                ins.then_inc(z_ready, 1)

            def sum_found(b):
                if b >= 2:
                    pe.wait_ge(x4_stats, TPB * (b - 1))
                keep_warm(WARM_FOUND[b], 7 if b < B - 1 else 0)
                pe.wait_ge(thresh_found, TPB * (b + 1))
                for t in range(TPB * b, TPB * b + TPB):
                    ins = nc.tensor.matmul(found_at(b), ones[:, 0:1], found[:, t:t + 1], start=(t % TPB == 0),
                                           stop=(t % TPB == TPB - 1))
                ins.then_inc(found_sum, 1)

            def wait_moved(t):
                if t < T - TPB - 1:
                    pe.wait_ge(hT_dve, t + 1)
                if t % TPB:
                    pe.wait_ge(hT_act, t // TPB + 1)

            def transpose_hidden(t):
                pe.wait_ge(hid_ready, t + 1)
                if t == 0:
                    pe.wait_ge(ln_stats, T)
                elif t < T - 1:
                    wait_moved(t - 1)
                for f in range(FT):
                    ins = nc.tensor.transpose(hidden_banks(t)[:, P * f:P * f + P], hidden[:, t % 2, P * f:P * f + P], ident[:, :])
                ins.then_inc(hT_ready, 1)

            def last_product_split(t):
                pe.wait_ge(hT_rest, t - (T - TPB) + 1)
                pe.wait_ge(x4_stats, t - 1)
                for f in range(FT):
                    for part in (hT_hi, hT_lo):
                        ins = nc.tensor.matmul(bank(6 + t % 2)[:, 0:D], part[:, t % 2, P * f:P * f + P], tfin_h[:, f, :],
                                               start=(f == 0 and part is hT_hi), stop=(f == FT - 1 and part is hT_lo))
                ins.then_inc(out_ready, 1)

            def last_product(t):
                wait_moved(t)
                if t >= 2:
                    pe.wait_ge(x4_stats, t - 1)
                if t % TPB:
                    pe.wait_ge(flag_read, min(t // TPB + 2, B - 1))
                for f in range(FT):
                    ins = nc.tensor.matmul(bank(6 + t % 2)[:, 0:D], hT[:, t % 2, P * f:P * f + P], tfin[:, f, :],
                                           start=(f == 0), stop=(f == FT - 1))
                ins.then_inc(out_ready, 1)

            pe.wait_ge(tern_ready, 2)
            pe.wait_ge(bsyn_ready, 1)
            transpose_x2(0)
            keep_warm(6, 3)
            transpose_x2(1)
            synapse(0)
            synapse(1)
            transpose_x2(2)
            transpose_x2(3)
            synapse(2)
            synapse(3)
            pe.wait_ge(ln_stats, T)
            keep_warm(36, 7)
            for b in range(B + 1):
                if b == 1:
                    pe.wait_ge(tern_ready, 4)
                if b == B:
                    last_product_split(T - 2)
                    last_product_split(T - 1)
                elif b >= 1:
                    last_product(TPB * (b - 1))
                if b == B - 1:
                    last_product(TPB * (b - 1) + 1)
                    pe.wait_ge(z_relu, T)
                if b + 2 < B:
                    synapse(TPB * (b + 2))
                if b < B:
                    sum_found(b)
                if 1 <= b < B - 1:
                    last_product(TPB * (b - 1) + 1)
                if b == 0:
                    keep_warm(8, 6)
                if b == B - 1:
                    keep_warm(10, 1)
                if b < B:
                    transpose_hidden(TPB * b)
                if b + 2 < B:
                    synapse(TPB * (b + 2) + 1)
                if b < B:
                    transpose_hidden(TPB * b + 1)


def kernel(**inputs):
    import numpy as _np
    import concourse.bacc as _bacc
    from concourse import mybir as _mybir
    from concourse.bass_utils import run_bass_kernel_spmd as _run

    a = {k: _np.asarray(v) for k, v in inputs.items()}

    def by_column(v):
        return v.reshape(-1, P).T

    cond_t = a["cond_2048"].T.reshape(KD, P, B).transpose(1, 0, 2).reshape(P, KD * B)
    cols = _np.concatenate([cond_t, by_column(a["L0_cond_b_emb"]), by_column(a["L0_cond_g_norm"]),
                            by_column(a["L0_ffn_b1"]), by_column(a["L1_cond_ln_gamma"]),
                            by_column(a["L1_cond_ln_beta"])], axis=1)
    rows = _np.concatenate([a["L0_cond_g_q"], a["L0_cond_g_k"], a["L0_ffn_b2"], a["L1_ffn_b_out"], a["L1_ffn_gamma"],
                            a["L1_ffn_beta"], a["L1_cond_ln_gamma"], a["L1_cond_ln_beta"], a["L1_cond_rms_weight"],
                            a["cond_2048"][1], a["L1_ffn_b_syn"]])[None, :]
    feed = {
        "x": a["x"].reshape(B * S, D), "cols": cols, "rows": rows, "w_emb": a["L0_cond_W_emb"],
        "w_qkv": a["L0_cond_W_qkv"], "w_out": a["L0_cond_W_out"], "w1": a["L0_ffn_w1"], "w2": a["L0_ffn_w2"],
        "wk_t": a["L1_cond_Wk"].T, "wo_t": a["L1_cond_Wo"].T, "wsyn_t": a["L1_ffn_W_syn"].T,
        "wout_t": a["L1_ffn_W_out"].T,
    }
    nc = _bacc.Bacc("TRN2", target_bir_lowering=False, num_devices=1)
    arrays, args = {}, []
    for name, v in feed.items():
        v = _np.ascontiguousarray(v)
        arrays[f"in_{name}"] = v
        args.append(nc.dram_tensor(f"in_{name}", v.shape, _mybir.dt.from_np(v.dtype), kind="ExternalInput").ap())
    args.append(nc.dram_tensor("out_x", (B * S, D), F32, kind="ExternalOutput").ap())
    build(nc, *args)
    res = _run(nc, [arrays], core_ids=[0])
    return res.results[0]["out_x"].reshape(B, S, D)
```
